# Optimizing a Trainium2 kernel written in Bass

```python
import numpy as np
import jax
import jax.numpy as jnp

def _softmax(x, axis=-1):
    return jax.nn.softmax(x, axis=axis)

def _gelu(x):
    return jax.nn.gelu(x, approximate=True)

def _silu(x):
    return jax.nn.silu(x)

def _sigmoid(x):
    return jax.nn.sigmoid(x)

def _layernorm(x, axis=-1, eps=1e-05):
    m = jnp.mean(x, axis=axis, keepdims=True)
    v = jnp.var(x, axis=axis, keepdims=True)
    return (x - m) / jnp.sqrt(v + eps)

def _scatter_add(tgt, idx, src, axis=0):
    return tgt.at[idx].add(src)

def _segment_sum(src, seg, n):
    return jax.ops.segment_sum(src, seg, n)
kernel_name = 'mk_decoder_postln_d4_seqx_r4_223642'

def setup_inputs(seed: int=0):
    np.random.seed(seed)
    _w = jnp.asarray

    def _rec_inputs():
        import jax
        import jax.numpy as jnp
        _rk = jax.random.key(seed)
        x = -0.0002928 + 1 * jax.random.normal(jax.random.fold_in(_rk, 1), (2, 1024, 256), jnp.float32)
        _lenS = 1024 - jax.random.randint(jax.random.fold_in(_rk, 7), (2,), 0, max(1, 1024 // 4) + 1, jnp.int32)
        _lenS2 = 77 - jax.random.randint(jax.random.fold_in(_rk, 8), (2,), 0, max(1, 77 // 4) + 1, jnp.int32)
        _ctx_768P = jax.random.normal(jax.random.fold_in(_rk, 11), (2, 16, 192), jnp.float32)
        _ctx_768c = jax.random.dirichlet(jax.random.fold_in(_rk, 511), 0.3 * jnp.ones((16,), jnp.float32), (2, 77))
        _ctx_768t = jnp.einsum('bsk,bkd->bsd', _ctx_768c, _ctx_768P)
        _ctx_768t = _ctx_768t * jax.lax.rsqrt(jnp.mean(jnp.square(_ctx_768t)) + 1e-12) * 0.953939
        ctx_768 = 2.09791e-05 + 1.00001 * (_ctx_768t + 0.3 * jax.random.normal(jax.random.fold_in(_rk, 611), (2, 77, 192), jnp.float32))
        return (x, ctx_768)
    x, ctx_768 = _rec_inputs()

    def _L0_attn_setup():
        import jax, jax.numpy as jnp
        import numpy as np
        HEADS = 16
        D_MODEL = 256
        EXPANSION = 2
        D_EXP = D_MODEL * EXPANSION
        D_HEAD = D_EXP // HEADS
        B, SEQ = (1, 512)
        LN_EPS = 1e-05
        NEG_BIG = -10000000000.0

        def layer_norm(x, w, b):
            mu = jnp.mean(x, axis=-1, keepdims=True)
            var = jnp.var(x, axis=-1, keepdims=True)
            return (x - mu) * jax.lax.rsqrt(var + LN_EPS) * w + b
        key = jax.random.key(seed)
        ks = jax.random.split(key, 8)
        d_out = 4 * D_EXP + HEADS
        x = jax.random.normal(ks[0], (B, SEQ, D_MODEL), dtype=jnp.float32)
        W_in = 0.02 * jax.random.normal(ks[1], (d_out, D_MODEL), dtype=jnp.float32)
        b_in = jnp.zeros((d_out,), dtype=jnp.float32)
        W_in = W_in.at[4 * D_EXP:].set(0.0)
        b_in = b_in.at[4 * D_EXP:].set(jnp.linspace(-8.0, 8.0, HEADS))
        W_out = 0.02 * (2 * 12) ** (-0.5) * jax.random.normal(ks[2], (D_MODEL, D_EXP), dtype=jnp.float32)
        in_ln_w = jnp.ones((D_MODEL,), dtype=jnp.float32)
        in_ln_b = jnp.zeros((D_MODEL,), dtype=jnp.float32)
        out_ln_w = jnp.ones((D_MODEL,), dtype=jnp.float32)
        out_ln_b = jnp.zeros((D_MODEL,), dtype=jnp.float32)
        smear_factor = jnp.linspace(-6.0, 6.0, HEADS)
        log_scale = jnp.zeros((HEADS,), dtype=jnp.float32)
        return {'x': x, 'W_in': W_in, 'b_in': b_in, 'in_ln_w': in_ln_w, 'in_ln_b': in_ln_b, 'W_out': W_out, 'out_ln_w': out_ln_w, 'out_ln_b': out_ln_b, 'smear_factor': smear_factor, 'log_scale': log_scale}
    _L0_attn_all = _L0_attn_setup()
    _L0_attn_in = {k: v for k, v in _L0_attn_all.items() if k in ('W_in', 'b_in', 'in_ln_w', 'in_ln_b', 'W_out', 'out_ln_w', 'out_ln_b', 'smear_factor', 'log_scale')}
    del _L0_attn_all

    def _L0_xattn_setup():
        import jax, jax.numpy as jnp
        import numpy as np
        HEADS = 8
        DIM_HEAD = 128
        ATTN_MATRIX_SCALE = 1.5
        SCALE = DIM_HEAD ** (-0.5)

        def _split_heads(t):
            b, n, _ = t.shape
            t = t.reshape(b, n, HEADS, DIM_HEAD)
            return t.transpose(2, 0, 1, 3).reshape(HEADS, b * n, DIM_HEAD)
        key = jax.random.key(seed)
        ks = jax.random.split(key, 7)
        b, n, m = (2, 512, 512)
        qd, cd, inner = (256, 192, HEADS * DIM_HEAD)
        x = jax.random.normal(ks[0], (b, n, qd), dtype=jnp.float32)
        context = jax.random.normal(ks[1], (b, m, cd), dtype=jnp.float32)
        Wq = jax.random.normal(ks[2], (qd, inner), dtype=jnp.float32) * qd ** (-0.5)
        Wk = jax.random.normal(ks[3], (cd, inner), dtype=jnp.float32) * cd ** (-0.5)
        Wv = jax.random.normal(ks[4], (cd, inner), dtype=jnp.float32) * cd ** (-0.5)
        Wout = jax.random.normal(ks[5], (inner, qd), dtype=jnp.float32) * inner ** (-0.5)
        bout = jnp.zeros((qd,), dtype=jnp.float32)
        return {'x': x, 'context': context, 'Wq': Wq, 'Wk': Wk, 'Wv': Wv, 'Wout': Wout, 'bout': bout}
    _L0_xattn_all = _L0_xattn_setup()
    _L0_xattn_in = {k: v for k, v in _L0_xattn_all.items() if k in ('Wq', 'Wk', 'Wv', 'Wout', 'bout')}
    del _L0_xattn_all

    def _L0_ffn_setup():
        import jax, jax.numpy as jnp
        import numpy as np
        D = 256
        I = 128
        E = 32
        K = 4
        T = 2 * 512
        C = 2 * T * K // E
        key = jax.random.key(seed)
        ks = jax.random.split(key, 9)
        bf = jnp.bfloat16
        std = 0.02
        x = jax.random.normal(ks[0], (2, 512, D), dtype=jnp.float32).astype(bf)
        gate_w = (std * jax.random.normal(ks[1], (E, D), dtype=jnp.float32)).astype(bf)
        bias = jnp.zeros((E,), jnp.float32)
        W1 = (std * jax.random.normal(ks[2], (E, D, I), dtype=jnp.float32)).astype(bf)
        W3 = (std * jax.random.normal(ks[3], (E, D, I), dtype=jnp.float32)).astype(bf)
        W2 = (std * jax.random.normal(ks[4], (E, I, D), dtype=jnp.float32)).astype(bf)
        sw1 = (std * jax.random.normal(ks[5], (I, D), dtype=jnp.float32)).astype(bf)
        sw3 = (std * jax.random.normal(ks[6], (I, D), dtype=jnp.float32)).astype(bf)
        sw2 = (std * jax.random.normal(ks[7], (D, I), dtype=jnp.float32)).astype(bf)
        return {'x': x, 'gate_w': gate_w, 'bias': bias, 'W1': W1, 'W3': W3, 'W2': W2, 'sw1': sw1, 'sw3': sw3, 'sw2': sw2}
    _L0_ffn_all = _L0_ffn_setup()
    _L0_ffn_in = {k: v for k, v in _L0_ffn_all.items() if k in ('gate_w', 'bias', 'W1', 'W3', 'W2', 'sw1', 'sw3', 'sw2')}
    del _L0_ffn_all

    def _L1_attn_setup():
        import jax, jax.numpy as jnp
        import numpy as np
        import math
        N_HEAD = 16
        N_KV_HEAD = 4
        HEAD_DIM = 64
        ROPE_THETA = 10000.0

        def _rope_cache(T, D, dtype):
            inv_freq = 1.0 / ROPE_THETA ** (jnp.arange(0, D, 2, dtype=dtype) / D)
            t = jnp.arange(T, dtype=dtype)
            freqs = jnp.einsum('i,j->ij', t, inv_freq)
            return (jnp.cos(freqs)[None, None], jnp.sin(freqs)[None, None])

        def _apply_rope(x, cos, sin):
            x1 = x[..., ::2]
            x2 = x[..., 1::2]
            return jnp.concatenate([x1 * cos - x2 * sin, x1 * sin + x2 * cos], axis=-1)
        key = jax.random.key(seed)
        k0, k1, k2, k3, k4 = jax.random.split(key, 5)
        B, T, C = (4, 512, 256)
        scale = 0.02
        return {'x': jax.random.normal(k0, (B, T, C), dtype=jnp.float32), 'Wq': jax.random.normal(k1, (C, N_HEAD * HEAD_DIM), dtype=jnp.float32) * scale, 'Wk': jax.random.normal(k2, (C, N_KV_HEAD * HEAD_DIM), dtype=jnp.float32) * scale, 'Wv': jax.random.normal(k3, (C, N_KV_HEAD * HEAD_DIM), dtype=jnp.float32) * scale, 'Wo': jax.random.normal(k4, (N_HEAD * HEAD_DIM, C), dtype=jnp.float32) * scale}
    _L1_attn_all = _L1_attn_setup()
    _L1_attn_in = {k: v for k, v in _L1_attn_all.items() if k in ('Wq', 'Wk', 'Wv', 'Wo')}
    del _L1_attn_all

    def _L1_xattn_setup():
        import jax, jax.numpy as jnp
        import numpy as np
        N_HEADS = 16
        key = jax.random.key(seed)
        ks = jax.random.split(key, 8)
        b, l, m = (8, 256, 256)
        d_embed, d_cross = (256, 192)
        s_q = 1.0 / np.sqrt(d_embed)
        s_kv = 1.0 / np.sqrt(d_cross)
        return {'x': jax.random.normal(ks[0], (b, l, d_embed), jnp.float32), 'y': jax.random.normal(ks[1], (b, m, d_cross), jnp.float32), 'Wq': jax.random.normal(ks[2], (d_embed, d_embed), jnp.float32) * s_q, 'bq': jax.random.normal(ks[3], (d_embed,), jnp.float32) * 0.01, 'Wkv': jax.random.normal(ks[4], (2 * d_embed, d_cross), jnp.float32) * s_kv, 'bkv': jax.random.normal(ks[5], (2 * d_embed,), jnp.float32) * 0.01, 'Wo': jax.random.normal(ks[6], (d_embed, d_embed), jnp.float32) * s_q, 'bo': jax.random.normal(ks[7], (d_embed,), jnp.float32) * 0.01}
    _L1_xattn_all = _L1_xattn_setup()
    _L1_xattn_in = {k: v for k, v in _L1_xattn_all.items() if k in ('Wq', 'bq', 'Wkv', 'bkv', 'Wo', 'bo')}
    del _L1_xattn_all

    def _L1_ffn_setup():
        import jax, jax.numpy as jnp
        import numpy as np
        D_MODEL = 256
        EXPERT_DIM = 128
        N_EXPERTS = 8
        TOP_K = 2

        def _sq_relu(h):
            return jnp.square(jax.nn.relu(h))
        key = jax.random.key(seed)
        ks = jax.random.split(key, 6)
        s = 0.02
        x = jax.random.normal(ks[0], (2, 512, D_MODEL), dtype=jnp.float32)
        Ws1 = jax.random.normal(ks[1], (D_MODEL, EXPERT_DIM), dtype=jnp.float32) * s
        Ws2 = jax.random.normal(ks[2], (EXPERT_DIM, D_MODEL), dtype=jnp.float32) * s
        W1 = jax.random.normal(ks[3], (N_EXPERTS, D_MODEL, EXPERT_DIM), dtype=jnp.float32) * s
        W2 = jax.random.normal(ks[4], (N_EXPERTS, EXPERT_DIM, D_MODEL), dtype=jnp.float32) * s
        Wr = jax.random.normal(ks[5], (D_MODEL, N_EXPERTS), dtype=jnp.float32) * s
        return {'x': x, 'Ws1': Ws1, 'Ws2': Ws2, 'W1': W1, 'W2': W2, 'Wr': Wr}
    _L1_ffn_all = _L1_ffn_setup()
    _L1_ffn_in = {k: v for k, v in _L1_ffn_all.items() if k in ('Ws1', 'Ws2', 'W1', 'W2', 'Wr')}
    del _L1_ffn_all

    def _L2_attn_setup():
        import jax, jax.numpy as jnp
        import numpy as np
        SEQ_LEN = 512
        DIM_EMB = 256
        DIM_K = 256
        DIM_V = 256
        BATCH = 4
        key = jax.random.key(seed)
        kx, kq, kk, kv, ko = jax.random.split(key, 5)
        s = DIM_EMB ** (-0.5)
        return {'x': jax.random.normal(kx, (BATCH, SEQ_LEN, DIM_EMB), dtype=jnp.float32), 'Wq': jax.random.normal(kq, (DIM_EMB, DIM_K), dtype=jnp.float32) * s, 'Wk': jax.random.normal(kk, (DIM_EMB, DIM_K), dtype=jnp.float32) * s, 'Wv': jax.random.normal(kv, (DIM_EMB, DIM_V), dtype=jnp.float32) * s, 'Wo': jax.random.normal(ko, (DIM_V, DIM_V), dtype=jnp.float32) * DIM_V ** (-0.5)}
    _L2_attn_all = _L2_attn_setup()
    _L2_attn_in = {k: v for k, v in _L2_attn_all.items() if k in ('Wq', 'Wk', 'Wv', 'Wo')}
    del _L2_attn_all

    def _L2_xattn_setup():
        import jax, jax.numpy as jnp
        import numpy as np
        DIM_Q = 256
        DIM_KV = 192
        N_HEADS = 4

        def _split_heads(x):
            b, l, d = x.shape
            return x.reshape(b, l, N_HEADS, d // N_HEADS).transpose(0, 2, 1, 3)
        key = jax.random.key(seed)
        ks = jax.random.split(key, 7)
        b, lq, lkv = (4, 512, 512)
        q = jax.random.normal(ks[0], (b, lq, DIM_Q), dtype=jnp.float32)
        kv = jax.random.normal(ks[1], (b, lkv, DIM_KV), dtype=jnp.float32)
        s_q = 1.0 / np.sqrt(DIM_Q)
        s_kv = 1.0 / np.sqrt(DIM_KV)
        Wq = jax.random.normal(ks[2], (DIM_Q, DIM_Q), dtype=jnp.float32) * s_q
        Wk = jax.random.normal(ks[3], (DIM_Q, DIM_KV), dtype=jnp.float32) * s_kv
        Wv = jax.random.normal(ks[4], (DIM_Q, DIM_KV), dtype=jnp.float32) * s_kv
        Wo = jax.random.normal(ks[5], (DIM_Q, DIM_Q), dtype=jnp.float32) * s_q
        bo = jax.random.normal(ks[6], (DIM_Q,), dtype=jnp.float32) * 0.01
        return {'q': q, 'kv': kv, 'Wq': Wq, 'Wk': Wk, 'Wv': Wv, 'Wo': Wo, 'bo': bo}
    _L2_xattn_all = _L2_xattn_setup()
    _L2_xattn_in = {k: v for k, v in _L2_xattn_all.items() if k in ('Wq', 'Wk', 'Wv', 'Wo', 'bo')}
    del _L2_xattn_all

    def _L2_ffn_setup():
        import jax, jax.numpy as jnp
        import numpy as np
        IN_DIM, OUT_DIM, N_PROTO, RANK = (256, 256, 32, 16)
        key = jax.random.key(seed)
        ks = jax.random.split(key, 5)
        x = jax.random.normal(ks[0], (2, 1024, IN_DIM), dtype=jnp.float32)
        prototypes = jax.random.normal(ks[1], (N_PROTO, IN_DIM), dtype=jnp.float32) * 0.02
        B = jax.random.normal(ks[2], (N_PROTO, RANK, IN_DIM), dtype=jnp.float32) * 0.02
        A = jax.random.normal(ks[3], (N_PROTO, OUT_DIM, RANK), dtype=jnp.float32) * 0.02
        bias = jnp.zeros((N_PROTO, OUT_DIM), dtype=jnp.float32)
        temp = jnp.asarray(1.0, dtype=jnp.float32)
        return {'x': x, 'prototypes': prototypes, 'B': B, 'A': A, 'bias': bias, 'temp': temp}
    _L2_ffn_all = _L2_ffn_setup()
    _L2_ffn_in = {k: v for k, v in _L2_ffn_all.items() if k in ('prototypes', 'B', 'A', 'bias', 'temp')}
    del _L2_ffn_all

    def _L3_attn_setup():
        import jax, jax.numpy as jnp
        import numpy as np
        from math import sqrt
        N_HEAD = 16
        W_SCALE = 0.02

        def _reference_tuple_inner(x, W_dq, W_uq, W_dkv, W_uk, W_uv, W_o):
            B, T, C = x.shape
            nh = N_HEAD
            hs = C // nh
            n_kvl = W_dkv.shape[0]
            k_eff = (W_dq.T @ W_uq.T @ W_uk).reshape(nh, hs, n_kvl)
            v_eff = jnp.transpose((W_uv.T @ W_o.T).reshape(n_kvl, nh, hs), (1, 0, 2))
            c_kv = x @ W_dkv.T
            q = x @ W_dq.T @ W_uq.T
            q = q.reshape(B, T, nh, hs)
            q_lat = jnp.einsum('bqhd,hdl->bhql', q, k_eff)
            attn = jnp.einsum('bhql,bkl->bhqk', q_lat, c_kv) / sqrt(hs)
            causal = jnp.tril(jnp.ones((T, T), dtype=bool))
            attn = jnp.where(causal[None, None], attn, -jnp.inf)
            attn = jax.nn.softmax(attn, axis=-1)
            y_lat = jnp.einsum('bhqk,bkl->bhql', attn, c_kv)
            y = jnp.einsum('bhql,hld->bqhd', y_lat, v_eff).reshape(B, T, C)
            return (y, c_kv)
        key = jax.random.key(seed)
        ks = jax.random.split(key, 7)
        B, T, C = (2, 512, 256)
        QL, KVL = (128, 128)
        return {'x': jax.random.normal(ks[0], (B, T, C), dtype=jnp.float32), 'W_dq': jax.random.normal(ks[1], (QL, C), dtype=jnp.float32) * W_SCALE, 'W_uq': jax.random.normal(ks[2], (C, QL), dtype=jnp.float32) * W_SCALE, 'W_dkv': jax.random.normal(ks[3], (KVL, C), dtype=jnp.float32) * W_SCALE, 'W_uk': jax.random.normal(ks[4], (C, KVL), dtype=jnp.float32) * W_SCALE, 'W_uv': jax.random.normal(ks[5], (C, KVL), dtype=jnp.float32) * W_SCALE, 'W_o': jax.random.normal(ks[6], (C, C), dtype=jnp.float32) * W_SCALE}
    _L3_attn_all = _L3_attn_setup()
    _L3_attn_in = {k: v for k, v in _L3_attn_all.items() if k in ('W_dq', 'W_uq', 'W_dkv', 'W_uk', 'W_uv', 'W_o')}
    del _L3_attn_all

    def _L3_xattn_setup():
        import jax, jax.numpy as jnp
        import numpy as np
        DIM = 256
        CTX_DIM = 192
        H = 16
        DH = 64
        INNER = H * DH
        EPS = 1e-05

        def layer_norm(x, gamma, beta):
            mu = jnp.mean(x, axis=-1, keepdims=True)
            var = jnp.mean(jnp.square(x - mu), axis=-1, keepdims=True)
            return (x - mu) * jax.lax.rsqrt(var + EPS) * gamma + beta
        key = jax.random.key(seed)
        ks = jax.random.split(key, 8)
        B, N, M = (4, 512, 512)
        x = jax.random.normal(ks[0], (B, N, DIM), dtype=jnp.float32)
        context = jax.random.normal(ks[1], (B, M, CTX_DIM), dtype=jnp.float32)
        g_x = jnp.ones((DIM,), jnp.float32)
        b_x = jnp.zeros((DIM,), jnp.float32)
        g_c = jnp.ones((CTX_DIM,), jnp.float32)
        b_c = jnp.zeros((CTX_DIM,), jnp.float32)
        Wq = jax.random.normal(ks[2], (DIM, INNER), dtype=jnp.float32) / np.sqrt(DIM)
        Wk = jax.random.normal(ks[3], (CTX_DIM, INNER), dtype=jnp.float32) / np.sqrt(CTX_DIM)
        Wv = jax.random.normal(ks[4], (CTX_DIM, INNER), dtype=jnp.float32) / np.sqrt(CTX_DIM)
        Wo = jax.random.normal(ks[5], (INNER, DIM), dtype=jnp.float32) / np.sqrt(INNER)
        return {'x': x, 'context': context, 'g_x': g_x, 'b_x': b_x, 'g_c': g_c, 'b_c': b_c, 'Wq': Wq, 'Wk': Wk, 'Wv': Wv, 'Wo': Wo}
    _L3_xattn_all = _L3_xattn_setup()
    _L3_xattn_in = {k: v for k, v in _L3_xattn_all.items() if k in ('g_x', 'b_x', 'g_c', 'b_c', 'Wq', 'Wk', 'Wv', 'Wo')}
    del _L3_xattn_all

    def _L3_ffn_setup():
        import jax, jax.numpy as jnp
        import numpy as np
        MICRO_BATCHES = 2
        TOP_K = 2
        NUM_EXPERTS = 8
        B, S, D = (4, 1024, 256)
        H = 4 * D
        key = jax.random.key(seed)
        ks = jax.random.split(key, 8)
        s = 0.02
        return {'x': jax.random.normal(ks[0], (B, S, D), jnp.float32), 'ln_scale': jnp.ones((D,), jnp.float32), 'ln_bias': jnp.zeros((D,), jnp.float32), 'attn_w': jax.random.normal(ks[1], (D, D), jnp.float32) * s, 'attn_b': jnp.zeros((D,), jnp.float32), 'gate_w': jax.random.normal(ks[2], (NUM_EXPERTS, D), jnp.float32) * s, 'w1': jax.random.normal(ks[3], (NUM_EXPERTS, D, H), jnp.float32) * s, 'b1': jnp.zeros((NUM_EXPERTS, H), jnp.float32), 'w2': jax.random.normal(ks[4], (NUM_EXPERTS, H, D), jnp.float32) * s, 'b2': jnp.zeros((NUM_EXPERTS, D), jnp.float32), 'next_w': jax.random.normal(ks[5], (D, D), jnp.float32) * s, 'next_b': jnp.zeros((D,), jnp.float32)}
    _L3_ffn_all = _L3_ffn_setup()
    _L3_ffn_in = {k: v for k, v in _L3_ffn_all.items() if k in ('ln_scale', 'ln_bias', 'attn_w', 'attn_b', 'gate_w', 'w1', 'b1', 'w2', 'b2', 'next_w', 'next_b')}
    del _L3_ffn_all
    return {'x': x, 'ctx_768': ctx_768, 'L0_attn_W_in': _L0_attn_in['W_in'], 'L0_attn_b_in': _L0_attn_in['b_in'], 'L0_attn_in_ln_w': _L0_attn_in['in_ln_w'], 'L0_attn_in_ln_b': _L0_attn_in['in_ln_b'], 'L0_attn_W_out': _L0_attn_in['W_out'], 'L0_attn_out_ln_w': _L0_attn_in['out_ln_w'], 'L0_attn_out_ln_b': _L0_attn_in['out_ln_b'], 'L0_attn_smear_factor': _L0_attn_in['smear_factor'], 'L0_attn_log_scale': _L0_attn_in['log_scale'], 'L0_xattn_Wq': _L0_xattn_in['Wq'], 'L0_xattn_Wk': _L0_xattn_in['Wk'], 'L0_xattn_Wv': _L0_xattn_in['Wv'], 'L0_xattn_Wout': _L0_xattn_in['Wout'], 'L0_xattn_bout': _L0_xattn_in['bout'], 'L0_ffn_gate_w': _L0_ffn_in['gate_w'], 'L0_ffn_bias': _L0_ffn_in['bias'], 'L0_ffn_W1': _L0_ffn_in['W1'], 'L0_ffn_W3': _L0_ffn_in['W3'], 'L0_ffn_W2': _L0_ffn_in['W2'], 'L0_ffn_sw1': _L0_ffn_in['sw1'], 'L0_ffn_sw3': _L0_ffn_in['sw3'], 'L0_ffn_sw2': _L0_ffn_in['sw2'], 'L1_attn_Wq': _L1_attn_in['Wq'], 'L1_attn_Wk': _L1_attn_in['Wk'], 'L1_attn_Wv': _L1_attn_in['Wv'], 'L1_attn_Wo': _L1_attn_in['Wo'], 'L1_xattn_Wq': _L1_xattn_in['Wq'], 'L1_xattn_bq': _L1_xattn_in['bq'], 'L1_xattn_Wkv': _L1_xattn_in['Wkv'], 'L1_xattn_bkv': _L1_xattn_in['bkv'], 'L1_xattn_Wo': _L1_xattn_in['Wo'], 'L1_xattn_bo': _L1_xattn_in['bo'], 'L1_ffn_Ws1': _L1_ffn_in['Ws1'], 'L1_ffn_Ws2': _L1_ffn_in['Ws2'], 'L1_ffn_W1': _L1_ffn_in['W1'], 'L1_ffn_W2': _L1_ffn_in['W2'], 'L1_ffn_Wr': _L1_ffn_in['Wr'], 'L2_attn_Wq': _L2_attn_in['Wq'], 'L2_attn_Wk': _L2_attn_in['Wk'], 'L2_attn_Wv': _L2_attn_in['Wv'], 'L2_attn_Wo': _L2_attn_in['Wo'], 'L2_xattn_Wq': _L2_xattn_in['Wq'], 'L2_xattn_Wk': _L2_xattn_in['Wk'], 'L2_xattn_Wv': _L2_xattn_in['Wv'], 'L2_xattn_Wo': _L2_xattn_in['Wo'], 'L2_xattn_bo': _L2_xattn_in['bo'], 'L2_ffn_prototypes': _L2_ffn_in['prototypes'], 'L2_ffn_B': _L2_ffn_in['B'], 'L2_ffn_A': _L2_ffn_in['A'], 'L2_ffn_bias': _L2_ffn_in['bias'], 'L2_ffn_temp': _L2_ffn_in['temp'], 'L3_attn_W_dq': _L3_attn_in['W_dq'], 'L3_attn_W_uq': _L3_attn_in['W_uq'], 'L3_attn_W_dkv': _L3_attn_in['W_dkv'], 'L3_attn_W_uk': _L3_attn_in['W_uk'], 'L3_attn_W_uv': _L3_attn_in['W_uv'], 'L3_attn_W_o': _L3_attn_in['W_o'], 'L3_xattn_g_x': _L3_xattn_in['g_x'], 'L3_xattn_b_x': _L3_xattn_in['b_x'], 'L3_xattn_g_c': _L3_xattn_in['g_c'], 'L3_xattn_b_c': _L3_xattn_in['b_c'], 'L3_xattn_Wq': _L3_xattn_in['Wq'], 'L3_xattn_Wk': _L3_xattn_in['Wk'], 'L3_xattn_Wv': _L3_xattn_in['Wv'], 'L3_xattn_Wo': _L3_xattn_in['Wo'], 'L3_ffn_ln_scale': _L3_ffn_in['ln_scale'], 'L3_ffn_ln_bias': _L3_ffn_in['ln_bias'], 'L3_ffn_attn_w': _L3_ffn_in['attn_w'], 'L3_ffn_attn_b': _L3_ffn_in['attn_b'], 'L3_ffn_gate_w': _L3_ffn_in['gate_w'], 'L3_ffn_w1': _L3_ffn_in['w1'], 'L3_ffn_b1': _L3_ffn_in['b1'], 'L3_ffn_w2': _L3_ffn_in['w2'], 'L3_ffn_b2': _L3_ffn_in['b2'], 'L3_ffn_next_w': _L3_ffn_in['next_w'], 'L3_ffn_next_b': _L3_ffn_in['next_b']}

def reference(x, ctx_768, L0_attn_W_in, L0_attn_b_in, L0_attn_in_ln_w, L0_attn_in_ln_b, L0_attn_W_out, L0_attn_out_ln_w, L0_attn_out_ln_b, L0_attn_smear_factor, L0_attn_log_scale, L0_xattn_Wq, L0_xattn_Wk, L0_xattn_Wv, L0_xattn_Wout, L0_xattn_bout, L0_ffn_gate_w, L0_ffn_bias, L0_ffn_W1, L0_ffn_W3, L0_ffn_W2, L0_ffn_sw1, L0_ffn_sw3, L0_ffn_sw2, L1_attn_Wq, L1_attn_Wk, L1_attn_Wv, L1_attn_Wo, L1_xattn_Wq, L1_xattn_bq, L1_xattn_Wkv, L1_xattn_bkv, L1_xattn_Wo, L1_xattn_bo, L1_ffn_Ws1, L1_ffn_Ws2, L1_ffn_W1, L1_ffn_W2, L1_ffn_Wr, L2_attn_Wq, L2_attn_Wk, L2_attn_Wv, L2_attn_Wo, L2_xattn_Wq, L2_xattn_Wk, L2_xattn_Wv, L2_xattn_Wo, L2_xattn_bo, L2_ffn_prototypes, L2_ffn_B, L2_ffn_A, L2_ffn_bias, L2_ffn_temp, L3_attn_W_dq, L3_attn_W_uq, L3_attn_W_dkv, L3_attn_W_uk, L3_attn_W_uv, L3_attn_W_o, L3_xattn_g_x, L3_xattn_b_x, L3_xattn_g_c, L3_xattn_b_c, L3_xattn_Wq, L3_xattn_Wk, L3_xattn_Wv, L3_xattn_Wo, L3_ffn_ln_scale, L3_ffn_ln_bias, L3_ffn_attn_w, L3_ffn_attn_b, L3_ffn_gate_w, L3_ffn_w1, L3_ffn_b1, L3_ffn_w2, L3_ffn_b2, L3_ffn_next_w, L3_ffn_next_b):
    import jax
    import jax.numpy as jnp

    def _L0_attn_ref(x, W_in, b_in, in_ln_w, in_ln_b, W_out, out_ln_w, out_ln_b, smear_factor, log_scale):
        import jax, jax.numpy as jnp
        import numpy as np
        HEADS = 16
        D_MODEL = 256
        EXPANSION = 2
        D_EXP = D_MODEL * EXPANSION
        D_HEAD = D_EXP // HEADS
        B, SEQ = (1, 512)
        LN_EPS = 1e-05
        NEG_BIG = -10000000000.0

        def layer_norm(x, w, b):
            mu = jnp.mean(x, axis=-1, keepdims=True)
            var = jnp.var(x, axis=-1, keepdims=True)
            return (x - mu) * jax.lax.rsqrt(var + LN_EPS) * w + b
        b, i, d = x.shape
        xn = layer_norm(x, in_ln_w, in_ln_b)
        proj = xn @ W_in.T + b_in
        q, k, v, p, y = jnp.split(proj, [D_EXP, 2 * D_EXP, 3 * D_EXP, 4 * D_EXP], axis=-1)
        to_heads = lambda t: t.reshape(b, i, HEADS, D_HEAD).transpose(0, 2, 1, 3)
        q, k, v = (to_heads(q), to_heads(k), to_heads(v))
        smear = jax.nn.sigmoid(smear_factor)[None, :, None, None]
        k_prev = jnp.pad(k, ((0, 0), (0, 0), (1, 0), (0, 0)))[:, :, :-1, :]
        k = (1 - smear) * k + smear * k_prev
        s = jnp.exp(log_scale)[None, :, None, None]
        pos = jnp.cumsum(jax.nn.sigmoid(y).transpose(0, 2, 1), axis=-1)
        relpos = pos[..., :, None] - pos[..., None, :]
        causal = jnp.triu(jnp.full((i, i), NEG_BIG, dtype=x.dtype), k=1)
        mask = causal - relpos
        scores = jnp.einsum('bhid,bhjd->bhij', q / s, k / s) / np.sqrt(D_HEAD) + mask
        attn = jax.nn.softmax(scores, axis=-1)
        o = jnp.einsum('bhij,bhjd->bhid', attn, v)
        o = o.transpose(0, 2, 1, 3).reshape(b, i, D_EXP)
        out = jax.nn.silu(p) * o @ W_out.T
        return layer_norm(out, out_ln_w, out_ln_b)

    def _L0_xattn_ref(x, context, Wq, Wk, Wv, Wout, bout):
        import jax, jax.numpy as jnp
        import numpy as np
        HEADS = 8
        DIM_HEAD = 128
        ATTN_MATRIX_SCALE = 1.5
        SCALE = DIM_HEAD ** (-0.5)

        def _split_heads(t):
            b, n, _ = t.shape
            t = t.reshape(b, n, HEADS, DIM_HEAD)
            return t.transpose(2, 0, 1, 3).reshape(HEADS, b * n, DIM_HEAD)
        b, n, _ = x.shape
        qh = _split_heads(jnp.einsum('bnq,qi->bni', x, Wq))
        kh = _split_heads(jnp.einsum('bmc,ci->bmi', context, Wk))
        vh = _split_heads(jnp.einsum('bmc,ci->bmi', context, Wv))
        sim = jnp.einsum('hid,hjd->hij', qh, kh) * SCALE
        mean = jnp.mean(sim, axis=-1, keepdims=True)
        sim = (sim - mean) * ATTN_MATRIX_SCALE + mean
        attn = jax.nn.softmax(sim, axis=-1)
        out = jnp.einsum('hij,hjd->hid', attn, vh)
        out = out.reshape(HEADS, b, n, DIM_HEAD).transpose(1, 2, 0, 3)
        out = out.reshape(b, n, HEADS * DIM_HEAD)
        return jnp.einsum('bni,iq->bnq', out, Wout) + bout

    def _L0_ffn_ref(x, gate_w, bias, W1, W3, W2, sw1, sw3, sw2):
        import jax, jax.numpy as jnp
        import numpy as np
        D = 256
        I = 128
        E = 32
        K = 4
        T = 2 * 512
        C = 2 * T * K // E
        X = x.reshape(-1, D)
        logits = (X @ gate_w.T).astype(jnp.float32)
        scores = jax.nn.sigmoid(logits)
        _, idx = jax.lax.top_k(scores + bias[None, :], K)
        w = jnp.take_along_axis(scores, idx, axis=-1)
        w = w / jnp.clip(jnp.sum(w, axis=-1, keepdims=True), 1e-12, None)
        w = w.astype(x.dtype)
        eid = idx.reshape(-1)
        onehot = (eid[:, None] == jnp.arange(E)[None, :]).astype(jnp.int32)
        pos = jnp.take_along_axis(jnp.cumsum(onehot, axis=0) - 1, eid[:, None], axis=1)[:, 0]
        valid = pos < C
        posc = jnp.minimum(pos, C - 1)
        Xrep = jnp.repeat(X, K, axis=0)
        xe = jnp.zeros((E, C, D), x.dtype).at[eid, posc].add(jnp.where(valid[:, None], Xrep, jnp.zeros((), x.dtype)))
        h = jax.nn.silu(jnp.einsum('ecd,edi->eci', xe, W1)) * jnp.einsum('ecd,edi->eci', xe, W3)
        ye = jnp.einsum('eci,eid->ecd', h, W2)
        gflat = jnp.where(valid, w.reshape(-1), jnp.zeros((), x.dtype))
        yrows = ye[eid, posc] * gflat[:, None]
        out = yrows.reshape(-1, K, D).sum(axis=1)
        out = out + jax.nn.silu(X @ sw1.T) * (X @ sw3.T) @ sw2.T
        return out.reshape(x.shape)

    def _L1_attn_ref(x, Wq, Wk, Wv, Wo):
        import jax, jax.numpy as jnp
        import numpy as np
        import math
        N_HEAD = 16
        N_KV_HEAD = 4
        HEAD_DIM = 64
        ROPE_THETA = 10000.0

        def _rope_cache(T, D, dtype):
            inv_freq = 1.0 / ROPE_THETA ** (jnp.arange(0, D, 2, dtype=dtype) / D)
            t = jnp.arange(T, dtype=dtype)
            freqs = jnp.einsum('i,j->ij', t, inv_freq)
            return (jnp.cos(freqs)[None, None], jnp.sin(freqs)[None, None])

        def _apply_rope(x, cos, sin):
            x1 = x[..., ::2]
            x2 = x[..., 1::2]
            return jnp.concatenate([x1 * cos - x2 * sin, x1 * sin + x2 * cos], axis=-1)
        B, T, C = x.shape
        H, Hkv, D = (N_HEAD, N_KV_HEAD, HEAD_DIM)
        q = (x @ Wq).reshape(B, T, H, D).transpose(0, 2, 1, 3)
        k = (x @ Wk).reshape(B, T, Hkv, D).transpose(0, 2, 1, 3)
        v = (x @ Wv).reshape(B, T, Hkv, D).transpose(0, 2, 1, 3)
        rep = H // Hkv
        k = jnp.repeat(k, rep, axis=1)
        v = jnp.repeat(v, rep, axis=1)
        cos, sin = _rope_cache(T, D, x.dtype)
        q = _apply_rope(q, cos, sin)
        k = _apply_rope(k, cos, sin)
        att = jnp.einsum('bhtd,bhsd->bhts', q, k) / math.sqrt(D)
        mask = jnp.tril(jnp.ones((T, T), dtype=bool))
        att = jnp.where(mask, att, -jnp.inf)
        att = jax.nn.softmax(att, axis=-1)
        y = jnp.einsum('bhts,bhsd->bhtd', att, v)
        y = y.transpose(0, 2, 1, 3).reshape(B, T, H * D)
        return y @ Wo

    def _L1_xattn_ref(x, y, Wq, bq, Wkv, bkv, Wo, bo):
        import jax, jax.numpy as jnp
        import numpy as np
        N_HEADS = 16
        b, l, d = x.shape
        m = y.shape[1]
        h = N_HEADS
        dh = d // h
        q = (jnp.einsum('bld,ed->ble', x, Wq) + bq).reshape(b, l, h, dh)
        kv = (jnp.einsum('bmc,ec->bme', y, Wkv) + bkv).reshape(b, m, h, 2 * dh)
        k, v = (kv[..., :dh], kv[..., dh:])
        scale = 1.0 / jnp.sqrt(jnp.asarray(dh, x.dtype))
        att = jax.nn.softmax(jnp.einsum('blhd,bmhd->blmh', q, k) * scale, axis=2)
        out = jnp.einsum('blmh,bmhd->blhd', att, v).reshape(b, l, d)
        return jnp.einsum('bld,ed->ble', out, Wo) + bo

    def _L1_ffn_ref(x, Ws1, Ws2, W1, W2, Wr):
        import jax, jax.numpy as jnp
        import numpy as np
        D_MODEL = 256
        EXPERT_DIM = 128
        N_EXPERTS = 8
        TOP_K = 2

        def _sq_relu(h):
            return jnp.square(jax.nn.relu(h))
        shape = x.shape
        xf = x.reshape(-1, D_MODEL)
        out_shared = _sq_relu(xf @ Ws1) @ Ws2
        logits = xf @ Wr
        top_vals, top_idx = jax.lax.top_k(logits, TOP_K)
        rw = jax.nn.softmax(top_vals.astype(jnp.float32), axis=-1).astype(x.dtype)
        onehot = jax.nn.one_hot(top_idx, N_EXPERTS, dtype=x.dtype)
        prob = jnp.einsum('tk,tke->te', rw, onehot)
        prob = jnp.trunc(prob)
        h = _sq_relu(jnp.einsum('td,edf->tef', xf, W1))
        y = jnp.einsum('tef,efd->ted', h, W2)
        out_routed = jnp.einsum('ted,te->td', y, prob)
        return (out_shared + out_routed).reshape(shape)

    def _L2_attn_ref(x, Wq, Wk, Wv, Wo):
        import jax, jax.numpy as jnp
        import numpy as np
        SEQ_LEN = 512
        DIM_EMB = 256
        DIM_K = 256
        DIM_V = 256
        BATCH = 4
        q = jnp.einsum('bse,ek->bsk', x, Wq)
        k = jnp.einsum('bse,ek->bsk', x, Wk)
        v = jnp.einsum('bse,ev->bsv', x, Wv)
        scores = jnp.einsum('bqk,bsk->bqs', q, k)
        S = scores.shape[-1]
        causal_mask = jnp.triu(jnp.ones((S, S), dtype=bool), k=1)
        scores = jnp.where(causal_mask[None], -jnp.inf, scores)
        attn = jax.nn.softmax(scores * Wq.shape[1] ** (-0.5), axis=-1)
        out = jnp.einsum('bqs,bsv->bqv', attn, v)
        return jnp.einsum('bqv,vo->bqo', out, Wo)

    def _L2_xattn_ref(q, kv, Wq, Wk, Wv, Wo, bo):
        import jax, jax.numpy as jnp
        import numpy as np
        DIM_Q = 256
        DIM_KV = 192
        N_HEADS = 4

        def _split_heads(x):
            b, l, d = x.shape
            return x.reshape(b, l, N_HEADS, d // N_HEADS).transpose(0, 2, 1, 3)
        qp = q @ Wq.T
        kp = kv @ Wk.T
        vp = kv @ Wv.T
        qh, kh, vh = (_split_heads(qp), _split_heads(kp), _split_heads(vp))
        scale = (DIM_Q // N_HEADS) ** (-0.5)
        scores = jnp.einsum('bhqd,bhkd->bhqk', qh, kh) * scale
        attn = jax.nn.softmax(scores, axis=-1)
        ctx = jnp.einsum('bhqk,bhkd->bhqd', attn, vh)
        b, h, lq, hd = ctx.shape
        ctx = ctx.transpose(0, 2, 1, 3).reshape(b, lq, h * hd)
        return ctx @ Wo.T + bo

    def _L2_ffn_ref(x, prototypes, B, A, bias, temp):
        import jax, jax.numpy as jnp
        import numpy as np
        IN_DIM, OUT_DIM, N_PROTO, RANK = (256, 256, 32, 16)
        lead = x.shape[:-1]
        xf = x.reshape(-1, IN_DIM)
        x2 = jnp.sum(xf * xf, axis=1, keepdims=True)
        p2 = jnp.sum(prototypes * prototypes, axis=1)
        d2 = x2 + p2[None, :] - 2.0 * (xf @ prototypes.T)
        dists = jnp.sqrt(jnp.maximum(d2, 0.0))
        t = jnp.maximum(jnp.abs(temp), 0.1)
        w = jax.nn.softmax(-dists / t, axis=1)
        topw, topi = jax.lax.top_k(w, 2)
        topw = topw / jnp.sum(topw, axis=1, keepdims=True)
        out = jnp.zeros((xf.shape[0], OUT_DIM), dtype=xf.dtype)
        for tslot in range(2):
            idx = topi[:, tslot]
            wt = topw[:, tslot:tslot + 1]
            h = jnp.einsum('nri,ni->nr', B[idx], xf)
            y = jnp.einsum('nor,nr->no', A[idx], h) + bias[idx]
            out = out + wt * y
        return out.reshape(*lead, OUT_DIM)

    def _L3_attn_ref(x, W_dq, W_uq, W_dkv, W_uk, W_uv, W_o):
        import jax, jax.numpy as jnp
        import numpy as np
        from math import sqrt
        N_HEAD = 16
        W_SCALE = 0.02

        def _reference_tuple_inner(x, W_dq, W_uq, W_dkv, W_uk, W_uv, W_o):
            B, T, C = x.shape
            nh = N_HEAD
            hs = C // nh
            n_kvl = W_dkv.shape[0]
            k_eff = (W_dq.T @ W_uq.T @ W_uk).reshape(nh, hs, n_kvl)
            v_eff = jnp.transpose((W_uv.T @ W_o.T).reshape(n_kvl, nh, hs), (1, 0, 2))
            c_kv = x @ W_dkv.T
            q = x @ W_dq.T @ W_uq.T
            q = q.reshape(B, T, nh, hs)
            q_lat = jnp.einsum('bqhd,hdl->bhql', q, k_eff)
            attn = jnp.einsum('bhql,bkl->bhqk', q_lat, c_kv) / sqrt(hs)
            causal = jnp.tril(jnp.ones((T, T), dtype=bool))
            attn = jnp.where(causal[None, None], attn, -jnp.inf)
            attn = jax.nn.softmax(attn, axis=-1)
            y_lat = jnp.einsum('bhqk,bkl->bhql', attn, c_kv)
            y = jnp.einsum('bhql,hld->bqhd', y_lat, v_eff).reshape(B, T, C)
            return (y, c_kv)
        return _reference_tuple_inner(x, W_dq, W_uq, W_dkv, W_uk, W_uv, W_o)[0]

    def _L3_xattn_ref(x, context, g_x, b_x, g_c, b_c, Wq, Wk, Wv, Wo):
        import jax, jax.numpy as jnp
        import numpy as np
        DIM = 256
        CTX_DIM = 192
        H = 16
        DH = 64
        INNER = H * DH
        EPS = 1e-05

        def layer_norm(x, gamma, beta):
            mu = jnp.mean(x, axis=-1, keepdims=True)
            var = jnp.mean(jnp.square(x - mu), axis=-1, keepdims=True)
            return (x - mu) * jax.lax.rsqrt(var + EPS) * gamma + beta
        B, N, _ = x.shape
        M = context.shape[1]
        xn = layer_norm(x, g_x, b_x)
        cn = layer_norm(context, g_c, b_c)
        q = (xn @ Wq).reshape(B, N, H, DH).transpose(0, 2, 1, 3)
        k = (cn @ Wk).reshape(B, M, H, DH).transpose(0, 2, 1, 3)
        v = (cn @ Wv).reshape(B, M, H, DH).transpose(0, 2, 1, 3)
        scale = jnp.float32(1.0 / np.sqrt(DH))
        sim = jnp.einsum('bhid,bhjd->bhij', q, k) * scale
        attn = jax.nn.softmax(sim, axis=-1)
        out = jnp.einsum('bhij,bhjd->bhid', attn, v)
        out = out.transpose(0, 2, 1, 3).reshape(B, N, INNER)
        return out @ Wo

    def _L3_ffn_ref(x, ln_scale, ln_bias, attn_w, attn_b, gate_w, w1, b1, w2, b2, next_w, next_b):
        import jax, jax.numpy as jnp
        import numpy as np
        MICRO_BATCHES = 2
        TOP_K = 2
        NUM_EXPERTS = 8
        B, S, D = (4, 1024, 256)
        H = 4 * D
        b, s, d = x.shape
        flat = x.reshape(b * s, d)
        mu = jnp.mean(flat, axis=-1, keepdims=True)
        var = jnp.mean((flat - mu) ** 2, axis=-1, keepdims=True)
        xn = (flat - mu) * jax.lax.rsqrt(var + 1e-05) * ln_scale + ln_bias
        x_attn = xn @ attn_w.T + attn_b + flat
        logits = x_attn @ gate_w.T
        _vals, _idx = jax.lax.top_k(logits, TOP_K)
        e = w1.shape[0]
        n = b * s // (MICRO_BATCHES * e)
        xe = x_attn.reshape(MICRO_BATCHES, e, n, d)
        h = jax.nn.gelu(jnp.einsum('mend,edh->menh', xe, w1) + b1[None, :, None, :], approximate=False)
        eo = jnp.einsum('menh,ehd->mend', h, w2) + b2[None, :, None, :]
        eo = eo.reshape(b * s, d)
        out = jax.nn.gelu(eo @ next_w.T + next_b, approximate=False)
        return out.reshape(b, s, d)
    x = _layernorm(x + _L0_attn_ref(x, L0_attn_W_in, L0_attn_b_in, L0_attn_in_ln_w, L0_attn_in_ln_b, L0_attn_W_out, L0_attn_out_ln_w, L0_attn_out_ln_b, L0_attn_smear_factor, L0_attn_log_scale), axis=-1)
    x = _layernorm(x + _L0_xattn_ref(x, ctx_768, L0_xattn_Wq, L0_xattn_Wk, L0_xattn_Wv, L0_xattn_Wout, L0_xattn_bout), axis=-1)
    x = _layernorm(x + _L0_ffn_ref(x, L0_ffn_gate_w, L0_ffn_bias, L0_ffn_W1, L0_ffn_W3, L0_ffn_W2, L0_ffn_sw1, L0_ffn_sw3, L0_ffn_sw2), axis=-1)
    x = _layernorm(x + _L1_attn_ref(x, L1_attn_Wq, L1_attn_Wk, L1_attn_Wv, L1_attn_Wo), axis=-1)
    x = _layernorm(x + _L1_xattn_ref(x, ctx_768, L1_xattn_Wq, L1_xattn_bq, L1_xattn_Wkv, L1_xattn_bkv, L1_xattn_Wo, L1_xattn_bo), axis=-1)
    x = _layernorm(x + _L1_ffn_ref(x, L1_ffn_Ws1, L1_ffn_Ws2, L1_ffn_W1, L1_ffn_W2, L1_ffn_Wr), axis=-1)
    x = _layernorm(x + _L2_attn_ref(x, L2_attn_Wq, L2_attn_Wk, L2_attn_Wv, L2_attn_Wo), axis=-1)
    x = _layernorm(x + _L2_xattn_ref(x, ctx_768, L2_xattn_Wq, L2_xattn_Wk, L2_xattn_Wv, L2_xattn_Wo, L2_xattn_bo), axis=-1)
    x = _layernorm(x + _L2_ffn_ref(x, L2_ffn_prototypes, L2_ffn_B, L2_ffn_A, L2_ffn_bias, L2_ffn_temp), axis=-1)
    x = _layernorm(x + _L3_attn_ref(x, L3_attn_W_dq, L3_attn_W_uq, L3_attn_W_dkv, L3_attn_W_uk, L3_attn_W_uv, L3_attn_W_o), axis=-1)
    x = _layernorm(x + _L3_xattn_ref(x, ctx_768, L3_xattn_g_x, L3_xattn_b_x, L3_xattn_g_c, L3_xattn_b_c, L3_xattn_Wq, L3_xattn_Wk, L3_xattn_Wv, L3_xattn_Wo), axis=-1)
    x = _layernorm(x + _L3_ffn_ref(x, L3_ffn_ln_scale, L3_ffn_ln_bias, L3_ffn_attn_w, L3_ffn_attn_b, L3_ffn_gate_w, L3_ffn_w1, L3_ffn_b1, L3_ffn_w2, L3_ffn_b2, L3_ffn_next_w, L3_ffn_next_b), axis=-1)
    return x

_drawn_inputs = setup_inputs


def setup_inputs(seed=0):
    import zlib

    import numpy as np

    out = dict(_drawn_inputs(seed))
    spreads = {'L0_attn_in_ln_w': (1.0, 0.2),
     'L0_attn_in_ln_b': (0.0, 0.1),
     'L0_attn_out_ln_w': (1.0, 0.2),
     'L0_attn_out_ln_b': (0.0, 0.1),
     'L0_attn_log_scale': (0.0, 0.8),
     'L0_xattn_bout': (0.0, 0.1),
     'L0_ffn_bias': (0.0, 0.8),
     'L2_ffn_bias': (0.0, 0.1),
     'L3_xattn_g_x': (1.0, 0.2),
     'L3_xattn_b_x': (0.0, 0.403),
     'L3_xattn_g_c': (1.0, 0.2),
     'L3_xattn_b_c': (0.0, 0.1),
     'L3_ffn_ln_scale': (1.0, 0.6),
     'L3_ffn_ln_bias': (0.0, 0.8),
     'L3_ffn_attn_b': (0.0, 0.8),
     'L3_ffn_b1': (0.0, 0.8),
     'L3_ffn_b2': (0.0, 0.506),
     'L3_ffn_next_b': (0.0, 0.1)}
    factors = {'L0_attn_smear_factor': 2.742,
     'L0_ffn_gate_w': 8.0,
     'L0_ffn_W1': 8.0,
     'L0_ffn_W3': 8.0,
     'L0_ffn_W2': 8.0,
     'L0_ffn_sw1': 6.159,
     'L0_ffn_sw3': 6.328,
     'L0_ffn_sw2': 6.432,
     'L1_attn_Wq': 8.0,
     'L1_attn_Wk': 8.0,
     'L1_xattn_bq': 8.0,
     'L1_xattn_bkv': 5.952,
     'L1_xattn_bo': 5.782,
     'L1_ffn_Ws1': 2.89,
     'L2_xattn_bo': 5.748,
     'L2_ffn_B': 3.812,
     'L2_ffn_A': 3.781,
     'L3_attn_W_dq': 8.0,
     'L3_attn_W_uq': 8.0,
     'L3_attn_W_dkv': 3.72,
     'L3_attn_W_uk': 8.0,
     'L3_attn_W_uv': 3.964,
     'L3_attn_W_o': 4.195,
     'L3_ffn_attn_w': 8.0,
     'L3_ffn_w1': 3.042,
     'L3_ffn_w2': 2.768}
    for name, (base, spread) in spreads.items():
        noise = np.random.default_rng([zlib.crc32(name.encode()), seed]).standard_normal(out[name].shape)
        drawn = base * np.exp(spread * noise) if base else spread * noise
        out[name] = jnp.asarray(drawn.astype(out[name].dtype))
    for name, factor in factors.items():
        out[name] = (out[name] * factor).astype(out[name].dtype)
    return out
```

```python
from contextlib import ExitStack, contextmanager

import concourse.bass as bass
from concourse import mybir

F32 = mybir.dt.float32
BF16 = mybir.dt.bfloat16
ALU = mybir.AluOpType
ACT = mybir.ActivationFunctionType
AX = mybir.AxisListType

P = 128
D = 256
DC = D // P
B, T = 2, 1024
N = B * T
NT = N // P
TB = T // P
M = 77
CTX = 192
EPS = 1e-5
GT = 4
GN = GT * P
NG = N // GN
ds = bass.ds


@contextmanager
def times(eng, n):
    if n == 1:
        yield 0
    else:
        with eng.Fori(0, n) as i:
            yield i


class Count:

    def __init__(self, eng, sem, n, turn):
        self.eng, self.sem, self.n, self.turn, self.at = eng, sem, n, turn, 0

    def step(self, ins):
        ins.then_inc(self.sem, 1)
        self.at += 1
        return self.at

    def value(self, at=None):
        return self.turn * self.n + (self.at if at is None else at)

    def wait(self, at=None):
        self.eng.wait_ge(self.sem, self.value(at))

    def close(self):
        assert self.at == self.n, f"{self.at} steps in a turn, not {self.n}"


class Phase:

    def __init__(self, k, name):
        self.k, self.name, self.ctx, self.sems, self.s = k, name, ExitStack(), [], {}

    def sb(self, name, shape, dt=F32):
        return self.ctx.enter_context(self.k.nc.sbuf_tensor(f"{self.name}_{name}", shape, dt))

    def sem(self, name):
        s = self.k.nc.alloc_semaphore(f"{self.name}_{name}")
        self.sems.append(s)
        return s

    def sems_of(self, names):
        self.s.update({n: self.sem(n) for n in names.split()})

    def __enter__(self):
        return self

    def __exit__(self, *exc):
        if exc[0] is None:
            self.ctx.close()
            self.k.nc.clear_and_free_semaphores(self.sems)
            self.k.nc.all_engine_barrier()


def weight_rows(w, kc=None):
    return w.rearrange("(c p) n -> p c n", p=P)


class Tail:

    def __init__(self, ph, x_in, x_out, xt_out, bias=None, pre=None):
        self.ph, self.x_in, self.x_out, self.xt_out, self.bias, self.pre = ph, x_in, x_out, xt_out, bias, pre
        k = ph.k
        self.y = k.ps[:, 2:4, :].rearrange("p b (t d) -> p (b t) d", d=D)
        self.tp = k.ps[:, 4:6, :]
        self.xin = ph.sb("xin", [P, GT, D])
        self.r = ph.sb("r", [P, GT, D])
        self.stats = ph.sb("stats", [P, GT, 6])
        self.mv = ph.sb("mv", [P, GT, 2])
        self.ve = ph.sb("ve", [P, GT])
        self.gap = ph.sb("gap", [P, 1])
        self.sd = ph.sb("sd", [P, GT])
        self.rs = ph.sb("rs", [P, GT])
        self.xn = ph.sb("xn", [P, GT, D])
        self.xts = ph.sb("xts", [P, DC, GN])
        ph.sems_of("y_ready xin_ld r_done chain ve_ready sd_ready xn_ready xn_turned xts_ready x_st xt_st")
        self.norms = 2 if pre else 1
        self.n_chain = (self.norms - 1) * (3 * GT + 3) + (bias is not None) + 2 * GT + 1

    def load(self, sp, g):
        ph = self.ph
        sp.wait_ge(ph.s["r_done"], g)
        sp.dma_start(self.xin[:], self.x_in[ds(g * GN, GN), :].rearrange("(t p) d -> p t d", p=P)).then_inc(ph.s["xin_ld"], 16)

    def store(self, pool, g):
        ph = self.ph
        pool.wait_ge(ph.s["xn_ready"], g + 1)
        pool.dma_start(self.x_out[ds(g * GN, GN), :].rearrange("(t p) d -> p t d", p=P), self.xn[:]).then_inc(ph.s["x_st"], 16)
        if self.xt_out is not None:
            pool.wait_ge(ph.s["xts_ready"], g + 1)
            pool.dma_start(self.xt_out[:, ds(g * GN, GN)].rearrange("(c p) t -> p c t", p=P), self.xts[:]).then_inc(ph.s["xt_st"], 16)

    def finish(self, pool):
        pool.wait_ge(self.ph.s["x_st"], 16 * NG)
        if self.xt_out is not None:
            pool.wait_ge(self.ph.s["xt_st"], 16 * NG)

    def _norm(self, dve, ch, g, n, src, dst, done=None):
        ph = self.ph
        for t in range(GT):
            ch.step(dve.bn_stats(self.stats[:, t, :], src[:, t, :]))
        ch.wait()
        dve.memset(self.gap[:], 0.0)
        for t in range(GT):
            ch.step(dve.bn_aggr(self.mv[:, t, :], self.stats[:, t, :]))
        ch.wait()
        dve.tensor_scalar(self.ve[:], self.mv[:, :, 1], EPS, None, ALU.add).then_inc(ph.s["ve_ready"], 1)
        dve.wait_ge(ph.s["sd_ready"], self.norms * g + n + 1)
        ch.step(dve.reciprocal(self.rs[:], self.sd[:]))
        ch.wait()
        for t in range(GT):
            ins = dve.tensor_scalar(dst[:, t, :], src[:, t, :], self.mv[:, t, 0:1], self.rs[:, t:t + 1],
                                    ALU.subtract, ALU.mult)
            if done is None:
                ch.step(ins)
        if done is None:
            ch.wait()
        else:
            ins.then_inc(done, 1)

    def vector(self, dve, g):
        ph = self.ph
        ch = Count(dve, ph.s["chain"], self.n_chain, g)
        dve.wait_ge(ph.s["y_ready"], g + 1)
        y = self.y
        if self.pre:
            w, b = self.pre
            self._norm(dve, ch, g, 0, self.y, self.r)
            for v, op in ((w, ALU.mult), (b, ALU.add)):
                ch.step(dve.tensor_tensor(self.r[:], self.r[:], v[:, None, :].to_broadcast([P, GT, D]), op))
                ch.wait()
            y = self.r
        dve.wait_ge(ph.s["xin_ld"], 16 * g + 16)
        dve.tensor_tensor(self.r[:], y[:], self.xin[:], ALU.add).then_inc(ph.s["r_done"], 1)
        dve.wait_ge(ph.s["r_done"], g + 1)
        if self.bias is not None:
            ch.step(dve.tensor_tensor(self.r[:], self.r[:], self.bias[:, None, :].to_broadcast([P, GT, D]), ALU.add))
            ch.wait()
        dve.wait_ge(ph.s["x_st"], 16 * g)
        if self.xt_out is not None:
            dve.wait_ge(ph.s["xn_turned"], g)
        self._norm(dve, ch, g, self.norms - 1, self.r, self.xn, ph.s["xn_ready"])
        ch.close()

    def scalar(self, act, g):
        ph = self.ph
        for n in range(self.norms):
            act.wait_ge(ph.s["ve_ready"], self.norms * g + n + 1)
            act.activation(self.sd[:], self.ve[:], ACT.Sqrt).then_inc(ph.s["sd_ready"], 1)
        if self.xt_out is not None:
            act.wait_ge(ph.s["xn_turned"], g + 1)
            act.wait_ge(ph.s["xt_st"], 16 * g)
            act.activation(self.xts[:], self.tp, ACT.Copy).then_inc(ph.s["xts_ready"], 1)

    def tensor(self, pe, g):
        ph = self.ph
        if self.xt_out is None:
            return
        pe.wait_ge(ph.s["xn_ready"], g + 1)
        pe.wait_ge(ph.s["xts_ready"], g)
        for c in range(DC):
            for t in range(GT):
                ins = pe.transpose(self.tp[:, c, t * P:(t + 1) * P], self.xn[:, t, c * P:(c + 1) * P], ph.k.ident[:])
        ins.then_inc(ph.s["xn_turned"], 1)


def norm_columns(k, name, x_in, xnt_out, w_col, b_col, x_rows=None):
    nc = k.nc
    with Phase(k, name) as ph:
        xin = ph.sb("xin", [P, 2, GT, D])
        xc = ph.sb("xc", [P, GT, D])
        wb = ph.sb("wb", [P, 2, DC])
        stats, mv = ph.sb("stats", [P, GT, 6]), ph.sb("mv", [P, GT, 2])
        ve, sd, rs = ph.sb("ve", [P, GT]), ph.sb("sd", [P, GT]), ph.sb("rs", [P, GT])
        gap = ph.sb("gap", [P, 1])
        xts = ph.sb("xts", [P, DC, GN])
        tp = k.ps[:, 4:6, :]
        ph.sems_of("wb_ld xin_ld chain ve_ready sd_ready xc_ready turned xts_ready xt_st")
        with nc.Block() as block:

            @block.sync
            def _(sp):
                sp.dma_start(wb[:, 0, :], w_col).then_inc(ph.s["wb_ld"], 16)
                sp.dma_start(wb[:, 1, :], b_col).then_inc(ph.s["wb_ld"], 16)
                with sp.Fori(0, NG) as g:
                    sp.wait_ge(ph.s["xc_ready"], g)
                    sp.dma_start(xin[:, 0, :, :], x_in[ds(g * GN, GN), :].rearrange("(t p) d -> p t d", p=P)).then_inc(ph.s["xin_ld"], 16)

            @block.vector
            def _(dve):
                with dve.Fori(0, NG) as g:
                    ch = Count(dve, ph.s["chain"], 2 * GT + 1, g)
                    dve.wait_ge(ph.s["xin_ld"], 16 * g + 16)
                    for t in range(GT):
                        ch.step(dve.bn_stats(stats[:, t, :], xin[:, 0, t, :]))
                    ch.wait()
                    dve.memset(gap[:], 0.0)
                    for t in range(GT):
                        ch.step(dve.bn_aggr(mv[:, t, :], stats[:, t, :]))
                    ch.wait()
                    dve.tensor_scalar(ve[:], mv[:, :, 1], EPS, None, ALU.add).then_inc(ph.s["ve_ready"], 1)
                    dve.wait_ge(ph.s["sd_ready"], g + 1)
                    ch.step(dve.reciprocal(rs[:], sd[:]))
                    ch.wait()
                    dve.wait_ge(ph.s["turned"], g)
                    for t in range(GT):
                        ins = dve.tensor_scalar(xc[:, t, :], xin[:, 0, t, :], mv[:, t, 0:1], rs[:, t:t + 1],
                                                ALU.subtract, ALU.mult)
                    ins.then_inc(ph.s["xc_ready"], 1)
                    ch.close()

            @block.scalar
            def _(act):
                act.wait_ge(ph.s["wb_ld"], 32)
                with act.Fori(0, NG) as g:
                    act.wait_ge(ph.s["ve_ready"], g + 1)
                    act.activation(sd[:], ve[:], ACT.Sqrt).then_inc(ph.s["sd_ready"], 1)
                    act.wait_ge(ph.s["turned"], g + 1)
                    act.wait_ge(ph.s["xt_st"], 16 * g)
                    for c in range(DC):
                        ins = act.activation(xts[:, c, :], tp[:, c, :], ACT.Identity, scale=wb[:, 0, c:c + 1],
                                             bias=wb[:, 1, c:c + 1])
                    ins.then_inc(ph.s["xts_ready"], 1)

            @block.tensor
            def _(pe):
                with pe.Fori(0, NG) as g:
                    pe.wait_ge(ph.s["xc_ready"], g + 1)
                    pe.wait_ge(ph.s["xts_ready"], g)
                    for c in range(DC):
                        for t in range(GT):
                            ins = pe.transpose(tp[:, c, t * P:(t + 1) * P], xc[:, t, c * P:(c + 1) * P], k.ident[:])
                    ins.then_inc(ph.s["turned"], 1)

            @block.gpsimd
            def _(pool):
                with pool.Fori(0, NG) as g:
                    pool.wait_ge(ph.s["xts_ready"], g + 1)
                    pool.dma_start(xnt_out[:, ds(g * GN, GN)].rearrange("(c p) t -> p c t", p=P), xts[:]).then_inc(ph.s["xt_st"], 16)
                pool.wait_ge(ph.s["xt_st"], 16 * NG)


class Unit:

    def __init__(self, tiles, scores, mask_at, maxima, exps, turns, values, group, first, last):
        self.tiles, self.scores, self.mask_at, self.maxima, self.exps = tiles, scores, mask_at, maxima, exps
        self.turns, self.values, self.group, self.first, self.last = turns, values, group, first, last


def causal_units(dh):
    per = min(TB, 512 // dh)
    units = []
    for b in range(B):
        for i in range(TB):
            w = (i + 1) * P
            scores = [(c, min(512, w - c), b * TB + i, b * T + c) for c in range(0, w, 512)]
            turns = [[(j * P, P, j * P) for j in range(c, min(c + 4, i + 1))] for c in range(0, i + 1, 4)]
            n = len(units)
            units.append(Unit([b * TB + i], scores, i * P, [(0, w)], [(0, 0, w)], turns,
                              [[(j * P, b * TB + j) for j in range(i + 1)]], n // per, n % per == 0, n % per == per - 1))
            units[-1].slot, units[-1].per = n % per, per
    return units


def cross_units(dh, keys, n_blocks):
    units = []
    step = P if n_blocks == 1 else 2 * P
    for u in range(NT // GT):
        tiles = [GT * u + j for j in range(GT)]
        kb = [tiles[0] // TB] if n_blocks == 1 else list(range(n_blocks))
        scores = [(j * step, n_blocks * M, t, kb[0] * M) for j, t in enumerate(tiles)]
        turns = [[(j * step + n * M, M, n * 512 + j * P) for j in range(GT)] for n in range(n_blocks)]
        values = [[(n * 512 + j * P, kb[n]) for n in range(n_blocks)] for j in range(GT)]
        exps = [(j, j * step, j * step + n_blocks * M) for j in range(GT)]
        units.append(Unit(tiles, scores, None, [(j * step, n_blocks * M) for j in range(GT)], exps, turns, values, u, True, True))
        units[-1].slot, units[-1].per = 0, GT
        units[-1].step = step
    return units


def attention(k, name, units, heads, dk, dh, qt, kt, v_all, o_all, kv_of=1, n_keys=N, key_rows=P):
    nc = k.nc
    cross = units[0].mask_at is None
    HB = min(2, heads)
    turns = heads // HB
    U = len(units)
    kc = -(-dk // P)
    kd = min(dk, P)
    nblk = v_all.shape[1]
    small = heads > 1
    before = [sum(len(u.turns) for u in units[:i]) for i in range(U + 1)]
    G = before[-1]
    OG = units[-1].group + 1
    per = units[0].per
    with Phase(k, name) as ph:
        nslot = HB if small else 1
        qs = ph.sb("q", [kd, nslot, kc, N])
        ks = ph.sb("k", [kd, nslot, kc, n_keys])
        vs = ph.sb("v", [key_rows, HB, nblk, dh]) if small else None
        probs = ph.sb("probs", [P, 2, 1024])
        pt = ph.sb("pt", [P, 2, 1024])
        nmax = ph.sb("nmax", [P, 2, GT])
        sums = ph.sb("sums", [P, 2, per])
        rsum = ph.sb("rsum", [P, 2, per])
        ph.sems_of("passed scores max_done exps turned moved values normed recips")
        q_ld, k_ld = [ph.sem(f"q_ld{p}") for p in range(HB)], [ph.sem(f"k_ld{p}") for p in range(HB)]
        v_ready = [ph.sem(f"v_ready{p}") for p in range(HB)]
        S = [k.ps[:, 0:2, :].rearrange("p b c -> p (b c)"), k.ps[:, 2:4, :].rearrange("p b c -> p (b c)")]
        TP = [k.ps[:, 4, :], k.ps[:, 5, :]]
        O = [k.ps[:, 6, :], k.ps[:, 7, :]]
        steps = [(p, u) for p in range(HB) for u in range(U)]
        W = HB * U

        def groups_before(n):
            return (n // U) * G + before[n % U]

        with nc.Block() as block:

            @block.sync
            def _(sp):
                with times(sp, turns) as t:
                    base = t * W
                    for p in range(HB):
                        sp.wait_ge(ph.s["values"], base + (p + 1) * U)
                        if kv_of == 1:
                            kh = t * HB + p
                        else:
                            kh = (t * HB) // kv_of
                        src_q = qt[ds(t * HB + p, 1)].rearrange("h (c d) n -> d (h c) n", d=kd)
                        src_k = kt[ds(kh, 1)].rearrange("h (c d) n -> d (h c) n", d=kd)
                        sp.dma_start(qs[:, p, :, :], src_q).then_inc(q_ld[p], 16)
                        sp.dma_start(ks[:, p, :, :], src_k).then_inc(k_ld[p], 16)

            @block.gpsimd
            def _(pool):
                if not small:
                    return
                with times(pool, turns) as t:
                    for p in range(HB):
                        kh = t * HB + p if kv_of == 1 else (t * HB) // kv_of
                        pool.wait_ge(ph.s["values"], t * W + (p + 1) * U)
                        pool.sem_inc(ph.s["passed"], 1)
                        pool.tensor_copy(vs[:, p, :, :], v_all[0:key_rows, :, ds(kh * dh, dh)]).then_inc(v_ready[p], 1)

            @block.tensor
            def _(pe):
                pe.sem_inc(ph.s["values"], W)
                with times(pe, turns) as t:
                    base = t * W

                    def scores(n):
                        p, i = steps[n]
                        u = units[i]
                        if i == 0:
                            pe.wait_ge(q_ld[p], 16 * t + 16)
                            pe.wait_ge(k_ld[p], 16 * t + 16)
                        pe.wait_ge(ph.s["exps"], base + n + 1)
                        s = S[n % 2]
                        for c0, w, tile, key in u.scores:
                            own = u.mask_at is not None and c0 <= u.mask_at < c0 + w
                            for c in range(kc):
                                ins = pe.matmul(s[:, c0:c0 + w], qs[:, p, c, tile * P:(tile + 1) * P], ks[:, p, c, key:key + w],
                                                start=c == 0, stop=c == kc - 1 and not own)
                            if own:
                                ins = pe.matmul(s[:, u.mask_at:u.mask_at + P], k.ident_b[:], k.mask[:], start=False, stop=True)
                        ins.then_inc(ph.s["scores"], 1)

                    def turn(n):
                        p, i = steps[n]
                        u = units[i]
                        pe.wait_ge(ph.s["exps"], base + n + 3)
                        g0 = groups_before(n)
                        for a, group in enumerate(u.turns):
                            pe.wait_ge(ph.s["moved"], t * (HB * G) + g0 + a + 1)
                            for src, rows, dst in group:
                                at = dst % 512
                                ins = pe.transpose(TP[(g0 + a) % 2][0:rows, at:at + P], probs[:, n % 2, src:src + rows], k.ident[:])
                            ins.then_inc(ph.s["turned"], 1)

                    def values(n):
                        p, i = steps[n]
                        u = units[i]
                        if i == 0 and small:
                            pe.wait_ge(v_ready[p], t + 1)
                        pe.wait_ge(ph.s["moved"], t * (HB * G) + groups_before(n) + len(u.turns) + 2)
                        og = p * OG + u.group
                        if u.first:
                            pe.wait_ge(ph.s["normed"], t * (HB * OG) + og + 1)
                        for j, blocks in enumerate(u.values):
                            o = O[og % 2][:, (u.slot + j) * dh:(u.slot + j + 1) * dh]
                            for a, (src, blk) in enumerate(blocks):
                                v = vs[:, p, blk, :] if small else v_all[0:key_rows, blk, :]
                                ins = pe.matmul(o, pt[0:key_rows, n % 2, src:src + P], v, start=a == 0, stop=a == len(blocks) - 1)
                        ins.then_inc(ph.s["values"], 1)

                    scores(0)
                    for n in range(W):
                        if n + 1 < W:
                            scores(n + 1)
                        turn(n)
                        if n:
                            values(n - 1)
                    values(W - 1)

            @block.scalar
            def _(act):
                act.sem_inc(ph.s["exps"], 2)
                with times(act, turns) as t:
                    base = t * W
                    for n, (p, i) in enumerate(steps):
                        u = units[i]
                        og = p * OG + u.group
                        act.wait_ge(ph.s["max_done"], base + n + 1)
                        act.wait_ge(ph.s["turned"], t * (HB * G) + (groups_before(n - 1) if n else 0))
                        if u.first:
                            act.wait_ge(ph.s["normed"], t * (HB * OG) + og + 1)
                        for j, c0, c1 in u.exps:
                            ins = act.activation(probs[:, n % 2, c0:c1], S[n % 2][:, c0:c1], ACT.Exp,
                                                 bias=nmax[:, n % 2, j:j + 1], accum_out=sums[:, og % 2, u.slot + j:u.slot + j + 1])
                        ins.then_inc(ph.s["exps"], 1)

            @block.vector
            def _(dve):
                dve.sem_inc(ph.s["moved"], 2)
                dve.sem_inc(ph.s["normed"], 2)
                with times(dve, turns) as t:
                    base = t * W

                    def maximum(n):
                        p, i = steps[n]
                        u = units[i]
                        dve.wait_ge(ph.s["scores"], base + n + 1)
                        if cross:
                            w = u.maxima[0][1]
                            src = S[n % 2][:, 0:GT * u.step].rearrange("p (j c) -> p j c", j=GT)[:, :, 0:w]
                            ins = dve.tensor_reduce(nmax[:, n % 2, 0:GT], src, AX.X, ALU.max, negate=True)
                        else:
                            ins = dve.tensor_reduce(nmax[:, n % 2, 0:1], S[n % 2][:, 0:u.maxima[0][1]], AX.X, ALU.max, negate=True)
                        ins.then_inc(ph.s["max_done"], 1)

                    def move(n):
                        p, i = steps[n]
                        u = units[i]
                        g0 = groups_before(n)
                        dve.wait_ge(ph.s["values"], base + W + max(n - 1, 0))
                        for a, group in enumerate(u.turns):
                            dve.wait_ge(ph.s["turned"], t * (HB * G) + g0 + a + 1)
                            rows = group[0][1]
                            lo, w = group[0][2], len(group) * P
                            dve.tensor_copy(pt[0:rows, n % 2, lo:lo + w], TP[(g0 + a) % 2][0:rows, 0:w]).then_inc(ph.s["moved"], 1)

                    def norm(n):
                        p, i = steps[n]
                        u = units[i]
                        if not u.last:
                            return
                        og = p * OG + u.group
                        dve.wait_ge(ph.s["exps"], base + n + 3)
                        dve.wait_ge(ph.s["values"], base + W + n + 1)
                        dve.reciprocal(rsum[:, og % 2, :], sums[:, og % 2, :]).then_inc(ph.s["recips"], 1)
                        dve.wait_ge(ph.s["recips"], t * (HB * OG) + og + 1)
                        tile0 = u.tiles[-1] - per + 1
                        src = O[og % 2][:, 0:per * dh].rearrange("p (t d) -> p t d", d=dh)
                        h = t * HB + p
                        dst = o_all[:, tile0:tile0 + per, ds(h * dh, dh)]
                        dve.tensor_tensor(dst, src, rsum[:, og % 2, :, None].to_broadcast([P, per, dh]), ALU.mult).then_inc(ph.s["normed"], 1)

                    maximum(0)
                    for n in range(W):
                        if n + 1 < W:
                            maximum(n + 1)
                        move(n)
                        if n:
                            norm(n - 1)
                    norm(W - 1)


def project_out(k, name, o_all, F, wo, x_in, x_out, xt_out, bias=None, pre=None, gate=None):
    nc = k.nc
    FC = F // P
    with Phase(k, name) as ph:
        tail_bias = ph.sb("bias", [P, D]) if bias is not None else None
        own = [ph.sb("ln_w", [P, D]), ph.sb("ln_b", [P, D])] if pre else None
        tail = Tail(ph, x_in, x_out, xt_out, tail_bias, own)
        w = ph.sb("w", [P, FC, D]) if wo is not None else None
        o_rows = ph.sb("o_rows", [P, GT, F])
        o_cols = ph.sb("o_cols", [P, FC, GN]) if wo is not None else None
        ph.sems_of("w_ld o_ready o_turned o_moved")
        n_ld = 16 * ((wo is not None) + (bias is not None) + 2 * bool(pre))
        TP = [k.ps[:, 0, :], k.ps[:, 1, :]]
        with nc.Block() as block:

            @block.sync
            def _(sp):
                if wo is not None:
                    sp.dma_start(w[:], weight_rows(wo)).then_inc(ph.s["w_ld"], 16)
                if bias is not None:
                    sp.dma_start(tail_bias[:], bias).then_inc(ph.s["w_ld"], 16)
                if pre:
                    sp.dma_start(own[0][:], pre[0]).then_inc(ph.s["w_ld"], 16)
                    sp.dma_start(own[1][:], pre[1]).then_inc(ph.s["w_ld"], 16)
                with sp.Fori(0, NG) as g:
                    tail.load(sp, g)

            @block.gpsimd
            def _(pool):
                with pool.Fori(0, NG) as g:
                    pool.wait_ge(ph.s["o_turned"] if wo is not None else ph.s["r_done"], g * FC if wo is not None else g)
                    src = o_all[:, ds(g * GT, GT), :]
                    if gate is not None:
                        ins = pool.tensor_tensor(o_rows[:], src, gate[:, ds(g * GT, GT), :], ALU.mult)
                    else:
                        ins = pool.tensor_copy(o_rows[:], src)
                    ins.then_inc(ph.s["o_ready"] if wo is not None else ph.s["y_ready"], 1)
                    tail.store(pool, g)
                tail.finish(pool)

            if wo is None:
                tail.y = o_rows

            @block.tensor
            def _(pe):
                if wo is not None:
                    pe.wait_ge(ph.s["w_ld"], n_ld)
                with pe.Fori(0, NG) as g:
                    if wo is not None:
                        pe.wait_ge(ph.s["o_ready"], g + 1)
                        for c in range(FC):
                            pe.wait_ge(ph.s["o_moved"], g * FC + max(c - 1, 0))
                            for t in range(GT):
                                ins = pe.transpose(TP[c % 2][:, t * P:(t + 1) * P], o_rows[:, t, c * P:(c + 1) * P], k.ident[:])
                            ins.then_inc(ph.s["o_turned"], 1)
                        pe.wait_ge(ph.s["o_moved"], g * FC + FC)
                        pe.wait_ge(ph.s["r_done"], g)
                        for t in range(GT):
                            for c in range(FC):
                                ins = pe.matmul(tail.y[:, t, :], o_cols[:, c, t * P:(t + 1) * P], w[:, c, :], start=c == 0, stop=c == FC - 1)
                        ins.then_inc(ph.s["y_ready"], 1)
                    tail.tensor(pe, g)

            @block.scalar
            def _(act):
                with act.Fori(0, NG) as g:
                    if wo is not None:
                        act.wait_ge(ph.s["y_ready"], g)
                        for c in range(FC):
                            act.wait_ge(ph.s["o_turned"], g * FC + c + 1)
                            act.activation(o_cols[:, c, :], TP[c % 2][:], ACT.Copy).then_inc(ph.s["o_moved"], 1)
                    tail.scalar(act, g)

            @block.vector
            def _(dve):
                if n_ld:
                    dve.wait_ge(ph.s["w_ld"], n_ld)
                with dve.Fori(0, NG) as g:
                    tail.vector(dve, g)


def l0_self_attention(k, x_in, x_out, xt_out):
    nc, a = k.nc, k.a
    H, E = 16, 512
    DH = E // H
    EC = E // P
    HPC = P // DH
    DK = DH + 2
    norm_columns(k, "l0n", x_in, k.xnt, a["L0_attn_in_ln_w"], a["L0_attn_in_ln_b"])
    qt, kt = k.dram("l0_qt", [H, DK, N]), k.dram("l0_kt", [H, DK, N])
    with ExitStack() as keep:
        v_all = keep.enter_context(nc.sbuf_tensor("l0_v_all", [P, NT, E], F32))
        o_all = keep.enter_context(nc.sbuf_tensor("l0_o_all", [P, NT, E], F32))
        gate = keep.enter_context(nc.sbuf_tensor("l0_gate", [P, NT, E], F32))
        with Phase(k, "l0p") as ph:
            w = ph.sb("w", [P, DC, 4 * E + H])
            bc = ph.sb("bc", [P, 2 * EC])
            by = ph.sb("by", [H, 1])
            brow = ph.sb("brow", [P, 2 * E])
            hf = ph.sb("hf", [P, 2, EC])
            sg = ph.sb("sg", [P, 6, EC])
            qb, kb = ph.sb("qb", [P, EC]), ph.sb("kb", [P, EC])
            xs = ph.sb("xs", [P, DC, T])
            st = ph.sb("st", [P, 2, T])
            kraw = ph.sb("kraw", [P, T])
            vtmp = ph.sb("vtmp", [P, E])
            sig = ph.sb("sig", [H, T])
            ones = ph.sb("ones", [H, T])
            pos = ph.sb("pos", [H, T])
            npos = ph.sb("npos", [H, T])
            ph.sems_of("w_ld x_ld prep pe_done act_q kraw_ready smear k_ready st_st0 st_st1 sig_ready ones_ready "
                       "pos_ready pos_st v_ready gate_sum gate_ready act_prep y_done ones_st")
            st_st = [ph.s["st_st0"], ph.s["st_st1"]]
            PA = [k.ps[:, 0:2, :].rearrange("p b c -> p (b c)"), k.ps[:, 2:4, :].rearrange("p b c -> p (b c)")]
            PY = k.ps[0:H, 4:6, :].rearrange("p b c -> p (b c)")
            PV, PG = k.ps[:, 6, :], k.ps[:, 7, :]
            CH = 2 * EC
            with nc.Block() as block:

                @block.sync
                def _(sp):
                    for dst, src in ((w[:], weight_rows(a["L0_attn_W_in"])), (bc[:], a["L0_attn_b_col"]), (by[:], a["L0_attn_b_y"]),
                                     (brow[:], a["L0_attn_b_row"]), (hf[:], a["L0_attn_by_head"])):
                        sp.dma_start(dst, src).then_inc(ph.s["w_ld"], 16)
                    with sp.Fori(0, B) as b:
                        sp.wait_ge(ph.s["pe_done"], b * (CH + 1 + 2 * TB))
                        sp.dma_start(xs[:], k.xnt[:, ds(b * T, T)].rearrange("(c p) t -> p c t", p=P)).then_inc(ph.s["x_ld"], 16)
                        for c in range(CH):
                            dst = qt if c < EC else kt
                            sp.wait_ge(ph.s["act_q"] if c < EC else ph.s["k_ready"], b * EC + c % EC + 1)
                            for h in range(HPC):
                                sp.dma_start(dst[(c % EC) * HPC + h, 0:DH, ds(b * T, T)], st[h * DH:(h + 1) * DH, c % 2, :])\
                                    .then_inc(st_st[c % 2], 16)

                @block.gpsimd
                def _(pool):
                    pool.memset(ones[:], 1.0).then_inc(ph.s["ones_ready"], 1)
                    pool.wait_ge(ph.s["ones_ready"], 1)
                    for b in range(B):
                        pool.dma_start(qt[:, DH, b * T:(b + 1) * T], ones[:]).then_inc(ph.s["ones_st"], 16)
                        pool.dma_start(kt[:, DH + 1, b * T:(b + 1) * T], ones[:]).then_inc(ph.s["ones_st"], 16)
                    with pool.Fori(0, B) as b:
                        pool.wait_ge(ph.s["pos_ready"], 2 * b + 2)
                        pool.dma_start(kt[:, DH, ds(b * T, T)], pos[:]).then_inc(ph.s["pos_st"], 16)
                        pool.dma_start(qt[:, DH + 1, ds(b * T, T)], npos[:]).then_inc(ph.s["pos_st"], 16)
                    pool.wait_ge(ph.s["ones_st"], 64)
                    pool.wait_ge(ph.s["pos_st"], 16 * 2 * B)
                    for s in st_st:
                        pool.wait_ge(s, 16 * HPC * B * EC)

                @block.tensor
                def _(pe):
                    pe.wait_ge(ph.s["w_ld"], 80)
                    with pe.Fori(0, B) as b:
                        pe.wait_ge(ph.s["x_ld"], 16 * b + 16)
                        pe.wait_ge(ph.s["sig_ready"], b)
                        for half in range(2):
                            for c in range(DC):
                                ins = pe.matmul(PY[:, half * 512:(half + 1) * 512], w[:, c, 4 * E:4 * E + H],
                                                xs[:, c, half * 512:(half + 1) * 512], start=c == 0, stop=c == DC - 1)
                        ins.then_inc(ph.s["pe_done"], 1)
                        for c in range(CH):
                            if c < 2:
                                pe.wait_ge(ph.s["kraw_ready"], b * EC)
                            elif c < EC + 2:
                                pe.wait_ge(ph.s["act_q"], b * EC + c - 1)
                            else:
                                pe.wait_ge(ph.s["kraw_ready"], b * EC + c - EC - 1)
                            for half in range(2):
                                for d in range(DC):
                                    ins = pe.matmul(PA[c % 2][:, half * 512:(half + 1) * 512], w[:, d, c * P:(c + 1) * P],
                                                    xs[:, d, half * 512:(half + 1) * 512], start=d == 0, stop=d == DC - 1)
                            ins.then_inc(ph.s["pe_done"], 1)
                        for j in range(TB):
                            pe.wait_ge(ph.s["v_ready"], b * TB + j)
                            for d in range(DC):
                                ins = pe.matmul(PV, xs[:, d, j * P:(j + 1) * P], w[:, d, 2 * E:3 * E], start=d == 0, stop=d == DC - 1)
                            ins.then_inc(ph.s["pe_done"], 1)
                            pe.wait_ge(ph.s["gate_sum"], b * TB + j)
                            for d in range(DC):
                                ins = pe.matmul(PG, xs[:, d, j * P:(j + 1) * P], w[:, d, 3 * E:4 * E], start=d == 0, stop=d == DC - 1)
                            ins.then_inc(ph.s["pe_done"], 1)

                @block.scalar
                def _(act):
                    act.wait_ge(ph.s["w_ld"], 80)
                    act.activation(sg[:, 0, :], hf[:, 0, :], ACT.Sigmoid).then_inc(ph.s["act_prep"], 1)
                    act.activation(sg[:, 1, :], hf[:, 1, :], ACT.Exp, scale=-1.0).then_inc(ph.s["act_prep"], 1)
                    act.wait_ge(ph.s["prep"], 5)
                    with act.Fori(0, B) as b:
                        done = b * (CH + 1 + 2 * TB)
                        act.wait_ge(ph.s["pe_done"], done + 1)
                        act.wait_ge(ph.s["pos_ready"], 2 * b)
                        act.activation(sig[:], PY, ACT.Sigmoid, bias=by[:, 0:1]).then_inc(ph.s["sig_ready"], 1)
                        for c in range(CH):
                            act.wait_ge(ph.s["pe_done"], done + c + 2)
                            e = c % EC
                            if c < EC:
                                if c >= 2:
                                    act.wait_ge(st_st[c % 2], 16 * HPC * (b * EC + c // 2))
                                else:
                                    act.wait_ge(st_st[c % 2], 16 * HPC * (b * EC))
                                act.activation(st[:, c % 2, :], PA[c % 2], ACT.Identity, scale=sg[:, 2, e:e + 1], bias=qb[:, e:e + 1])\
                                    .then_inc(ph.s["act_q"], 1)
                            else:
                                act.wait_ge(ph.s["k_ready"], b * EC + e)
                                act.activation(kraw[:], PA[c % 2], ACT.Identity, scale=sg[:, 1, e:e + 1], bias=kb[:, e:e + 1])\
                                    .then_inc(ph.s["kraw_ready"], 1)
                        for j in range(TB):
                            act.wait_ge(ph.s["gate_sum"], b * TB + j + 1)
                            act.activation(gate[:, ds(b * TB + j, 1), :], vtmp[:, None, :], ACT.Silu).then_inc(ph.s["gate_ready"], 1)

                @block.vector
                def _(dve):
                    dve.wait_ge(ph.s["act_prep"], 2)
                    dve.tensor_scalar(sg[:, 2, :], sg[:, 1, :], DH ** -0.5, None, ALU.mult).then_inc(ph.s["prep"], 1)
                    dve.tensor_scalar(sg[:, 3, :], sg[:, 0, :], -1.0, 1.0, ALU.mult, ALU.add).then_inc(ph.s["prep"], 1)
                    dve.tensor_tensor(kb[:], bc[:, EC:2 * EC], sg[:, 1, :], ALU.mult).then_inc(ph.s["prep"], 1)
                    dve.wait_ge(ph.s["prep"], 3)
                    dve.tensor_tensor(qb[:], bc[:, 0:EC], sg[:, 2, :], ALU.mult).then_inc(ph.s["prep"], 1)
                    dve.wait_ge(ph.s["ones_ready"], 1)
                    dve.tensor_copy(sg[:, 4, :], sg[:, 3, :]).then_inc(ph.s["prep"], 1)
                    with dve.Fori(0, B) as b:
                        done = b * (CH + 1 + 2 * TB)
                        dve.wait_ge(ph.s["sig_ready"], b + 1)
                        dve.wait_ge(ph.s["pos_st"], 32 * b)
                        dve.tensor_tensor_scan(pos[:], ones[:], sig[:], 0.0, ALU.mult, ALU.add).then_inc(ph.s["pos_ready"], 1)
                        dve.wait_ge(ph.s["pos_ready"], 2 * b + 1)
                        dve.tensor_scalar(npos[:], pos[:], -1.0, None, ALU.mult).then_inc(ph.s["pos_ready"], 1)
                        for c in range(EC):
                            dve.wait_ge(ph.s["kraw_ready"], b * EC + c + 1)
                            n_st = 16 * HPC * (b * EC + EC // 2 + c // 2)
                            dve.wait_ge(st_st[c % 2], n_st)
                            s = st[:, c % 2, :]
                            dve.tensor_scalar(s, kraw[:], sg[:, 4, c:c + 1], None, ALU.mult).then_inc(ph.s["smear"], 1)
                            dve.wait_ge(ph.s["smear"], b * EC + c + 1)
                            dve.scalar_tensor_tensor(out=st[:, c % 2, 1:T], in0=kraw[:, 0:T - 1], scalar=sg[:, 0, c:c + 1],
                                                     in1=st[:, c % 2, 1:T], op0=ALU.mult, op1=ALU.add).then_inc(ph.s["k_ready"], 1)
                        for j in range(TB):
                            dve.wait_ge(ph.s["pe_done"], done + CH + 2 + 2 * j)
                            dve.tensor_tensor(v_all[:, ds(b * TB + j, 1), :], PV[:, None, :], brow[:, None, 0:E], ALU.add).then_inc(ph.s["v_ready"], 1)
                            dve.wait_ge(ph.s["pe_done"], done + CH + 3 + 2 * j)
                            dve.wait_ge(ph.s["gate_ready"], b * TB + j)
                            dve.tensor_tensor(vtmp[:], PG, brow[:, E:2 * E], ALU.add).then_inc(ph.s["gate_sum"], 1)

        attention(k, "l0a", causal_units(DH), H, DK, DH, qt, kt, v_all, o_all)
        project_out(k, "l0o", o_all, E, a["L0_attn_W_out"], x_in, x_out, xt_out, pre=(a["L0_attn_out_ln_w"], a["L0_attn_out_ln_b"]),
                    gate=gate)


class Job:

    def __init__(self, parts, kind, scale=1.0, bias=None, dsts=None, n_dst=0, dst=None, needs=0):
        self.parts, self.kind, self.scale, self.bias, self.dsts, self.n_dst, self.dst, self.needs = \
            parts, kind, scale, bias, dsts, n_dst, dst, needs


def column_parts(w, xs, c):
    return [(h * 512, 512, [(w[:, d, c * P:(c + 1) * P], xs[:, d, h * 512:(h + 1) * 512]) for d in range(w.shape[1])])
            for h in range(T // 512)]


def row_parts(w, xs, c0, F, j0):
    return [(i * F, F, [(xs[:, d, (j0 + i) * P:(j0 + i + 1) * P], w[:, d, c0:c0 + F]) for d in range(w.shape[1])])
            for i in range(1024 // F)]


def project_in(k, ph, xt, xs, jobs, loads, rope=None):
    nc = k.nc
    NJ = len(jobs)
    assert NJ % 2 == 0
    st = ph.sb("st", [P, 2, T])
    tmp = ph.sb("tmp", [P, 4, T]) if rope else None
    freed = [ph.sem("freed0"), ph.sem("freed1")]
    stored = [ph.sem("stored0"), ph.sem("stored1")]
    ph.sems_of("w_ld x_ld jobs_done staged kept rows_done mults rotated rstored")
    slot = [k.ps[:, 0:2, :].rearrange("p b c -> p (b c)"), k.ps[:, 2:4, :].rearrange("p b c -> p (b c)")]
    stores = [j for j in range(NJ) if jobs[j].kind == "store"]
    keeps = [j for j in range(NJ) if jobs[j].kind == "keep"]
    firsts = [j for j in range(NJ) if jobs[j].kind == "first"]
    rows = [j for j in range(NJ) if jobs[j].kind == "rows"]
    R = len(firsts)
    out_of = [[sum(jobs[i].n_dst for i in range(j) if i % 2 == s and jobs[i].kind == "store") for j in range(NJ + 1)] for s in range(2)]
    with nc.Block() as block:

        @block.sync
        def _(sp):
            for dst, src in loads:
                sp.dma_start(dst, src).then_inc(ph.s["w_ld"], 16)
            with sp.Fori(0, B) as b:
                sp.wait_ge(ph.s["jobs_done"], b * NJ)
                sp.dma_start(xs[:], xt[:, ds(b * T, T)].rearrange("(c p) t -> p c t", p=P)).then_inc(ph.s["x_ld"], 16)
                for n, j in enumerate(stores):
                    sp.wait_ge(ph.s["staged"], b * len(stores) + n + 1)
                    for r0, r1, dst in jobs[j].dsts(b):
                        sp.dma_start(dst, st[r0:r1, j % 2, :]).then_inc(stored[j % 2], 16)
                for n, j in enumerate(firsts):
                    sp.wait_ge(ph.s["rotated"], 2 * (b * R + n) + 2)
                    for half in range(2):
                        for r0, r1, dst in jobs[j + half].dsts(b):
                            sp.dma_start(dst, st[r0:r1, half, :]).then_inc(ph.s["rstored"], 16)
            for s in range(2):
                if out_of[s][NJ]:
                    sp.wait_ge(stored[s], 16 * B * out_of[s][NJ])
            if R:
                sp.wait_ge(ph.s["rstored"], 16 * B * R * 2 * jobs[firsts[0]].n_dst)

        @block.tensor
        def _(pe):
            pe.wait_ge(ph.s["w_ld"], 16 * len(loads))
            with pe.Fori(0, B) as b:
                pe.wait_ge(ph.s["x_ld"], 16 * b + 16)
                for j, job in enumerate(jobs):
                    pe.wait_ge(freed[j % 2], b * (NJ // 2) + j // 2)
                    if job.needs:
                        pe.wait_ge(ph.s["kept"], b * len(keeps) + job.needs)
                    for c0, w, terms in job.parts:
                        for n, (lhsT, rhs) in enumerate(terms):
                            ins = pe.matmul(slot[j % 2][:, c0:c0 + w], lhsT, rhs, start=n == 0, stop=n == len(terms) - 1)
                    ins.then_inc(ph.s["jobs_done"], 1)

        @block.scalar
        def _(act):
            act.wait_ge(ph.s["w_ld"], 16 * len(loads))
            with act.Fori(0, B) as b:
                for j, job in enumerate(jobs):
                    if job.kind in ("first", "second"):
                        continue
                    act.wait_ge(ph.s["jobs_done"], b * NJ + j + 1)
                    bias = 0.0 if job.bias is None else job.bias
                    if job.kind == "store":
                        act.wait_ge(stored[j % 2], 16 * (b * out_of[j % 2][NJ] + out_of[j % 2][j]))
                        act.activation(st[:, j % 2, :], slot[j % 2], ACT.Identity, scale=job.scale, bias=bias).then_inc(ph.s["staged"], 1)
                        act.wait_ge(ph.s["staged"], b * len(stores) + stores.index(j) + 1)
                    elif job.kind == "keep":
                        act.activation(job.dst, slot[j % 2], ACT.Identity, scale=job.scale, bias=bias).then_inc(ph.s["kept"], 1)
                        act.wait_ge(ph.s["kept"], b * len(keeps) + keeps.index(j) + 1)
                    else:
                        F = job.parts[0][1]
                        act.activation(job.dst(b), slot[j % 2].rearrange("p (t f) -> p t f", f=F), ACT.Copy).then_inc(ph.s["rows_done"], 1)
                        act.wait_ge(ph.s["rows_done"], b * len(rows) + rows.index(j) + 1)
                    act.sem_inc(freed[j % 2], 1)

        @block.vector
        def _(dve):
            if not R:
                return
            cos, sin = rope
            dve.wait_ge(ph.s["w_ld"], 16 * len(loads))
            with dve.Fori(0, B) as b:
                for n, j in enumerate(firsts):
                    for half, (f, o) in enumerate(((cos, sin), (sin, cos))):
                        dve.wait_ge(ph.s["jobs_done"], b * NJ + j + half + 1)
                        if half == 0:
                            dve.wait_ge(ph.s["rotated"], 2 * (b * R + n))
                        dve.tensor_tensor(tmp[:, 2 * half, :], slot[half], f[:], ALU.mult).then_inc(ph.s["mults"], 1)
                        dve.tensor_tensor(tmp[:, 2 * half + 1, :], slot[half], o[:], ALU.mult).then_inc(freed[half], 1)
                    dve.wait_ge(freed[1], b * (NJ // 2) + (j + 1) // 2 + 1)
                    dve.sem_inc(ph.s["mults"], 1)

        @block.gpsimd
        def _(pool):
            if not R:
                return
            with pool.Fori(0, B) as b:
                for n, j in enumerate(firsts):
                    pool.wait_ge(ph.s["mults"], 3 * (b * R + n) + 3)
                    pool.wait_ge(ph.s["rstored"], 16 * 2 * jobs[j].n_dst * (b * R + n))
                    pool.tensor_tensor(st[:, 0, :], tmp[:, 0, :], tmp[:, 2, :], ALU.subtract).then_inc(ph.s["rotated"], 1)
                    pool.tensor_tensor(st[:, 1, :], tmp[:, 1, :], tmp[:, 3, :], ALU.add).then_inc(ph.s["rotated"], 1)


def flat(dram):
    return dram.rearrange("h d n -> (h d) n")


def to_flat(dram, c):
    return lambda b: [(0, P, flat(dram)[c * P:(c + 1) * P, ds(b * T, T)])]


def l1_self_attention(k, x_in, x_out, xt_out):
    nc, a = k.nc, k.a
    H, KV, DH = 16, 4, 64
    HF = DH // 2
    FQ, FK = H * DH, KV * DH
    qt, kt = k.dram("l1_qt", [H, DH, N]), k.dram("l1_kt", [KV, DH, N])
    with ExitStack() as keep:
        v_all = keep.enter_context(nc.sbuf_tensor("l1_v_all", [P, NT, FK], F32))
        o_all = keep.enter_context(nc.sbuf_tensor("l1_o_all", [P, NT, FQ], F32))
        with Phase(k, "l1p") as ph:
            w = ph.sb("w", [P, DC, FQ + 2 * FK])
            cos, sin = ph.sb("cos", [P, T]), ph.sb("sin", [P, T])
            xs = ph.sb("xs", [P, DC, T])
            jobs = []

            def halves(dram, g, half):
                return lambda b: [(h * HF, (h + 1) * HF, dram[4 * g + h, half * HF:(half + 1) * HF, ds(b * T, T)]) for h in range(4)]

            for dram, n, c0 in ((qt, FQ // (2 * P), 0), (kt, FK // (2 * P), FQ // P)):
                for g in range(n):
                    for half, kind in enumerate(("first", "second")):
                        jobs.append(Job(column_parts(w, xs, c0 + 2 * g + half), kind, dsts=halves(dram, g, half), n_dst=4))
            for j in range(0, TB, 4):
                jobs.append(Job(row_parts(w, xs, FQ + FK, FK, j), "rows", dst=lambda b, j=j: v_all[:, ds(b * TB + j, 4), :]))
            project_in(k, ph, k.xt, xs, jobs,
                       [(w[:, :, 0:FQ], weight_rows(a["L1_attn_Wq"])), (w[:, :, FQ:FQ + FK], weight_rows(a["L1_attn_Wk"])),
                        (w[:, :, FQ + FK:], weight_rows(a["L1_attn_Wv"])), (cos[:], a["c_cos"]), (sin[:], a["c_sin"])], (cos, sin))
        attention(k, "l1a", causal_units(DH), H, DH, DH, qt, kt, v_all, o_all, kv_of=H // KV)
        project_out(k, "l1o", o_all, FQ, a["L1_attn_Wo"], x_in, x_out, xt_out)


def l2_self_attention(k, x_in, x_out, xt_out):
    nc, a = k.nc, k.a
    qt, kt = k.dram("l2_qt", [1, D, N]), k.dram("l2_kt", [1, D, N])
    with ExitStack() as keep:
        v_all = keep.enter_context(nc.sbuf_tensor("l2_v_all", [P, NT, D], F32))
        o_all = keep.enter_context(nc.sbuf_tensor("l2_o_all", [P, NT, D], F32))
        with Phase(k, "l2p") as ph:
            w = ph.sb("w", [P, DC, 3 * D])
            xs = ph.sb("xs", [P, DC, T])
            jobs = [Job(column_parts(w, xs, c), "store", scale=D ** -0.5 if c < DC else 1.0, dsts=to_flat((qt, kt)[c // DC], c % DC), n_dst=1)
                    for c in range(2 * DC)]
            jobs += [Job(row_parts(w, xs, 2 * D, D, j), "rows", dst=lambda b, j=j: v_all[:, ds(b * TB + j, 4), :]) for j in range(0, TB, 4)]
            project_in(k, ph, k.xt, xs, jobs, [(w[:, :, i * D:(i + 1) * D], weight_rows(a[f"L2_attn_{m}"])) for i, m in enumerate(("Wq", "Wk", "Wv"))])
        attention(k, "l2a", causal_units(D), 1, D, D, qt, kt, v_all, o_all)
        project_out(k, "l2o", o_all, D, a["L2_attn_Wo"], x_in, x_out, xt_out)


def l3_self_attention(k, x_in, x_out, xt_out):
    nc, a = k.nc, k.a
    H, DH = 16, 16
    qt, kt = k.dram("l3_qt", [H, DH, N]), k.dram("l3_kt", [H, DH, N])
    with ExitStack() as keep:
        v_all = keep.enter_context(nc.sbuf_tensor("l3_v_all", [P, NT, D], F32))
        o_all = keep.enter_context(nc.sbuf_tensor("l3_o_all", [P, NT, D], F32))
        k_eff = keep.enter_context(nc.sbuf_tensor("l3_k_eff", [P, 1, D], F32))
        v_eff = keep.enter_context(nc.sbuf_tensor("l3_v_eff", [P, 1, D], F32))
        with Phase(k, "l3e") as ph:
            ph.sems_of("w_ld prod copied")
            uq, uk, uv = (ph.sb(n, [P, DC, P]) for n in ("uq", "uk", "uv"))
            wo = ph.sb("wo", [P, DC, D])
            dq = ph.sb("dq", [P, D])
            inner = ph.sb("inner", [P, P])
            with nc.Block() as block:

                @block.sync
                def _(sp):
                    for dst, src in ((uq, "W_uq"), (uk, "W_uk"), (uv, "W_uv"), (wo, "W_o")):
                        sp.dma_start(dst[:], weight_rows(a[f"L3_attn_{src}"])).then_inc(ph.s["w_ld"], 16)
                    sp.dma_start(dq[:], a["L3_attn_W_dq"]).then_inc(ph.s["w_ld"], 16)

                @block.tensor
                def _(pe):
                    pe.wait_ge(ph.s["w_ld"], 80)
                    for c in range(DC):
                        ins = pe.matmul(k.ps[:, 0, 0:P], uq[:, c, :], uk[:, c, :], start=c == 0, stop=c == DC - 1)
                    ins.then_inc(ph.s["prod"], 1)
                    for c in range(DC):
                        ins = pe.matmul(k.ps[:, 1, 0:D], uv[:, c, :], wo[:, c, :], start=c == 0, stop=c == DC - 1)
                    ins.then_inc(ph.s["prod"], 1)
                    pe.wait_ge(ph.s["copied"], 1)
                    pe.matmul(k.ps[:, 2, 0:D], inner[:], dq[:], start=True, stop=True).then_inc(ph.s["prod"], 1)

                @block.scalar
                def _(act):
                    for n, (dst, src) in enumerate(((inner[:], k.ps[:, 0, 0:P]), (v_eff[:, 0, :], k.ps[:, 1, 0:D]), (k_eff[:, 0, :], k.ps[:, 2, 0:D]))):
                        act.wait_ge(ph.s["prod"], n + 1)
                        act.activation(dst, src, ACT.Copy).then_inc(ph.s["copied"], 1)
                    act.wait_ge(ph.s["copied"], 3)

        with Phase(k, "l3p") as ph:
            w = ph.sb("w", [P, DC, 2 * P])
            uq = ph.sb("uq", [P, 1, D])
            xs = ph.sb("xs", [P, DC, T])
            lat = ph.sb("lat", [P, 2, T])
            low, latent = lat[:, 0:1, :], lat[:, 1:2, :]
            jobs = [Job(column_parts(w, xs, c), "keep", dst=lat[:, c, :]) for c in range(2)]
            jobs += [Job(column_parts(uq, low, c), "store", scale=DH ** -0.5, dsts=to_flat(qt, c), n_dst=1, needs=2) for c in range(2)]
            jobs += [Job(column_parts(k_eff, latent, c), "store", dsts=to_flat(kt, c), n_dst=1, needs=2) for c in range(2)]
            jobs += [Job(row_parts(v_eff, latent, 0, D, j), "rows", dst=lambda b, j=j: v_all[:, ds(b * TB + j, 4), :], needs=2) for j in range(0, TB, 4)]
            project_in(k, ph, k.xt, xs, jobs, [(w[:, :, 0:P], weight_rows(a["L3_attn_W_dq_T"])), (w[:, :, P:], weight_rows(a["L3_attn_W_dkv"])),
                                               (uq[:, 0, :], a["L3_attn_W_uq_T"])])
        attention(k, "l3a", causal_units(DH), H, DH, DH, qt, kt, v_all, o_all)
        project_out(k, "l3o", o_all, D, None, x_in, x_out, xt_out)


def context(k, name, kt, v_all, F, wk, wv, bk=None, bv=None, norm=None):
    nc, a = k.nc, k.a
    FC = F // P
    CR = CTX - P
    NM = B * M
    W = min(F, 512)
    with Phase(k, name) as ph:
        ca, cb = ph.sb("ca", [P, NM]), ph.sb("cb", [CR, NM])
        wka, wkb = ph.sb("wka", [P, F]), ph.sb("wkb", [CR, F])
        wva, wvb = ph.sb("wva", [P, F]), ph.sb("wvb", [CR, F])
        bkc = ph.sb("bkc", [P, FC]) if bk is not None else None
        bvr = ph.sb("bvr", [M, F]) if bv is not None else None
        st = ph.sb("st", [P, FC, NM])
        loads = [(wka[:], wk[0:P, :]), (wkb[:], wk[P:CTX, :]), (wva[:], wv[0:P, :]), (wvb[:], wv[P:CTX, :])]
        if bk is not None:
            loads += [(bkc[:], bk), (bvr[:], bv)]
        if norm is None:
            loads += [(ca[:], a["ctx_T"][0:P, :]), (cb[:], a["ctx_T"][P:CTX, :])]
        else:
            rows = ph.sb("rows", [M, B, CTX])
            stats, mv = ph.sb("stats", [M, B, 6]), ph.sb("mv", [M, B, 2])
            ve, sd, rs = ph.sb("ve", [M, B]), ph.sb("sd", [M, B]), ph.sb("rs", [M, B])
            na, nb = ph.sb("na", [P, 2]), ph.sb("nb", [CR, 2])
            gap = ph.sb("gap", [M, 1])
            loads += [(rows[:], a["ctx_rows"]), (na[:], norm[0:P, :]), (nb[:], norm[P:CTX, :])]
        ph.sems_of("ld chain sd_ready turned cols prods k_moved v_moved k_st")
        bank = [k.ps[:, 0, :], k.ps[:, 1, :]]
        n_v = B * (F // W)
        with nc.Block() as block:

            @block.sync
            def _(sp):
                for dst, src in loads:
                    sp.dma_start(dst, src).then_inc(ph.s["ld"], 16)
                sp.wait_ge(ph.s["k_moved"], FC)
                sp.dma_start(flat(kt).rearrange("(c p) n -> p c n", p=P), st[:]).then_inc(ph.s["k_st"], 16)
                sp.wait_ge(ph.s["k_st"], 16)

            @block.tensor
            def _(pe):
                pe.wait_ge(ph.s["ld"], 16 * len(loads))
                if norm is not None:
                    pe.wait_ge(ph.s["chain"], 2 * B + 3)
                    for b in range(B):
                        pe.transpose(k.ps[:, 2, b * P:b * P + M], rows[:, b, 0:P], k.ident[0:M, 0:M])
                        ins = pe.transpose(k.ps[0:CR, 3, b * P:b * P + M], rows[:, b, P:CTX], k.ident[0:M, 0:M])
                    ins.then_inc(ph.s["turned"], 1)
                    pe.wait_ge(ph.s["cols"], 2 * B)
                n = 0
                for c in range(FC):
                    if n >= 2:
                        pe.wait_ge(ph.s["k_moved"], n - 1)
                    pe.matmul(bank[n % 2][:, 0:NM], wka[:, c * P:(c + 1) * P], ca[:], start=True, stop=False)
                    pe.matmul(bank[n % 2][:, 0:NM], wkb[:, c * P:(c + 1) * P], cb[:], start=False, stop=True).then_inc(ph.s["prods"], 1)
                    n += 1
                pe.wait_ge(ph.s["k_moved"], FC)
                for i in range(n_v):
                    b, f = i // (F // W), i % (F // W)
                    if i >= 2:
                        pe.wait_ge(ph.s["v_moved"], i - 1)
                    o = bank[n % 2][0:M, 0:W]
                    pe.matmul(o, ca[:, b * M:(b + 1) * M], wva[:, f * W:(f + 1) * W], start=True, stop=False)
                    pe.matmul(o, cb[:, b * M:(b + 1) * M], wvb[:, f * W:(f + 1) * W], start=False, stop=True).then_inc(ph.s["prods"], 1)
                    n += 1

            @block.scalar
            def _(act):
                act.wait_ge(ph.s["ld"], 16 * len(loads))
                if norm is not None:
                    act.wait_ge(ph.s["chain"], 2 * B + 1)
                    act.activation(sd[:], ve[:], ACT.Sqrt).then_inc(ph.s["sd_ready"], 1)
                    act.wait_ge(ph.s["turned"], 1)
                    for b in range(B):
                        act.activation(ca[:, b * M:(b + 1) * M], k.ps[:, 2, b * P:b * P + M], ACT.Identity, scale=na[:, 0:1], bias=na[:, 1:2]).then_inc(ph.s["cols"], 1)
                        act.activation(cb[:, b * M:(b + 1) * M], k.ps[0:CR, 3, b * P:b * P + M], ACT.Identity, scale=nb[:, 0:1], bias=nb[:, 1:2]).then_inc(ph.s["cols"], 1)
                for c in range(FC):
                    act.wait_ge(ph.s["prods"], c + 1)
                    act.activation(st[:, c, :], bank[c % 2][:, 0:NM], ACT.Identity, bias=0.0 if bk is None else bkc[:, c:c + 1]).then_inc(ph.s["k_moved"], 1)

            @block.vector
            def _(dve):
                dve.wait_ge(ph.s["ld"], 16 * len(loads))
                if norm is not None:
                    for b in range(B):
                        dve.bn_stats(stats[:, b, :], rows[:, b, :]).then_inc(ph.s["chain"], 1)
                    dve.wait_ge(ph.s["chain"], B)
                    dve.memset(gap[:], 0.0)
                    for b in range(B):
                        dve.bn_aggr(mv[:, b, :], stats[:, b, :]).then_inc(ph.s["chain"], 1)
                    dve.wait_ge(ph.s["chain"], 2 * B)
                    dve.tensor_scalar(ve[:], mv[:, :, 1], EPS, None, ALU.add).then_inc(ph.s["chain"], 1)
                    dve.wait_ge(ph.s["sd_ready"], 1)
                    dve.reciprocal(rs[:], sd[:]).then_inc(ph.s["chain"], 1)
                    dve.wait_ge(ph.s["chain"], 2 * B + 2)
                    for b in range(B):
                        ins = dve.tensor_scalar(rows[:, b, :], rows[:, b, :], mv[:, b, 0:1], rs[:, b:b + 1], ALU.subtract, ALU.mult)
                    ins.then_inc(ph.s["chain"], 1)
                for i in range(n_v):
                    b, f = i // (F // W), i % (F // W)
                    dve.wait_ge(ph.s["prods"], FC + i + 1)
                    src = bank[(FC + i) % 2][0:M, 0:W]
                    if bv is None:
                        ins = dve.tensor_copy(v_all[:, b, f * W:(f + 1) * W], src)
                    else:
                        ins = dve.tensor_tensor(v_all[:, b, f * W:(f + 1) * W], src, bvr[:, f * W:(f + 1) * W], ALU.add)
                    ins.then_inc(ph.s["v_moved"], 1)


def cross_attention(k, name, H, DH, x_in, x_out, xt_out, xq, wq, wk, wv, wo, scale, bq=None, bk=None, bv=None, bo=None,
                    norm=None, shared_keys=False):
    nc = k.nc
    F = H * DH
    FC = F // P
    qt, kt = k.dram(f"{name}_qt", [H, DH, N]), k.dram(f"{name}_kt", [H, DH, B * M])
    with ExitStack() as keep:
        v_all = keep.enter_context(nc.sbuf_tensor(f"{name}_v_all", [M, B, F], F32))
        o_all = keep.enter_context(nc.sbuf_tensor(f"{name}_o_all", [P, NT, F], F32))
        context(k, f"{name}c", kt, v_all, F, wk, wv, bk, bv, norm)
        with Phase(k, f"{name}p") as ph:
            w = ph.sb("w", [P, DC, F])
            xs = ph.sb("xs", [P, DC, T])
            loads = [(w[:], weight_rows(wq))]
            if bq is not None:
                b_q, b_s = ph.sb("b_q", [P, FC]), ph.sb("b_s", [P, FC])
                ph.sems_of("b_ld b_scaled")
                with nc.Block() as block:

                    @block.sync
                    def _(sp):
                        sp.dma_start(b_q[:], bq).then_inc(ph.s["b_ld"], 16)

                    @block.vector
                    def _(dve):
                        dve.wait_ge(ph.s["b_ld"], 16)
                        dve.tensor_scalar(b_s[:], b_q[:], scale, None, ALU.mult).then_inc(ph.s["b_scaled"], 1)
                        dve.wait_ge(ph.s["b_scaled"], 1)

            jobs = [Job(column_parts(w, xs, c), "store", scale=scale, bias=None if bq is None else b_s[:, c:c + 1], dsts=to_flat(qt, c), n_dst=1)
                    for c in range(FC)]
            project_in(k, ph, xq, xs, jobs, loads)
        attention(k, f"{name}a", cross_units(DH, M, B if shared_keys else 1), H, DH, DH, qt, kt, v_all, o_all, n_keys=B * M, key_rows=M)
        project_out(k, f"{name}o", o_all, F, wo, x_in, x_out, xt_out, bias=bo)


def l0_cross_attention(k, x_in, x_out, xt_out):
    a = k.a
    H, DH = 8, 128
    cross_attention(k, "x0", H, DH, x_in, x_out, xt_out, k.xt, a["L0_xattn_Wq"], a["L0_xattn_Wk"], a["L0_xattn_Wv"], a["L0_xattn_Wout"],
                    1.5 * DH ** -0.5, bo=a["L0_xattn_bout"], shared_keys=True)


def l1_cross_attention(k, x_in, x_out, xt_out):
    a = k.a
    cross_attention(k, "x1", 16, 16, x_in, x_out, xt_out, k.xt, a["L1_xattn_Wq"], a["L1_xattn_Wk"], a["L1_xattn_Wv"], a["L1_xattn_Wo"],
                    16 ** -0.5, bq=a["L1_xattn_bq"], bk=a["L1_xattn_bk"], bv=a["L1_xattn_bv"], bo=a["L1_xattn_bo"])


def l2_cross_attention(k, x_in, x_out, xt_out):
    a = k.a
    cross_attention(k, "x2", 4, 64, x_in, x_out, xt_out, k.xt, a["L2_xattn_Wq"], a["L2_xattn_Wk"], a["L2_xattn_Wv"], a["L2_xattn_Wo"],
                    64 ** -0.5, bo=a["L2_xattn_bo"])


def l3_cross_attention(k, x_in, x_out, xt_out):
    a = k.a
    norm_columns(k, "x3n", x_in, k.xnt, a["L3_xattn_g_x"], a["L3_xattn_b_x"])
    cross_attention(k, "x3", 16, 64, x_in, x_out, xt_out, k.xnt, a["L3_xattn_Wq"], a["L3_xattn_Wk"], a["L3_xattn_Wv"], a["L3_xattn_Wo"],
                    64 ** -0.5, norm=a["L3_xattn_norm_c"])


def top_mask(dve, ph, ch, sel, m8, K, E, tmp, mask):
    gt, eq, rank, need, reset = tmp
    for t in range(NT):
        ch.step(dve.max(m8[:, t, :], sel[:, t, :]))
    ch.wait()
    least = m8[:, :, K - 1:K].to_broadcast([P, NT, E])
    ch.step(dve.tensor_tensor(gt[:], sel[:], least, ALU.is_gt))
    ch.step(dve.tensor_tensor(eq[:], sel[:], least, ALU.is_equal))
    ch.wait()
    ch.step(dve.tensor_reduce(need[:], gt[:], AX.X, ALU.add))
    ch.step(dve.tensor_tensor_scan(rank[:].rearrange("p t e -> p (t e)"), reset[:].rearrange("p t e -> p (t e)"),
                                   eq[:].rearrange("p t e -> p (t e)"), 0.0, ALU.mult, ALU.add))
    ch.wait()
    ch.step(dve.tensor_scalar(need[:], need[:], -1.0, float(K), ALU.mult, ALU.add))
    ch.wait()
    ch.step(dve.tensor_tensor(rank[:], rank[:], need[:, :, None].to_broadcast([P, NT, E]), ALU.is_le))
    ch.wait()
    ch.step(dve.tensor_tensor(eq[:], eq[:], rank[:], ALU.mult))
    ch.wait()
    ch.step(dve.tensor_tensor(mask[:], gt[:], eq[:], ALU.add))
    ch.wait()


def top_mask_buffers(ph, E):
    return [ph.sb("gt", [P, NT, E]), ph.sb("eq", [P, NT, E]), ph.sb("rank", [P, NT, E]), ph.sb("need", [P, NT]), ph.sb("reset", [P, NT, E])]


def l0_gates(k, gates):
    nc, a = k.nc, k.a
    E, K = 32, 4
    CAP = 2 * (N // 2) * K // E
    with Phase(k, "g0") as ph:
        xt_all = ph.sb("xt", [P, DC, N])
        wgb, wg = ph.sb("wgb", [P, DC, E], BF16), ph.sb("wg", [P, DC, E])
        bias = ph.sb("bias", [P, E])
        before = ph.sb("before", [P, P])
        ones = ph.sb("ones", [P, P])
        sc, sel, mask = ph.sb("sc", [P, NT, E]), ph.sb("sel", [P, NT, E]), ph.sb("mask", [P, NT, E])
        by_expert, resets, upto = ph.sb("by_expert", [P, E, NT]), ph.sb("resets", [P, E, NT]), ph.sb("upto", [P, E, NT])
        earlier = ph.sb("earlier", [P, NT, E])
        m8 = ph.sb("m8", [P, NT, 8])
        total, inv = ph.sb("total", [P, NT]), ph.sb("inv", [P, NT])
        tmp = top_mask_buffers(ph, E)
        ph.sems_of("ld conv logits_done sc_ready chain mask_ready pos_done")
        logits = k.ps[:, 0, :].rearrange("p (t e) -> p t e", e=E)
        place = k.ps[:, 1, :].rearrange("p (t e) -> p t e", e=E)
        with nc.Block() as block:

            @block.sync
            def _(sp):
                sp.dma_start(wgb[:], weight_rows(a["L0_ffn_gate_w"])).then_inc(ph.s["ld"], 16)
                sp.dma_start(bias[:], a["L0_ffn_bias"]).then_inc(ph.s["ld"], 16)
                sp.dma_start(before[:], a["c_before"]).then_inc(ph.s["ld"], 16)
                sp.dma_start(xt_all[:], weight_rows(k.xt)).then_inc(ph.s["ld"], 16)

            @block.gpsimd
            def _(pool):
                pool.memset(ones[:], 1.0).then_inc(ph.s["conv"], 1)
                pool.memset(tmp[4][:], 1.0).then_inc(ph.s["conv"], 1)
                pool.memset(resets[:], 1.0).then_inc(ph.s["conv"], 1)
                pool.wait_ge(ph.s["conv"], 3)
                pool.memset(tmp[4][:, :, 0:1], 0.0).then_inc(ph.s["conv"], 1)
                pool.memset(resets[:, :, 0:1], 0.0).then_inc(ph.s["conv"], 1)
                pool.wait_ge(ph.s["ld"], 64)
                pool.tensor_copy(wg[:], wgb[:]).then_inc(ph.s["conv"], 1)

            @block.tensor
            def _(pe):
                pe.wait_ge(ph.s["conv"], 6)
                for t in range(NT):
                    for d in range(DC):
                        ins = pe.matmul(logits[:, t, :], xt_all[:, d, t * P:(t + 1) * P], wg[:, d, :], start=d == 0, stop=d == DC - 1)
                ins.then_inc(ph.s["logits_done"], 1)
                pe.wait_ge(ph.s["mask_ready"], 1)
                for t in range(NT):
                    pe.matmul(place[:, t, :], before[:], mask[:, t, :], start=True, stop=False)
                    ins = pe.matmul(place[:, t, :], ones[:], earlier[:, t, :], start=False, stop=True)
                ins.then_inc(ph.s["pos_done"], 1)

            @block.scalar
            def _(act):
                act.wait_ge(ph.s["logits_done"], 1)
                act.activation(sc[:], logits, ACT.Sigmoid).then_inc(ph.s["sc_ready"], 1)

            @block.vector
            def _(dve):
                ch = Count(dve, ph.s["chain"], 0, 0)
                dve.wait_ge(ph.s["conv"], 6)
                dve.wait_ge(ph.s["sc_ready"], 1)
                ch.step(dve.tensor_tensor(sel[:], sc[:], bias[:, None, :].to_broadcast([P, NT, E]), ALU.add))
                ch.wait()
                top_mask(dve, ph, ch, sel, m8, K, E, tmp, mask)
                ch.step(dve.tensor_copy(by_expert[:], mask[:].rearrange("p t e -> p e t")))
                ch.step(dve.tensor_tensor(sel[:], sc[:], mask[:], ALU.mult))
                ch.wait()
                ch.step(dve.tensor_tensor_scan(upto[:].rearrange("p e t -> p (e t)"), resets[:].rearrange("p e t -> p (e t)"),
                                               by_expert[:].rearrange("p e t -> p (e t)"), 0.0, ALU.mult, ALU.add))
                ch.wait()
                dve.tensor_tensor(earlier[:], upto[:].rearrange("p e t -> p t e"), mask[:], ALU.subtract).then_inc(ph.s["mask_ready"], 1)
                ch.step(dve.tensor_reduce(total[:], sel[:], AX.X, ALU.add))
                ch.wait()
                ch.step(dve.tensor_scalar(total[:], total[:], 1e-12, None, ALU.max))
                ch.wait()
                ch.step(dve.reciprocal(inv[:], total[:]))
                ch.wait()
                ch.step(dve.tensor_tensor(sel[:], sel[:], inv[:, :, None].to_broadcast([P, NT, E]), ALU.mult))
                dve.wait_ge(ph.s["pos_done"], 1)
                ch.wait()
                ch.step(dve.scalar_tensor_tensor(out=gates[:, :, 0:E], in0=place, scalar=float(CAP), in1=sel[:], op0=ALU.is_lt, op1=ALU.mult))
                ch.step(dve.memset(gates[:, :, E:E + 1], 1.0))
                ch.wait()


def l1_gates(k, gates):
    nc, a = k.nc, k.a
    E, K = 8, 2
    with Phase(k, "g1") as ph:
        xt_all = ph.sb("xt", [P, DC, N])
        wg = ph.sb("wg", [P, DC, E])
        lg, m8 = ph.sb("lg", [P, NT, E]), ph.sb("m8", [P, NT, 8])
        gap, ex, den = ph.sb("gap", [P, NT]), ph.sb("ex", [P, NT]), ph.sb("den", [P, NT])
        inv, r = ph.sb("inv", [P, NT]), ph.sb("r", [P, 2, NT])
        m1, m2 = ph.sb("m1", [P, NT, E]), ph.sb("m2", [P, NT, E])
        tmp = top_mask_buffers(ph, E)
        ph.sems_of("ld conv logits_done chain gap_ready ex_ready")
        logits = k.ps[:, 0, 0:NT * E].rearrange("p (t e) -> p t e", e=E)
        with nc.Block() as block:

            @block.sync
            def _(sp):
                sp.dma_start(wg[:], weight_rows(a["L1_ffn_Wr"])).then_inc(ph.s["ld"], 16)
                sp.dma_start(xt_all[:], weight_rows(k.xt)).then_inc(ph.s["ld"], 16)

            @block.gpsimd
            def _(pool):
                pool.memset(tmp[4][:], 1.0).then_inc(ph.s["conv"], 1)
                pool.wait_ge(ph.s["conv"], 1)
                pool.memset(tmp[4][:, :, 0:1], 0.0).then_inc(ph.s["conv"], 1)

            @block.tensor
            def _(pe):
                pe.wait_ge(ph.s["ld"], 32)
                for t in range(NT):
                    for d in range(DC):
                        ins = pe.matmul(logits[:, t, :], xt_all[:, d, t * P:(t + 1) * P], wg[:, d, :], start=d == 0, stop=d == DC - 1)
                ins.then_inc(ph.s["logits_done"], 1)

            @block.scalar
            def _(act):
                act.wait_ge(ph.s["gap_ready"], 1)
                act.activation(ex[:], gap[:], ACT.Exp).then_inc(ph.s["ex_ready"], 1)

            @block.vector
            def _(dve):
                ch = Count(dve, ph.s["chain"], 0, 0)
                dve.wait_ge(ph.s["conv"], 2)
                dve.wait_ge(ph.s["logits_done"], 1)
                ch.step(dve.tensor_copy(lg[:], logits))
                ch.wait()
                top_mask(dve, ph, ch, lg, m8, 2, E, tmp, m2)
                dve.tensor_tensor(gap[:], m8[:, :, 1], m8[:, :, 0], ALU.subtract).then_inc(ph.s["gap_ready"], 1)
                dve.wait_ge(ph.s["gap_ready"], 1)
                top_mask(dve, ph, ch, lg, m8, 1, E, tmp, m1)
                ch.step(dve.tensor_tensor(m2[:], m2[:], m1[:], ALU.subtract))
                dve.wait_ge(ph.s["ex_ready"], 1)
                ch.step(dve.tensor_scalar(den[:], ex[:], 1.0, None, ALU.add))
                ch.wait()
                ch.step(dve.reciprocal(inv[:], den[:]))
                ch.wait()
                ch.step(dve.tensor_scalar(r[:, 0, :], inv[:], 1.0, None, ALU.is_ge))
                ch.step(dve.tensor_tensor(r[:, 1, :], ex[:], inv[:], ALU.mult))
                ch.wait()
                ch.step(dve.tensor_scalar(den[:], r[:, 1, :], 1.0, None, ALU.is_ge))
                ch.wait()
                ch.step(dve.tensor_tensor(m1[:], m1[:], r[:, 0, :, None].to_broadcast([P, NT, E]), ALU.mult))
                ch.step(dve.tensor_tensor(m2[:], m2[:], den[:, :, None].to_broadcast([P, NT, E]), ALU.mult))
                ch.wait()
                ch.step(dve.tensor_tensor(gates[:, :, 0:E], m1[:], m2[:], ALU.add))
                ch.step(dve.memset(gates[:, :, E:E + 1], 1.0))
                ch.wait()


def experts(k, name, E, acc, gates, w1, w2, w3=None, half=False):
    nc = k.nc
    I = P
    gated = w3 is not None
    mats = [m for m in (w1, w3) if m is not None]
    NM = len(mats)
    with Phase(k, name) as ph:
        xt_all = ph.sb("xt", [P, DC, N])
        wf = ph.sb("wf", [P, 2, NM + 1, 2 * P])
        wh = ph.sb("wh", [P, 2, NM + 1, 2 * P], BF16) if half else None
        sl = ph.sb("sl", [P, 2, GN])
        hid = ph.sb("hid", [P, 2, GN])
        ph.sems_of("x_ld h_done sl_ready hid_ready y_done added cleared wide passed")
        w_ld = [ph.sem("w_ld0"), ph.sem("w_ld1")]
        H1 = [k.ps[:, 0, :], k.ps[:, 1, :]]
        H3 = [k.ps[:, 2, :], k.ps[:, 3, :]]
        Y = [k.ps[:, 4 + 2 * s:6 + 2 * s, :].rearrange("p b (t d) -> p (b t) d", d=D) for s in range(2)]
        first = wh if half else wf

        def turns(eng):
            with eng.Fori(0, E // 2) as t:
                yield t * 2, 2
            yield E, 1

        def w_ready(eng, e, s):
            if half:
                eng.wait_ge(ph.s["wide"], e + s + 2)
            else:
                eng.wait_ge(w_ld[s], e * (8 * (NM + 1)) + 16 * (NM + 1))

        with nc.Block() as block:

            @block.sync
            def _(sp):
                sp.dma_start(xt_all[:], weight_rows(k.xt)).then_inc(ph.s["x_ld"], 16)
                for e, n in turns(sp):
                    for s in range(n):
                        if half:
                            sp.wait_ge(ph.s["wide"], e + s)
                        else:
                            sp.wait_ge(ph.s["y_done"], NG * (e + s + 1))
                        for m in range(NM):
                            sp.dma_start(first[:, s, m, :].rearrange("p (c i) -> p c i", c=DC),
                                         mats[m][ds(e + s, 1), :, :].rearrange("o (c p) i -> p (o c) i", p=P)).then_inc(w_ld[s], 16)
                        sp.dma_start(first[:, s, NM, :], w2[ds(e + s, 1), :, :].rearrange("o i d -> i (o d)")).then_inc(w_ld[s], 16)

            @block.gpsimd
            def _(pool):
                pool.memset(acc[:], 0.0).then_inc(ph.s["cleared"], 1)
                if not half:
                    return
                pool.sem_inc(ph.s["wide"], 1)
                for e, n in turns(pool):
                    for s in range(n):
                        pool.wait_ge(w_ld[s], e * (8 * (NM + 1)) + 16 * (NM + 1))
                        pool.wait_ge(ph.s["y_done"], NG * (e + s + 1))
                        pool.sem_inc(ph.s["passed"], 1)
                        pool.tensor_copy(wf[:, s, :, :], wh[:, s, :, :]).then_inc(ph.s["wide"], 1)

            @block.tensor
            def _(pe):
                pe.sem_inc(ph.s["y_done"], 2 * NG)
                pe.wait_ge(ph.s["x_ld"], 16)
                for e, n in turns(pe):
                    W = NG * n

                    def hidden(i):
                        s, g = i // NG, i % NG
                        if g == 0:
                            w_ready(pe, e, s)
                        pe.wait_ge(ph.s["hid_ready"], NG * e + i + 1)
                        for m, bank in zip(range(NM), (H1, H3)):
                            for d in range(DC):
                                ins = pe.matmul(bank[i % 2], wf[:, s, m, d * I:(d + 1) * I], xt_all[:, d, g * GN:(g + 1) * GN], start=d == 0, stop=d == DC - 1)
                        ins.then_inc(ph.s["h_done"], 1)

                    def outputs(i):
                        s, g = i // NG, i % NG
                        pe.wait_ge(ph.s["hid_ready"], NG * e + i + 3)
                        pe.wait_ge(ph.s["added"], NG * e + i + 1)
                        for j in range(GT):
                            ins = pe.matmul(Y[i % 2][:, j, :], hid[:, i % 2, j * P:(j + 1) * P], wf[:, s, NM, :], start=True, stop=True)
                        ins.then_inc(ph.s["y_done"], 1)

                    hidden(0)
                    for i in range(W):
                        if i + 1 < W:
                            hidden(i + 1)
                        outputs(i)

            @block.scalar
            def _(act):
                if not gated:
                    return
                for e, n in turns(act):
                    for i in range(NG * n):
                        act.wait_ge(ph.s["h_done"], NG * e + i + 1)
                        act.wait_ge(ph.s["hid_ready"], NG * e + i + 1)
                        act.activation(sl[:, i % 2, :], H1[i % 2], ACT.Silu).then_inc(ph.s["sl_ready"], 1)

            @block.vector
            def _(dve):
                dve.sem_inc(ph.s["hid_ready"], 2)
                dve.sem_inc(ph.s["added"], 2)
                dve.wait_ge(ph.s["cleared"], 1)
                for e, n in turns(dve):
                    W = NG * n

                    def hidden(i):
                        dve.wait_ge(ph.s["y_done"], NG * e + i - 1 + 2 * NG if i else NG * e + 2 * NG)
                        if gated:
                            dve.wait_ge(ph.s["sl_ready"], NG * e + i + 1)
                            ins = dve.tensor_tensor(hid[:, i % 2, :], sl[:, i % 2, :], H3[i % 2], ALU.mult)
                        else:
                            dve.wait_ge(ph.s["h_done"], NG * e + i + 1)
                            dve.tensor_scalar(sl[:, i % 2, :], H1[i % 2], 0.0, None, ALU.max).then_inc(ph.s["sl_ready"], 1)
                            dve.wait_ge(ph.s["sl_ready"], NG * e + i + 1)
                            ins = dve.tensor_tensor(hid[:, i % 2, :], sl[:, i % 2, :], sl[:, i % 2, :], ALU.mult)
                        ins.then_inc(ph.s["hid_ready"], 1)

                    def add(i):
                        s, g = i // NG, i % NG
                        dve.wait_ge(ph.s["y_done"], NG * e + i + 1 + 2 * NG)
                        dve.wait_ge(ph.s["added"], NG * e + max(i + 2 - 1, 0))
                        for j in range(GT):
                            t = g * GT + j
                            ins = dve.scalar_tensor_tensor(out=acc[:, t, :], in0=Y[i % 2][:, j, :], scalar=gates[:, t, ds(e + s, 1)],
                                                           in1=acc[:, t, :], op0=ALU.mult, op1=ALU.add)
                        ins.then_inc(ph.s["added"], 1)

                    hidden(0)
                    for i in range(W):
                        if i + 1 < W:
                            hidden(i + 1)
                        add(i)


def l0_feed_forward(k, x_in, x_out, xt_out):
    nc, a = k.nc, k.a
    with ExitStack() as keep:
        acc = keep.enter_context(nc.sbuf_tensor("f0_acc", [P, NT, D], F32))
        gates = keep.enter_context(nc.sbuf_tensor("f0_gates", [P, NT, 33], F32))
        l0_gates(k, gates)
        experts(k, "f0", 32, acc, gates, a["L0_ffn_W1"], a["L0_ffn_W2"], a["L0_ffn_W3"], half=True)
        project_out(k, "f0o", acc, D, None, x_in, x_out, xt_out)


def l1_feed_forward(k, x_in, x_out, xt_out):
    nc, a = k.nc, k.a
    with ExitStack() as keep:
        acc = keep.enter_context(nc.sbuf_tensor("f1_acc", [P, NT, D], F32))
        gates = keep.enter_context(nc.sbuf_tensor("f1_gates", [P, NT, 9], F32))
        l1_gates(k, gates)
        experts(k, "f1", 8, acc, gates, a["L1_ffn_W1"], a["L1_ffn_W2"])
        project_out(k, "f1o", acc, D, None, x_in, x_out, xt_out)


def l2_weights(k, wts):
    nc, a = k.nc, k.a
    E = 32
    with Phase(k, "g2") as ph:
        xt_all = ph.sb("xt", [P, DC, N])
        xr = ph.sb("xr", [P, NT, D])
        pt = ph.sb("pt", [P, DC, E])
        pt2 = ph.sb("pt2", [P, DC, E])
        ones = ph.sb("ones", [P, P])
        temp = ph.sb("temp", [P, 2])
        p2 = ph.sb("p2", [P, E])
        x2 = ph.sb("x2", [P, NT])
        d2, w = ph.sb("d2", [P, NT, E]), ph.sb("w", [P, NT, E])
        mask = ph.sb("mask", [P, NT, E])
        m8 = ph.sb("m8", [P, NT, 8])
        least, total, inv = ph.sb("least", [P, NT]), ph.sb("total", [P, NT]), ph.sb("inv", [P, NT])
        tmp = top_mask_buffers(ph, E)
        ph.sems_of("ld xr_ld conv pt2_ready prods chain d_ready sq_ready z_ready e_ready x2_done")
        xp = k.ps[:, 0, :].rearrange("p (t e) -> p t e", e=E)
        pp = k.ps[:, 1, 0:E]
        with nc.Block() as block:

            @block.sync
            def _(sp):
                sp.dma_start(pt[:], weight_rows(a["L2_ffn_prototypes"])).then_inc(ph.s["ld"], 16)
                sp.dma_start(temp[:, 0:1], a["L2_ffn_temp"]).then_inc(ph.s["ld"], 16)
                sp.dma_start(xt_all[:], weight_rows(k.xt)).then_inc(ph.s["ld"], 16)
                sp.dma_start(xr[:], k.x_now.rearrange("(t p) d -> p t d", p=P)).then_inc(ph.s["xr_ld"], 16)

            @block.gpsimd
            def _(pool):
                pool.memset(ones[:], 1.0).then_inc(ph.s["conv"], 1)
                pool.memset(tmp[4][:], 1.0).then_inc(ph.s["conv"], 1)
                pool.wait_ge(ph.s["conv"], 2)
                pool.memset(tmp[4][:, :, 0:1], 0.0).then_inc(ph.s["conv"], 1)

            @block.tensor
            def _(pe):
                pe.wait_ge(ph.s["ld"], 48)
                pe.wait_ge(ph.s["conv"], 3)
                for t in range(NT):
                    for d in range(DC):
                        pe.matmul(xp[:, t, :], xt_all[:, d, t * P:(t + 1) * P], pt[:, d, :], start=d == 0, stop=d == DC - 1)
                pe.wait_ge(ph.s["pt2_ready"], 1)
                for d in range(DC):
                    ins = pe.matmul(pp, ones[:], pt2[:, d, :], start=d == 0, stop=d == DC - 1)
                ins.then_inc(ph.s["prods"], 1)

            @block.scalar
            def _(act):
                act.wait_ge(ph.s["xr_ld"], 16)
                for t in range(NT):
                    ins = act.activation(xr[:, t, :], xr[:, t, :], ACT.Square, accum_out=x2[:, t:t + 1])
                ins.then_inc(ph.s["x2_done"], 1)
                act.wait_ge(ph.s["d_ready"], 1)
                act.activation(d2[:], d2[:], ACT.Sqrt).then_inc(ph.s["sq_ready"], 1)
                act.wait_ge(ph.s["z_ready"], 1)
                act.activation(w[:], d2[:], ACT.Exp).then_inc(ph.s["e_ready"], 1)

            @block.vector
            def _(dve):
                ch = Count(dve, ph.s["chain"], 0, 0)

                def wide(v):
                    return v[:, :, None].to_broadcast([P, NT, E])

                dve.wait_ge(ph.s["ld"], 48)
                dve.tensor_tensor(pt2[:], pt[:], pt[:], ALU.mult).then_inc(ph.s["pt2_ready"], 1)
                ch.step(dve.tensor_scalar(temp[:, 1:2], temp[:, 0:1], -1.0, None, ALU.mult))
                ch.wait()
                ch.step(dve.tensor_tensor(temp[:, 0:1], temp[:, 0:1], temp[:, 1:2], ALU.max))
                ch.wait()
                ch.step(dve.tensor_scalar(temp[:, 0:1], temp[:, 0:1], 0.1, -1.0, ALU.max, ALU.mult))
                ch.wait()
                ch.step(dve.reciprocal(temp[:, 1:2], temp[:, 0:1]))
                dve.wait_ge(ph.s["prods"], 1)
                ch.step(dve.tensor_copy(p2[:], pp))
                ch.wait()
                ch.step(dve.scalar_tensor_tensor(out=d2[:], in0=xp, scalar=-2.0, in1=p2[:, None, :].to_broadcast([P, NT, E]), op0=ALU.mult, op1=ALU.add))
                ch.wait()
                dve.wait_ge(ph.s["x2_done"], 1)
                ch.step(dve.tensor_tensor(d2[:], d2[:], wide(x2), ALU.add))
                ch.wait()
                dve.tensor_scalar(d2[:], d2[:], 0.0, None, ALU.max).then_inc(ph.s["d_ready"], 1)
                dve.wait_ge(ph.s["sq_ready"], 1)
                ch.step(dve.tensor_scalar(d2[:], d2[:], temp[:, 1:2], None, ALU.mult))
                ch.wait()
                ch.step(dve.tensor_reduce(least[:], d2[:], AX.X, ALU.max))
                ch.wait()
                dve.tensor_tensor(d2[:], d2[:], wide(least), ALU.subtract).then_inc(ph.s["z_ready"], 1)
                dve.wait_ge(ph.s["e_ready"], 1)
                ch.step(dve.tensor_reduce(total[:], w[:], AX.X, ALU.add))
                ch.wait()
                ch.step(dve.reciprocal(inv[:], total[:]))
                ch.wait()
                ch.step(dve.tensor_tensor(w[:], w[:], wide(inv), ALU.mult))
                ch.wait()
                dve.wait_ge(ph.s["conv"], 3)
                top_mask(dve, ph, ch, w, m8, 2, E, tmp, mask)
                ch.step(dve.tensor_tensor(w[:], w[:], mask[:], ALU.mult))
                ch.wait()
                ch.step(dve.tensor_reduce(total[:], w[:], AX.X, ALU.add))
                ch.wait()
                ch.step(dve.reciprocal(inv[:], total[:]))
                ch.wait()
                ch.step(dve.tensor_tensor(wts[:], w[:], wide(inv), ALU.mult))
                ch.wait()


def l2_feed_forward(k, x_in, x_out, xt_out):
    nc, a = k.nc, k.a
    E, R = 32, 16
    ER = E * R
    RC = ER // P
    k.x_now = x_in
    with ExitStack() as keep:
        wts = keep.enter_context(nc.sbuf_tensor("f2_wts", [P, NT, E], F32))
        l2_weights(k, wts)
        with Phase(k, "f2") as ph:
            tail = Tail(ph, x_in, x_out, xt_out)
            wb, wa, bias = ph.sb("wb", [P, DC, ER]), ph.sb("wa", [P, RC, D]), ph.sb("wbias", [E, D])
            xs = ph.sb("xs", [P, DC, GN])
            low = ph.sb("low", [P, 2, ER])
            wrow = ph.sb("wrow", [P, GT, E])
            cols = ph.sb("cols", [P, RC, P])
            wcol = ph.sb("wcol", [E, P])
            ph.sems_of("w_ld xs_ld low_done weighted turned moved tile_done wrow_ready")
            with nc.Block() as block:

                @block.sync
                def _(sp):
                    for dst, src in ((wb[:], weight_rows(a["L2_ffn_B"])), (wa[:], weight_rows(a["L2_ffn_A"])), (bias[:], a["L2_ffn_bias"])):
                        sp.dma_start(dst, src).then_inc(ph.s["w_ld"], 16)
                    with sp.Fori(0, NG) as g:
                        sp.wait_ge(ph.s["low_done"], GT * g)
                        sp.dma_start(xs[:], k.xt[:, ds(g * GN, GN)].rearrange("(c p) t -> p c t", p=P)).then_inc(ph.s["xs_ld"], 16)
                        tail.load(sp, g)

                @block.gpsimd
                def _(pool):
                    with pool.Fori(0, NG) as g:
                        pool.wait_ge(ph.s["y_ready"], g)
                        pool.tensor_copy(wrow[:], wts[:, ds(g * GT, GT), :]).then_inc(ph.s["wrow_ready"], 1)
                        tail.store(pool, g)
                    tail.finish(pool)

                @block.tensor
                def _(pe):
                    pe.wait_ge(ph.s["w_ld"], 48)
                    with pe.Fori(0, NG) as g:
                        pe.wait_ge(ph.s["xs_ld"], 16 * g + 16)

                        def lower(j):
                            pe.wait_ge(ph.s["weighted"], GT * g + max(j - 1, 0))
                            for d in range(DC):
                                ins = pe.matmul(k.ps[:, j % 2, :], xs[:, d, j * P:(j + 1) * P], wb[:, d, :], start=d == 0, stop=d == DC - 1)
                            ins.then_inc(ph.s["low_done"], 1)

                        lower(0)
                        for j in range(GT):
                            if j + 1 < GT:
                                lower(j + 1)
                            pe.wait_ge(ph.s["weighted"], GT * g + j + 1)
                            pe.wait_ge(ph.s["wrow_ready"], g + 1)
                            pe.wait_ge(ph.s["moved"], 2 * (GT * g + j))
                            for c in range(RC):
                                pe.transpose(k.ps[:, 6, c * P:(c + 1) * P], low[:, j % 2, c * P:(c + 1) * P], k.ident[:])
                            pe.transpose(k.ps[0:E, 7, 0:P], wrow[:, j, :], k.ident[:]).then_inc(ph.s["turned"], 1)
                            pe.wait_ge(ph.s["moved"], 2 * (GT * g + j) + 2)
                            if j == 0:
                                pe.wait_ge(ph.s["r_done"], g)
                            for c in range(RC):
                                pe.matmul(tail.y[:, j, :], cols[:, c, :], wa[:, c, :], start=c == 0, stop=False)
                            ins = pe.matmul(tail.y[:, j, :], wcol[:], bias[:], start=False, stop=True)
                            ins.then_inc(ph.s["tile_done"] if j < GT - 1 else ph.s["y_ready"], 1)
                        tail.tensor(pe, g)

                @block.scalar
                def _(act):
                    with act.Fori(0, NG) as g:
                        for j in range(GT):
                            act.wait_ge(ph.s["turned"], GT * g + j + 1)
                            if j:
                                act.wait_ge(ph.s["tile_done"], (GT - 1) * g + j)
                            else:
                                act.wait_ge(ph.s["y_ready"], g)
                            act.activation(cols[:].rearrange("p c t -> p (c t)"), k.ps[:, 6, :], ACT.Copy).then_inc(ph.s["moved"], 1)
                            act.activation(wcol[:], k.ps[0:E, 7, 0:P], ACT.Copy).then_inc(ph.s["moved"], 1)
                        tail.scalar(act, g)

                @block.vector
                def _(dve):
                    with dve.Fori(0, NG) as g:
                        for j in range(GT):
                            dve.wait_ge(ph.s["low_done"], GT * g + j + 1)
                            dve.wait_ge(ph.s["wrow_ready"], g + 1)
                            dve.wait_ge(ph.s["turned"], GT * g + max(j - 1, 0))
                            dve.tensor_tensor(low[:, j % 2, :].rearrange("p (e r) -> p e r", r=R), k.ps[:, j % 2, :].rearrange("p (e r) -> p e r", r=R),
                                              wrow[:, j, :, None].to_broadcast([P, E, R]), ALU.mult).then_inc(ph.s["weighted"], 1)
                        tail.vector(dve, g)


def l3_feed_forward(k, x_in, x_out, xt_out):
    nc, a = k.nc, k.a
    E, HID = 8, 1024
    HC = HID // P
    TW = 2 * P
    norm_columns(k, "f3n", x_in, k.xnt, a["L3_ffn_ln_scale"], a["L3_ffn_ln_bias"])
    with ExitStack() as keep:
        y_all = keep.enter_context(nc.sbuf_tensor("f3_y_all", [P, NT, D], F32))
        with Phase(k, "f3") as ph:
            wat, wnx = ph.sb("wat", [P, DC, D]), ph.sb("wnx", [P, DC, D])
            bat, bnx = ph.sb("bat", [P, DC]), ph.sb("bnx", [P, D])
            xn, xs = ph.sb("xn", [P, 2, DC, TW]), ph.sb("xs", [P, 2, DC, TW])
            w1, w2 = ph.sb("w1", [P, 2, DC, HID]), ph.sb("w2", [P, 2, HC, D])
            b1, b2 = ph.sb("b1", [P, 2, HC]), ph.sb("b2", [P, 2, DC])
            xa = ph.sb("xa", [P, DC, TW])
            hid = ph.sb("hid", [P, HC, TW])
            eo = ph.sb("eo", [P, DC, TW])
            pre = ph.sb("pre", [P, 2, D])
            ph.sems_of("c_ld xa_mm xa_ready h_mm h_ready eo_mm eo_ready y_mm pre_ready y_ready")
            ld = [ph.sem("ld0"), ph.sem("ld1")]
            NLD = 8
            with nc.Block() as block:

                @block.sync
                def _(sp):
                    for dst, src in ((wat[:], weight_rows(a["L3_ffn_attn_w"])), (wnx[:], weight_rows(a["L3_ffn_next_w"])), (bat[:], a["L3_ffn_attn_b"]),
                                     (bnx[:], a["L3_ffn_next_b"])):
                        sp.dma_start(dst, src).then_inc(ph.s["c_ld"], 16)
                    with sp.Fori(0, E // 2) as t:
                        for s in range(2):
                            e = t * 2 + s
                            sp.wait_ge(ph.s["y_mm"], e + 1)
                            for half in range(2):
                                for dst, src in ((xn, k.xnt), (xs, k.xt)):
                                    sp.dma_start(dst[:, s, :, half * P:(half + 1) * P], src[:, ds(half * T + e * P, P)].rearrange("(c p) t -> p c t", p=P)).then_inc(ld[s], 16)
                            sp.dma_start(w1[:, s, :, :], a["L3_ffn_w1"][ds(e, 1), :, :].rearrange("o (c p) n -> p (o c) n", p=P)).then_inc(ld[s], 16)
                            sp.dma_start(w2[:, s, :, :], a["L3_ffn_w2"][ds(e, 1), :, :].rearrange("o (c p) n -> p (o c) n", p=P)).then_inc(ld[s], 16)
                            sp.dma_start(b1[:, s, :], a["L3_ffn_b1"][ds(e, 1), :, :].rearrange("o p c -> p (o c)")).then_inc(ld[s], 16)
                            sp.dma_start(b2[:, s, :], a["L3_ffn_b2"][ds(e, 1), :, :].rearrange("o p c -> p (o c)")).then_inc(ld[s], 16)

                @block.tensor
                def _(pe):
                    pe.sem_inc(ph.s["y_mm"], 2)
                    pe.wait_ge(ph.s["c_ld"], 64)
                    with pe.Fori(0, E // 2) as t:
                        for s in range(2):
                            e = t * 2 + s
                            pe.wait_ge(ld[s], 16 * NLD * t + 16 * NLD)
                            pe.wait_ge(ph.s["xa_ready"], DC * e)
                            for c in range(DC):
                                for d in range(DC):
                                    ins = pe.matmul(k.ps[:, 0, c * TW:(c + 1) * TW], wat[:, d, c * P:(c + 1) * P], xn[:, s, d, :], start=d == 0, stop=d == DC - 1)
                            ins.then_inc(ph.s["xa_mm"], 1)
                            pe.wait_ge(ph.s["xa_ready"], DC * e + DC)
                            for c in range(HC):
                                pe.wait_ge(ph.s["h_ready"], HC * e + max(c - 3, 0))
                                for d in range(DC):
                                    ins = pe.matmul(k.ps[:, 1 + c % 4, 0:TW], w1[:, s, d, c * P:(c + 1) * P], xa[:, d, :], start=d == 0, stop=d == DC - 1)
                                ins.then_inc(ph.s["h_mm"], 1)
                            pe.wait_ge(ph.s["eo_ready"], DC * e)
                            for c in range(DC):
                                for d in range(HC):
                                    if c == 0:
                                        pe.wait_ge(ph.s["h_ready"], HC * e + d + 1)
                                    ins = pe.matmul(k.ps[:, 5, c * TW:(c + 1) * TW], w2[:, s, d, c * P:(c + 1) * P], hid[:, d, :], start=d == 0, stop=d == HC - 1)
                            ins.then_inc(ph.s["eo_mm"], 1)
                            pe.wait_ge(ph.s["eo_ready"], DC * e + DC)
                            pe.wait_ge(ph.s["pre_ready"], e)
                            for j in range(2):
                                for d in range(DC):
                                    ins = pe.matmul(k.ps[:, 6, j * D:(j + 1) * D], eo[:, d, j * P:(j + 1) * P], wnx[:, d, :], start=d == 0, stop=d == DC - 1)
                            ins.then_inc(ph.s["y_mm"], 1)

                @block.scalar
                def _(act):
                    act.wait_ge(ph.s["c_ld"], 64)
                    with act.Fori(0, E // 2) as t:
                        for s in range(2):
                            e = t * 2 + s
                            act.wait_ge(ld[s], 16 * NLD * t + 16 * NLD)
                            for c in range(HC):
                                act.wait_ge(ph.s["h_mm"], HC * e + c + 1)
                                if c == 0:
                                    act.wait_ge(ph.s["eo_mm"], e)
                                act.activation(hid[:, c, :], k.ps[:, 1 + c % 4, 0:TW], ACT.Gelu, bias=b1[:, s, c:c + 1]).then_inc(ph.s["h_ready"], 1)
                            act.wait_ge(ph.s["pre_ready"], e + 1)
                            act.activation(y_all[:, ds(e, 2, E), :], pre[:], ACT.Gelu).then_inc(ph.s["y_ready"], 1)
                    act.wait_ge(ph.s["y_ready"], E)

                @block.vector
                def _(dve):
                    dve.wait_ge(ph.s["c_ld"], 64)
                    with dve.Fori(0, E // 2) as t:
                        for s in range(2):
                            e = t * 2 + s
                            dve.wait_ge(ld[s], 16 * NLD * t + 16 * NLD)
                            dve.wait_ge(ph.s["xa_mm"], e + 1)
                            dve.wait_ge(ph.s["h_mm"], HC * e)
                            for c in range(DC):
                                dve.scalar_tensor_tensor(out=xa[:, c, :], in0=k.ps[:, 0, c * TW:(c + 1) * TW], scalar=bat[:, c:c + 1], in1=xs[:, s, c, :],
                                                         op0=ALU.add, op1=ALU.add).then_inc(ph.s["xa_ready"], 1)
                            dve.wait_ge(ph.s["eo_mm"], e + 1)
                            dve.wait_ge(ph.s["y_mm"], e + 2)
                            for c in range(DC):
                                dve.tensor_scalar(eo[:, c, :], k.ps[:, 5, c * TW:(c + 1) * TW], b2[:, s, c:c + 1], None, ALU.add).then_inc(ph.s["eo_ready"], 1)
                            dve.wait_ge(ph.s["y_mm"], e + 3)
                            dve.wait_ge(ph.s["y_ready"], e)
                            dve.tensor_tensor(pre[:], k.ps[:, 6, :].rearrange("p (j d) -> p j d", d=D), bnx[:, None, :].to_broadcast([P, 2, D]), ALU.add).then_inc(ph.s["pre_ready"], 1)

        project_out(k, "f3o", y_all, D, None, x_in, x_out, xt_out)


class Kernel:

    def __init__(self, nc, a):
        self.nc, self.a = nc, a
        self.ps = nc.alloc_psum_tensor("ps", [P, 8, 512], F32)
        self.ident = nc.alloc_sbuf_tensor("ident", [P, P], F32)
        self.ident_b = nc.alloc_sbuf_tensor("ident_b", [P, P], BF16)
        self.mask = nc.alloc_sbuf_tensor("mask", [P, P], BF16)
        self.x = [self.dram("x0", [N, D]), self.dram("x1", [N, D])]
        self.xt = self.dram("xt", [D, N])
        self.xnt = self.dram("xnt", [D, N])

    def dram(self, name, shape, dt=F32):
        return self.nc.dram_tensor(name, tuple(shape), dt).ap()


def constants(k):
    nc = k.nc
    with Phase(k, "const") as ph:
        ph.sems_of("ld conv")
        idf = ph.sb("idf", [P, 2, P])
        with nc.Block() as block:

            @block.sync
            def _(sp):
                sp.dma_start(k.ident[:], k.a["c_ident"]).then_inc(ph.s["ld"], 16)
                sp.dma_start(idf[:, 0, :], k.a["c_mask"]).then_inc(ph.s["ld"], 16)
                sp.wait_ge(ph.s["ld"], 32)

            @block.vector
            def _(dve):
                dve.wait_ge(ph.s["ld"], 32)
                dve.tensor_copy(k.ident_b[:], k.ident[:]).then_inc(ph.s["conv"], 1)
                dve.tensor_copy(k.mask[:], idf[:, 0, :]).then_inc(ph.s["conv"], 1)
                dve.wait_ge(ph.s["conv"], 2)


STAGES = [l0_self_attention, l0_cross_attention, l0_feed_forward, l1_self_attention, l1_cross_attention, l1_feed_forward,
          l2_self_attention, l2_cross_attention, l2_feed_forward, l3_self_attention, l3_cross_attention, l3_feed_forward]


def build(nc, a, out, stages):
    k = Kernel(nc, a)
    constants(k)
    x = a["x"]
    for n, stage in enumerate(stages):
        last = n == len(stages) - 1
        x_out = out if last else k.x[n % 2]
        stage(k, x, x_out, None if last else k.xt)
        x = x_out


def layouts(i):
    import numpy as np

    def cols(v):
        return np.ascontiguousarray(np.reshape(v, (-1, P)).T)

    def rows(v, n=P):
        return np.ascontiguousarray(np.broadcast_to(np.reshape(v, (1, -1)), (n, np.size(v))))

    def by_halves(w):
        return w.reshape(D, -1, 4, 32, 2).transpose(0, 1, 4, 2, 3).reshape(D, -1)

    def kv(w, n):
        return w.reshape((16, 2, 16) + w.shape[1:])[:, n].reshape((256,) + w.shape[1:])

    freq = np.float32(1.0) / np.float32(10000.0) ** (np.arange(0, 64, 2, dtype=np.float32) / np.float32(64))
    angle = np.tile(freq, 4)[:, None] * np.arange(T, dtype=np.float32)[None, :]
    rope = [(f(angle.astype(np.float64)) * 64 ** -0.25).astype(np.float32) for f in (np.cos, np.sin)]

    c = {k: np.asarray(v) for k, v in i.items()}
    r = {
        "c_ident": np.eye(P, dtype=np.float32),
        "c_mask": np.where(np.arange(P)[None, :] > np.arange(P)[:, None], np.float32(-1e30), np.float32(0)),
        "x": c["x"].reshape(N, D),
        "L0_attn_in_ln_w": cols(c["L0_attn_in_ln_w"]),
        "L0_attn_in_ln_b": cols(c["L0_attn_in_ln_b"]),
        "L0_attn_W_in": c["L0_attn_W_in"].T,
        "L0_attn_b_col": cols(c["L0_attn_b_in"][:1024]),
        "L0_attn_b_y": c["L0_attn_b_in"][2048:].reshape(16, 1),
        "L0_attn_b_row": rows(c["L0_attn_b_in"][1024:2048]),
        "L0_attn_by_head": np.stack([cols(np.repeat(c["L0_attn_smear_factor"], 32)), cols(np.repeat(c["L0_attn_log_scale"], 32))], 1),
        "L0_attn_W_out": c["L0_attn_W_out"].T,
        "L0_attn_out_ln_w": rows(c["L0_attn_out_ln_w"]),
        "L0_attn_out_ln_b": rows(c["L0_attn_out_ln_b"]),
        "c_before": np.triu(np.ones((P, P), np.float32), 1),
        "L0_ffn_gate_w": c["L0_ffn_gate_w"].T,
        "L0_ffn_bias": rows(c["L0_ffn_bias"]),
        "L0_ffn_W1": np.concatenate([c["L0_ffn_W1"], c["L0_ffn_sw1"].T[None]]),
        "L0_ffn_W3": np.concatenate([c["L0_ffn_W3"], c["L0_ffn_sw3"].T[None]]),
        "L0_ffn_W2": np.concatenate([c["L0_ffn_W2"], c["L0_ffn_sw2"].T[None]]),
        "L1_ffn_W1": np.concatenate([c["L1_ffn_W1"], c["L1_ffn_Ws1"][None]]),
        "L1_ffn_W2": np.concatenate([c["L1_ffn_W2"], c["L1_ffn_Ws2"][None]]),
        "L1_ffn_Wr": c["L1_ffn_Wr"],
        "L2_ffn_prototypes": c["L2_ffn_prototypes"].T,
        "L2_ffn_temp": rows(c["L2_ffn_temp"]),
        "L2_ffn_B": c["L2_ffn_B"].reshape(512, D).T,
        "L2_ffn_A": c["L2_ffn_A"].transpose(0, 2, 1).reshape(512, D),
        "L2_ffn_bias": c["L2_ffn_bias"],
        "L3_ffn_ln_scale": cols(c["L3_ffn_ln_scale"]),
        "L3_ffn_ln_bias": cols(c["L3_ffn_ln_bias"]),
        "L3_ffn_attn_w": c["L3_ffn_attn_w"].T,
        "L3_ffn_attn_b": cols(c["L3_ffn_attn_b"]),
        "L3_ffn_next_w": c["L3_ffn_next_w"].T,
        "L3_ffn_next_b": rows(c["L3_ffn_next_b"]),
        "L3_ffn_w1": c["L3_ffn_w1"],
        "L3_ffn_w2": c["L3_ffn_w2"],
        "L3_ffn_b1": c["L3_ffn_b1"].reshape(8, 8, P).transpose(0, 2, 1),
        "L3_ffn_b2": c["L3_ffn_b2"].reshape(8, 2, P).transpose(0, 2, 1),
        "c_cos": rope[0],
        "c_sin": rope[1],
        "L1_attn_Wq": by_halves(c["L1_attn_Wq"]),
        "L1_attn_Wk": by_halves(c["L1_attn_Wk"]),
        "L3_attn_W_dq": c["L3_attn_W_dq"],
        "L3_attn_W_dq_T": c["L3_attn_W_dq"].T,
        "L3_attn_W_dkv": c["L3_attn_W_dkv"].T,
        "L3_attn_W_uq": c["L3_attn_W_uq"],
        "L3_attn_W_uq_T": c["L3_attn_W_uq"].T,
        "L3_attn_W_uk": c["L3_attn_W_uk"],
        "L3_attn_W_uv": c["L3_attn_W_uv"],
        "L3_attn_W_o": c["L3_attn_W_o"].T,
        "ctx_T": c["ctx_768"].reshape(B * M, CTX).T,
        "ctx_rows": c["ctx_768"].transpose(1, 0, 2),
        "L0_xattn_bout": rows(c["L0_xattn_bout"]),
        "L1_xattn_Wq": c["L1_xattn_Wq"].T,
        "L1_xattn_bq": cols(c["L1_xattn_bq"]),
        "L1_xattn_Wk": kv(c["L1_xattn_Wkv"], 0).T,
        "L1_xattn_Wv": kv(c["L1_xattn_Wkv"], 1).T,
        "L1_xattn_bk": cols(kv(c["L1_xattn_bkv"], 0)),
        "L1_xattn_bv": rows(kv(c["L1_xattn_bkv"], 1), M),
        "L1_xattn_Wo": c["L1_xattn_Wo"].T,
        "L1_xattn_bo": rows(c["L1_xattn_bo"]),
        "L2_xattn_bo": rows(c["L2_xattn_bo"]),
        "L3_xattn_g_x": cols(c["L3_xattn_g_x"]),
        "L3_xattn_b_x": cols(c["L3_xattn_b_x"]),
        "L3_xattn_norm_c": np.stack([c["L3_xattn_g_c"], c["L3_xattn_b_c"]], 1),
    }
    for name in ("L0_xattn_Wq L0_xattn_Wk L0_xattn_Wv L0_xattn_Wout L1_attn_Wv L1_attn_Wo L2_attn_Wq L2_attn_Wk L2_attn_Wv L2_attn_Wo "
                 "L3_xattn_Wq L3_xattn_Wk L3_xattn_Wv L3_xattn_Wo").split():
        r[name] = c[name]
    for name in "L2_xattn_Wq L2_xattn_Wk L2_xattn_Wv L2_xattn_Wo".split():
        r[name] = c[name].T
    return {k: np.ascontiguousarray(v) for k, v in r.items()}


def kernel(**inputs):
    import numpy as _np
    import concourse.bacc as _bacc
    from concourse import mybir as _mybir
    from concourse.bass_utils import run_bass_kernel_spmd as _run

    nc = _bacc.Bacc("TRN2", target_bir_lowering=False, num_devices=1)
    arrays, args = {}, {}
    for name, v in layouts(inputs).items():
        arrays[f"in_{name}_dram"] = v
        args[name] = nc.dram_tensor(f"in_{name}_dram", v.shape, _mybir.dt.from_np(v.dtype), kind="ExternalInput").ap()
    out = nc.dram_tensor("out_dram", (N, D), F32, kind="ExternalOutput").ap()
    build(nc, args, out, STAGES)
    r = _run(nc, [arrays], core_ids=[0])
    return _np.asarray(r.results[0]["out_dram"]).reshape(B, T, D)
```

```python
from contextlib import ExitStack, contextmanager

import concourse.bass as bass
from concourse import mybir

F32 = mybir.dt.float32
BF16 = mybir.dt.bfloat16
ALU = mybir.AluOpType
ACT = mybir.ActivationFunctionType
AX = mybir.AxisListType

P = 128
D = 256
DC = D // P
B, T = 2, 1024
N = B * T
NT = N // P
TB = T // P
M = 77
CTX = 192
EPS = 1e-5
GT = 4
GN = GT * P
NG = N // GN
ds = bass.ds


@contextmanager
def times(eng, n):
    if n == 1:
        yield 0
    else:
        with eng.Fori(0, n) as i:
            yield i


def after(eng, sem, n):
    if not (isinstance(n, int) and n == 0):
        eng.wait_ge(sem, n)


class Count:

    def __init__(self, eng, sem, n, turn):
        self.eng, self.sem, self.n, self.turn, self.at = eng, sem, n, turn, 0

    def step(self, ins):
        ins.then_inc(self.sem, 1)
        self.at += 1
        return self.at

    def value(self, at=None):
        return self.turn * self.n + (self.at if at is None else at)

    def wait(self, at=None):
        self.eng.wait_ge(self.sem, self.value(at))

    def close(self):
        assert self.at == self.n, f"{self.at} steps in a turn, not {self.n}"


class Phase:

    def __init__(self, k, name):
        self.k, self.name, self.ctx, self.sems, self.s = k, name, ExitStack(), [], {}

    def sb(self, name, shape, dt=F32):
        return self.ctx.enter_context(self.k.nc.sbuf_tensor(f"{self.name}_{name}", shape, dt))

    def sem(self, name):
        s = self.k.nc.alloc_semaphore(f"{self.name}_{name}")
        self.sems.append(s)
        return s

    def sems_of(self, names):
        self.s.update({n: self.sem(n) for n in names.split()})

    def __enter__(self):
        return self

    def __exit__(self, *exc):
        if exc[0] is None:
            self.ctx.close()
            self.k.nc.clear_and_free_semaphores(self.sems)
            self.k.nc.all_engine_barrier()


def weight_rows(w, kc=None):
    return w.rearrange("(c p) n -> p c n", p=P)


class Tail:

    def __init__(self, ph, x_in, x_out, xt_out, bias=None, pre=None):
        self.ph, self.x_in, self.x_out, self.xt_out, self.bias, self.pre = ph, x_in, x_out, xt_out, bias, pre
        k = ph.k
        self.y = k.ps[:, 2:4, :].rearrange("p b (t d) -> p (b t) d", d=D)
        self.y_of = lambda g: self.y
        self.own_y = True
        self.tp = k.ps[:, 4:6, :]
        self.xin = ph.sb("xin", [P, GT, D])
        self.r = ph.sb("r", [P, GT, D])
        self.stats = ph.sb("stats", [P, GT, 6])
        self.mv = ph.sb("mv", [P, GT, 2])
        self.ve = ph.sb("ve", [P, GT])
        self.gap = ph.sb("gap", [P, 1])
        self.sd = ph.sb("sd", [P, GT])
        self.rs = ph.sb("rs", [P, GT])
        self.xn = ph.sb("xn", [P, GT, D])
        self.xts = ph.sb("xts", [P, DC, GN])
        ph.sems_of("y_ready xin_ld r_done chain ve_ready sd_ready xn_ready xn_turned xts_ready x_st xt_st")
        self.norms = 2 if pre else 1
        self.n_chain = (self.norms - 1) * (3 * GT + 3) + (bias is not None) + 2 * GT + 1

    def load(self, sp, g):
        ph = self.ph
        after(sp, ph.s["r_done"], g)
        sp.dma_start(self.xin[:], self.x_in[ds(g * GN, GN), :].rearrange("(t p) d -> p t d", p=P)).then_inc(ph.s["xin_ld"], 16)

    def store(self, pool, g):
        ph = self.ph
        pool.wait_ge(ph.s["xn_ready"], g + 1)
        pool.dma_start(self.x_out[ds(g * GN, GN), :].rearrange("(t p) d -> p t d", p=P), self.xn[:]).then_inc(ph.s["x_st"], 16)
        if self.xt_out is not None:
            pool.wait_ge(ph.s["xts_ready"], g + 1)
            pool.dma_start(self.xt_out[:, ds(g * GN, GN)].rearrange("(c p) t -> p c t", p=P), self.xts[:]).then_inc(ph.s["xt_st"], 16)

    def finish(self, pool):
        pool.wait_ge(self.ph.s["x_st"], 16 * NG)
        if self.xt_out is not None:
            pool.wait_ge(self.ph.s["xt_st"], 16 * NG)

    def _norm(self, dve, ch, g, n, src, dst, done=None):
        ph = self.ph
        for t in range(GT):
            ch.step(dve.bn_stats(self.stats[:, t, :], src[:, t, :]))
        ch.wait()
        dve.memset(self.gap[:], 0.0)
        for t in range(GT):
            ch.step(dve.bn_aggr(self.mv[:, t, :], self.stats[:, t, :]))
        ch.wait()
        dve.tensor_scalar(self.ve[:], self.mv[:, :, 1], EPS, None, ALU.add).then_inc(ph.s["ve_ready"], 1)
        dve.wait_ge(ph.s["sd_ready"], self.norms * g + n + 1)
        ch.step(dve.reciprocal(self.rs[:], self.sd[:]))
        ch.wait()
        for t in range(GT):
            ins = dve.tensor_scalar(dst[:, t, :], src[:, t, :], self.mv[:, t, 0:1], self.rs[:, t:t + 1],
                                    ALU.subtract, ALU.mult)
            if done is None:
                ch.step(ins)
        if done is None:
            ch.wait()
        else:
            ins.then_inc(done, 1)

    def vector(self, dve, g):
        ph = self.ph
        ch = Count(dve, ph.s["chain"], self.n_chain, g)
        after(dve, ph.s["xn_ready"], g)
        if self.own_y:
            dve.wait_ge(ph.s["y_ready"], g + 1)
        y = self.y_of(g)
        if self.pre:
            w, b = self.pre
            self._norm(dve, ch, g, 0, y, self.r)
            for v, op in ((w, ALU.mult), (b, ALU.add)):
                ch.step(dve.tensor_tensor(self.r[:], self.r[:], v[:, None, :].to_broadcast([P, GT, D]), op))
                ch.wait()
            y = self.r
        dve.wait_ge(ph.s["xin_ld"], 16 * g + 16)
        dve.tensor_tensor(self.r[:], y[:], self.xin[:], ALU.add).then_inc(ph.s["r_done"], 1)
        dve.wait_ge(ph.s["r_done"], g + 1)
        if self.bias is not None:
            ch.step(dve.tensor_tensor(self.r[:], self.r[:], self.bias[:, None, :].to_broadcast([P, GT, D]), ALU.add))
            ch.wait()
        after(dve, ph.s["x_st"], 16 * g)
        if self.xt_out is not None:
            after(dve, ph.s["xn_turned"], g)
        self._norm(dve, ch, g, self.norms - 1, self.r, self.xn, ph.s["xn_ready"])
        ch.close()

    def scalar(self, act, g):
        ph = self.ph
        for n in range(self.norms):
            act.wait_ge(ph.s["ve_ready"], self.norms * g + n + 1)
            act.activation(self.sd[:], self.ve[:], ACT.Sqrt).then_inc(ph.s["sd_ready"], 1)
        if self.xt_out is not None:
            act.wait_ge(ph.s["xn_turned"], g + 1)
            after(act, ph.s["xt_st"], 16 * g)
            act.activation(self.xts[:], self.tp, ACT.Copy).then_inc(ph.s["xts_ready"], 1)

    def tensor(self, pe, g):
        ph = self.ph
        if self.xt_out is None:
            return
        pe.wait_ge(ph.s["xn_ready"], g + 1)
        after(pe, ph.s["xts_ready"], g)
        for c in range(DC):
            for t in range(GT):
                ins = pe.transpose(self.tp[:, c, t * P:(t + 1) * P], self.xn[:, t, c * P:(c + 1) * P], ph.k.ident[:])
        ins.then_inc(ph.s["xn_turned"], 1)


def norm_columns(k, name, x_in, xnt_out, w_col, b_col):
    nc = k.nc
    with Phase(k, name) as ph:
        xin = ph.sb("xin", [P, NG, GT, D])
        xc = ph.sb("xc", [P, NG, GT, D])
        wb = ph.sb("wb", [P, 2, DC])
        stats, mv = ph.sb("stats", [P, NG, GT, 6]), ph.sb("mv", [P, NG, GT, 2])
        ve, sd, rs = ph.sb("ve", [P, NG, GT]), ph.sb("sd", [P, NG, GT]), ph.sb("rs", [P, NG, GT])
        gap = ph.sb("gap", [P, 1])
        xts = ph.sb("xts", [P, 2, DC, GN])
        TP = [k.ps[:, 4:6, :], k.ps[:, 6:8, :]]
        ph.sems_of("wb_ld chain ve_ready sd_ready xc_ready turned xts_ready xt_st")
        xin_ld = [ph.sem(f"xin_ld{g}") for g in range(NG)]
        with nc.Block() as block:

            @block.sync
            def _(sp):
                for g in range(NG):
                    sp.dma_start(xin[:, g, :, :], x_in[g * GN:(g + 1) * GN, :].rearrange("(t p) d -> p t d", p=P)).then_inc(xin_ld[g], 16)
                sp.dma_start(wb[:, 0, :], w_col).then_inc(ph.s["wb_ld"], 16)
                sp.dma_start(wb[:, 1, :], b_col).then_inc(ph.s["wb_ld"], 16)

            @block.vector
            def _(dve):
                ch = Count(dve, ph.s["chain"], 0, 0)

                def moments(g):
                    dve.wait_ge(xin_ld[g], 16)
                    for t in range(GT):
                        ch.step(dve.bn_stats(stats[:, g, t, :], xin[:, g, t, :]))
                    ch.wait()
                    for t in range(GT):
                        ch.step(dve.bn_aggr(mv[:, g, t, :], stats[:, g, t, :]))
                    ch.wait()
                    dve.tensor_scalar(ve[:, g, :], mv[:, g, :, 1], EPS, None, ALU.add).then_inc(ph.s["ve_ready"], 1)

                def normed(g):
                    dve.wait_ge(ph.s["sd_ready"], g + 1)
                    ch.step(dve.reciprocal(rs[:, g, :], sd[:, g, :]))
                    ch.wait()
                    for t in range(GT):
                        ins = dve.tensor_scalar(xc[:, g, t, :], xin[:, g, t, :], mv[:, g, t, 0:1], rs[:, g, t:t + 1],
                                                ALU.subtract, ALU.mult)
                    ins.then_inc(ph.s["xc_ready"], 1)

                moments(0)
                for g in range(NG):
                    if g + 1 < NG:
                        moments(g + 1)
                    normed(g)

            @block.scalar
            def _(act):
                act.wait_ge(ph.s["wb_ld"], 32)

                def columns(g):
                    act.wait_ge(ph.s["turned"], g + 1)
                    if g >= 2:
                        act.wait_ge(ph.s["xt_st"], 16 * (g - 1))
                    for c in range(DC):
                        ins = act.activation(xts[:, g % 2, c, :], TP[g % 2][:, c, :], ACT.Identity, scale=wb[:, 0, c:c + 1],
                                             bias=wb[:, 1, c:c + 1])
                    ins.then_inc(ph.s["xts_ready"], 1)

                for g in range(NG):
                    act.wait_ge(ph.s["ve_ready"], g + 1)
                    act.activation(sd[:, g, :], ve[:, g, :], ACT.Sqrt).then_inc(ph.s["sd_ready"], 1)
                    if g >= 2:
                        columns(g - 2)
                columns(NG - 2)
                columns(NG - 1)

            @block.tensor
            def _(pe):
                for g in range(NG):
                    pe.wait_ge(ph.s["xc_ready"], g + 1)
                    if g >= 2:
                        pe.wait_ge(ph.s["xts_ready"], g - 1)
                    for c in range(DC):
                        for t in range(GT):
                            ins = pe.transpose(TP[g % 2][:, c, t * P:(t + 1) * P], xc[:, g, t, c * P:(c + 1) * P], k.ident[:])
                    ins.then_inc(ph.s["turned"], 1)

            @block.gpsimd
            def _(pool):
                for g in range(NG):
                    pool.wait_ge(ph.s["xts_ready"], g + 1)
                    if g:
                        pool.wait_ge(ph.s["xt_st"], 16 * g)
                    pool.dma_start(xnt_out[:, g * GN:(g + 1) * GN].rearrange("(c p) t -> p c t", p=P), xts[:, g % 2, :, :]).then_inc(ph.s["xt_st"], 16)
                pool.wait_ge(ph.s["xt_st"], 16 * NG)


class Unit:

    def __init__(self, tiles, scores, mask_at, maxima, exps, turns, values, group, first, last):
        self.tiles, self.scores, self.mask_at, self.maxima, self.exps = tiles, scores, mask_at, maxima, exps
        self.turns, self.values, self.group, self.first, self.last = turns, values, group, first, last


def causal_units(dh):
    per = min(TB, 512 // dh)
    units = []
    for b in range(B):
        for i in range(TB):
            w = (i + 1) * P
            scores = [(c, min(512, w - c), b * TB + i, b * T + c) for c in range(0, w, 512)]
            turns = [[(j * P, P, j * P) for j in range(c, min(c + 4, i + 1))] for c in range(0, i + 1, 4)]
            n = len(units)
            units.append(Unit([b * TB + i], scores, i * P, [(0, w)], [(0, 0, w)], turns,
                              [[(j * P, b * TB + j) for j in range(i + 1)]], n // per, n % per == 0, n % per == per - 1))
            units[-1].slot, units[-1].per = n % per, per
    return units


def cross_units(dh, keys, n_blocks):
    units = []
    step = P if n_blocks == 1 else 2 * P
    for u in range(NT // GT):
        tiles = [GT * u + j for j in range(GT)]
        kb = [tiles[0] // TB] if n_blocks == 1 else list(range(n_blocks))
        scores = [(j * step, n_blocks * M, t, kb[0] * M) for j, t in enumerate(tiles)]
        turns = [[(j * step + n * M, M, n * 512 + j * P) for j in range(GT)] for n in range(n_blocks)]
        values = [[(n * 512 + j * P, kb[n]) for n in range(n_blocks)] for j in range(GT)]
        exps = [(j, j * step, j * step + n_blocks * M) for j in range(GT)]
        units.append(Unit(tiles, scores, None, [(j * step, n_blocks * M) for j in range(GT)], exps, turns, values, u, True, True))
        units[-1].slot, units[-1].per = 0, GT
        units[-1].step = step
    return units


def attention(k, name, units, heads, dk, dh, qt, kt, v_all, o_all, kv_of=1, n_keys=N, key_rows=P):
    nc = k.nc
    cross = units[0].mask_at is None
    HB = min(2, heads)
    turns = heads // HB
    U = len(units)
    kc = -(-dk // P)
    kd = min(dk, P)
    nblk = v_all.shape[1]
    small = heads > 1
    before = [sum(len(u.turns) for u in units[:i]) for i in range(U + 1)]
    G = before[-1]
    OG = units[-1].group + 1
    per = units[0].per
    with Phase(k, name) as ph:
        nslot = HB if small else 1
        qs = ph.sb("q", [kd, nslot, kc, N])
        ks = ph.sb("k", [kd, nslot, kc, n_keys])
        vs = ph.sb("v", [key_rows, HB, nblk, dh]) if small else None
        probs = ph.sb("probs", [P, 2, 1024])
        pt = ph.sb("pt", [P, 2, 1024])
        nmax = ph.sb("nmax", [P, 2, GT])
        sums = ph.sb("sums", [P, 2, per])
        rsum = ph.sb("rsum", [P, 2, per])
        ph.sems_of("passed scores max_done exps turned moved values normed recips")
        q_ld, k_ld = [ph.sem(f"q_ld{p}") for p in range(HB)], [ph.sem(f"k_ld{p}") for p in range(HB)]
        v_ready = [ph.sem(f"v_ready{p}") for p in range(HB)]
        S = [k.ps[:, 0:2, :].rearrange("p b c -> p (b c)"), k.ps[:, 2:4, :].rearrange("p b c -> p (b c)")]
        TP = [k.ps[:, 4, :], k.ps[:, 5, :]]
        O = [k.ps[:, 6, :], k.ps[:, 7, :]]
        steps = [(p, u) for p in range(HB) for u in range(U)]
        W = HB * U

        def groups_before(n):
            return (n // U) * G + before[n % U]

        with nc.Block() as block:

            @block.sync
            def _(sp):
                with times(sp, turns) as t:
                    base = t * W
                    for p in range(HB):
                        sp.wait_ge(ph.s["values"], base + (p + 1) * U)
                        if kv_of == 1:
                            kh = t * HB + p
                        else:
                            kh = (t * HB) // kv_of
                        src_q = qt[ds(t * HB + p, 1)].rearrange("h (c d) n -> d (h c) n", d=kd)
                        src_k = kt[ds(kh, 1)].rearrange("h (c d) n -> d (h c) n", d=kd)
                        sp.dma_start(qs[:, p, :, :], src_q).then_inc(q_ld[p], 16)
                        sp.dma_start(ks[:, p, :, :], src_k).then_inc(k_ld[p], 16)

            @block.gpsimd
            def _(pool):
                if not small:
                    return
                with times(pool, turns) as t:
                    for p in range(HB):
                        kh = t * HB + p if kv_of == 1 else (t * HB) // kv_of
                        pool.wait_ge(ph.s["values"], t * W + (p + 1) * U)
                        pool.sem_inc(ph.s["passed"], 1)
                        pool.tensor_copy(vs[:, p, :, :], v_all[0:key_rows, :, ds(kh * dh, dh)]).then_inc(v_ready[p], 1)

            @block.tensor
            def _(pe):
                pe.sem_inc(ph.s["values"], W)
                with times(pe, turns) as t:
                    base = t * W

                    def scores(n):
                        p, i = steps[n]
                        u = units[i]
                        if i == 0:
                            pe.wait_ge(q_ld[p], 16 * t + 16)
                            pe.wait_ge(k_ld[p], 16 * t + 16)
                        pe.wait_ge(ph.s["exps"], base + n + 1)
                        s = S[n % 2]
                        for c0, w, tile, key in u.scores:
                            own = u.mask_at is not None and c0 <= u.mask_at < c0 + w
                            for c in range(kc):
                                ins = pe.matmul(s[:, c0:c0 + w], qs[:, p, c, tile * P:(tile + 1) * P], ks[:, p, c, key:key + w],
                                                start=c == 0, stop=c == kc - 1 and not own)
                            if own:
                                ins = pe.matmul(s[:, u.mask_at:u.mask_at + P], k.ident_b[:], k.mask[:], start=False, stop=True)
                        ins.then_inc(ph.s["scores"], 1)

                    def turn(n):
                        p, i = steps[n]
                        u = units[i]
                        pe.wait_ge(ph.s["exps"], base + n + 3)
                        g0 = groups_before(n)
                        for a, group in enumerate(u.turns):
                            pe.wait_ge(ph.s["moved"], t * (HB * G) + g0 + a + 1)
                            for src, rows, dst in group:
                                at = dst % 512
                                ins = pe.transpose(TP[(g0 + a) % 2][0:rows, at:at + P], probs[:, n % 2, src:src + rows], k.ident[:])
                            ins.then_inc(ph.s["turned"], 1)

                    def values(n):
                        p, i = steps[n]
                        u = units[i]
                        if i == 0 and small:
                            pe.wait_ge(v_ready[p], t + 1)
                        pe.wait_ge(ph.s["moved"], t * (HB * G) + groups_before(n) + len(u.turns) + 2)
                        og = p * OG + u.group
                        if u.first:
                            pe.wait_ge(ph.s["normed"], t * (HB * OG) + og + 1)
                        for j, blocks in enumerate(u.values):
                            o = O[og % 2][:, (u.slot + j) * dh:(u.slot + j + 1) * dh]
                            for a, (src, blk) in enumerate(blocks):
                                v = vs[:, p, blk, :] if small else v_all[0:key_rows, blk, :]
                                ins = pe.matmul(o, pt[0:key_rows, n % 2, src:src + P], v, start=a == 0, stop=a == len(blocks) - 1)
                        ins.then_inc(ph.s["values"], 1)

                    scores(0)
                    for n in range(W):
                        if n + 1 < W:
                            scores(n + 1)
                        turn(n)
                        if n:
                            values(n - 1)
                    values(W - 1)

            @block.scalar
            def _(act):
                act.sem_inc(ph.s["exps"], 2)
                with times(act, turns) as t:
                    base = t * W
                    for n, (p, i) in enumerate(steps):
                        u = units[i]
                        og = p * OG + u.group
                        act.wait_ge(ph.s["max_done"], base + n + 1)
                        act.wait_ge(ph.s["turned"], t * (HB * G) + (groups_before(n - 1) if n else 0))
                        if u.first:
                            act.wait_ge(ph.s["normed"], t * (HB * OG) + og + 1)
                        for j, c0, c1 in u.exps:
                            ins = act.activation(probs[:, n % 2, c0:c1], S[n % 2][:, c0:c1], ACT.Exp,
                                                 bias=nmax[:, n % 2, j:j + 1], accum_out=sums[:, og % 2, u.slot + j:u.slot + j + 1])
                        ins.then_inc(ph.s["exps"], 1)

            @block.vector
            def _(dve):
                dve.sem_inc(ph.s["moved"], 2)
                dve.sem_inc(ph.s["normed"], 2)
                with times(dve, turns) as t:
                    base = t * W

                    def maximum(n):
                        p, i = steps[n]
                        u = units[i]
                        dve.wait_ge(ph.s["scores"], base + n + 1)
                        if cross:
                            w = u.maxima[0][1]
                            src = S[n % 2][:, 0:GT * u.step].rearrange("p (j c) -> p j c", j=GT)[:, :, 0:w]
                            ins = dve.tensor_reduce(nmax[:, n % 2, 0:GT], src, AX.X, ALU.max, negate=True)
                        else:
                            ins = dve.tensor_reduce(nmax[:, n % 2, 0:1], S[n % 2][:, 0:u.maxima[0][1]], AX.X, ALU.max, negate=True)
                        ins.then_inc(ph.s["max_done"], 1)

                    def move(n):
                        p, i = steps[n]
                        u = units[i]
                        g0 = groups_before(n)
                        dve.wait_ge(ph.s["values"], base + W + max(n - 1, 0))
                        for a, group in enumerate(u.turns):
                            dve.wait_ge(ph.s["turned"], t * (HB * G) + g0 + a + 1)
                            rows = group[0][1]
                            lo, w = group[0][2], len(group) * P
                            dve.tensor_copy(pt[0:rows, n % 2, lo:lo + w], TP[(g0 + a) % 2][0:rows, 0:w]).then_inc(ph.s["moved"], 1)

                    def norm(n):
                        p, i = steps[n]
                        u = units[i]
                        if not u.last:
                            return
                        og = p * OG + u.group
                        dve.wait_ge(ph.s["exps"], base + n + 3)
                        dve.wait_ge(ph.s["values"], base + W + n + 1)
                        dve.reciprocal(rsum[:, og % 2, :], sums[:, og % 2, :]).then_inc(ph.s["recips"], 1)
                        dve.wait_ge(ph.s["recips"], t * (HB * OG) + og + 1)
                        tile0 = u.tiles[-1] - per + 1
                        src = O[og % 2][:, 0:per * dh].rearrange("p (t d) -> p t d", d=dh)
                        h = t * HB + p
                        dst = o_all[:, tile0:tile0 + per, ds(h * dh, dh)]
                        dve.tensor_tensor(dst, src, rsum[:, og % 2, :, None].to_broadcast([P, per, dh]), ALU.mult).then_inc(ph.s["normed"], 1)

                    maximum(0)
                    for n in range(W):
                        if n + 1 < W:
                            maximum(n + 1)
                        move(n)
                        if n:
                            norm(n - 1)
                    norm(W - 1)


F16 = mybir.dt.float16


class Stack:

    def __init__(self, dh, q_parts, k_parts, rows, max_rows, m0, m_row, m_chunk, q_fill=1.0):
        self.dh, self.q_parts, self.k_parts, self.rows, self.max_rows = dh, q_parts, k_parts, rows, max_rows
        self.m0, self.m_row, self.m_chunk, self.q_fill = m0, m_row, m_chunk, q_fill


STACK_32 = Stack(32, [(0, 0, "h"), (0, 32, "h"), (0, 64, "l")], [(0, 0, "h"), (0, 32, "l"), (0, 64, "h")], [104], 102, 96, 102, 0)
STACK_16 = Stack(16, [(0, 0, "h"), (0, 16, "h"), (0, 32, "l"), (0, 48, "l")], [(0, 0, "h"), (0, 16, "l"), (0, 32, "h"), (0, 48, "l")],
                 [68], 66, 64, 66, 0, q_fill=0.0)
STACK_64 = Stack(64, [(0, 0, "h"), (0, 64, "h"), (1, 0, "l")], [(0, 0, "h"), (0, 64, "l"), (1, 0, "h")], [128, 66], 128, 64, 64, 1)
HU = 4
QC = 512


class First:

    def __init__(self, tile, n, step, key, w, chunk, masked):
        self.tile, self.n, self.step, self.key, self.w, self.chunk, self.masked = tile, n, step, key, w, chunk, masked


class Second:

    def __init__(self, group, key, vb, off, masked, first, last):
        self.group, self.key, self.vb, self.off, self.masked, self.first, self.last = group, key, vb, off, masked, first, last


class Plan:
    def __init__(self, firsts, seconds, key_rows, n_keys, merge):
        self.firsts, self.seconds, self.key_rows, self.n_keys, self.merge = firsts, seconds, key_rows, n_keys, merge


def causal_plan():
    gq = QC // P
    firsts = []
    for i in range(NT):
        b, j = i // TB, i % TB
        for c in range(j // gq + 1):
            w = min(QC, (j + 1) * P - c * QC)
            firsts.append(First(i, 1, w, b * T + c * QC, w, c, c == j // gq))
    seconds = [Second(b * (T // QC) + c, b * T + j * P, b * TB + j, max(0, j * P - c * QC), j >= c * gq, j == 0, j == (c + 1) * gq - 1)
               for b in range(B) for c in range(T // QC) for j in range((c + 1) * gq)]
    return Plan(firsts, seconds, P, N, True)


def context_plan():
    gq = QC // P
    firsts = [First(g * gq, gq, P, g // (T // QC) * M, M, 0, False) for g in range(N // QC)]
    seconds = [Second(g, g // (T // QC) * M, g // (T // QC), 0, False, True, True) for g in range(N // QC)]
    return Plan(firsts, seconds, M, B * M, False)


def stacked_attention(k, name, plan, H, stack, q, kk, v_all, o_all, kv_of=1, q_pos=None, k_pos=None, pool_share=3):
    nc = k.nc
    dh = stack.dh
    V1 = dh + 1
    VW = V1 + dh
    wide = VW <= P
    OM = VW if wide else V1
    C = len(stack.rows)
    R = stack.m_row
    GQ = QC // P
    KR = plan.key_rows
    firsts, seconds = plan.firsts, plan.seconds
    NA = len(firsts) + 1
    NB = len(seconds)
    M = HU * NB
    OG = N // QC
    NS = 3 if NB % 3 == 0 else 2
    AHEAD = 2
    SLOTS = 8
    LAG = 3 if plan.merge or C > 1 else 2
    after_turn = ["norm", "copy"] if plan.merge else ["copy", "norm"]
    norm_at = LAG + 3 if plan.merge else LAG + 2
    last_of = [n for n in range(NB) if seconds[n].last]
    n_ld = len(stack.q_parts) + len(stack.k_parts) + (2 if q_pos is not None else 0)
    assert NB % 4 == 0 and M % NS == 0 and M % SLOTS == 0 and (HU * NA) % 2 == 0 and H % HU == 0 and kv_of in (1, HU)
    spread = NB - max(1, NB // 8)
    beside = [[a for a in range(NA) if n == (NB - 1 if a == NA - 1 else a * spread // (NA - 1))] for n in range(NB)]
    by_pool = [n % 4 >= 4 - pool_share for n in range(NB)]
    nth = [sum(1 for i in range(n) if by_pool[i] == by_pool[n]) for n in range(NB)]
    NP, NV = sum(by_pool), NB - sum(by_pool)
    with Phase(k, name) as ph:
        qs = ph.sb("qs", [P, HU, C, N], F16)
        ks = ph.sb("ks", [P, HU, C, plan.n_keys], F16)
        vs = ph.sb("vs", [KR, 2, v_all.shape[1], VW], F16)
        probs = ph.sb("probs", [KR, SLOTS, QC])
        p_hi, p_lo = ph.sb("p_hi", [KR, SLOTS, QC], F16), ph.sb("p_lo", [KR, SLOTS, QC], F16)
        nmax = ph.sb("nmax", [P, 2, 2, NT])
        mh, ml = ph.sb("mh", [NT, 2, P], F16), ph.sb("ml", [NT, 2, P], F16)
        o_st = ph.sb("o_st", [OM, 2, QC])
        both = ph.sb("both", [P, 2, GQ, dh]) if wide else None
        rinv = ph.sb("rinv", [P, 2, GQ])
        ph.sems_of("filled a_done maxed merged split b_done exps lo_dve lo_pool values o_copied o_turned o_normed "
                   "v_hi v_ready passed loading turning lower summed recips")
        qk_ld = [ph.sem(f"qk_ld{p}") for p in range(HU)]
        m_ld = [ph.sem(f"m_ld{p}") for p in range(HU)]
        SA = [k.ps[:, i, :] for i in range(2)]
        SB = [k.ps[0:KR, 2 + i, :] for i in range(NS)]
        O = [k.ps[0:OM, 5 + i, :] for i in range(2)]
        OR = k.ps[:, 7, 0:GQ * OM].rearrange("p (t d) -> p t d", d=OM)
        s = ph.s

        def turns(eng):
            if H > HU:
                with eng.Fori(0, H // HU - 1) as t:
                    yield t, True
            yield H // HU - 1, False

        def at(t, p):
            return t * HU + p, t + p // HU, p % HU

        def lower_part(eng, sem, t, m):
            p, n = divmod(m, NB)
            h = t * HU + p
            w = QC - seconds[n].off
            eng.wait_ge(s["exps"], NB * h + n + 1 + NS)
            eng.tensor_tensor(p_lo[:, m % SLOTS, 0:w], probs[:, m % SLOTS, 0:w], p_hi[:, m % SLOTS, 0:w], ALU.subtract).then_inc(sem, 1)

        with nc.Block() as block:

            @block.sync
            def _(sp):

                def load(h, t, p):
                    sp.wait_ge(s["values"], NB * h + NB)
                    sp.sem_inc(s["loading"], 1)
                    kv = h if kv_of == 1 else t
                    for dst, parts, src, head in ((qs, stack.q_parts, q, h), (ks, stack.k_parts, kk, kv)):
                        for c, r0, part in parts:
                            of_heads = src[part].rearrange("(h d) n -> h d n", d=dh)
                            sp.dma_start(dst[r0:r0 + dh, p, c, :], of_heads[ds(head, 1)].rearrange("h d n -> (h d) n")).then_inc(qk_ld[p], 16)
                    if q_pos is not None:
                        sp.dma_start(qs[99:102, p, 0, :], q_pos[ds(h, 1)].rearrange("h r n -> (h r) n")).then_inc(qk_ld[p], 16)
                        sp.dma_start(ks[96:99, p, 0, :], k_pos[ds(h, 1)].rearrange("h r n -> (h r) n")).then_inc(qk_ld[p], 16)

                def maximum_rows(h, t, p):
                    sp.wait_ge(s["maxed"], NA * h + NA + 2)
                    for i, m in enumerate((mh, ml)):
                        sp.dma_start(qs[R + i:R + i + 1, p, stack.m_chunk, :], m[:, p % 2, :]).then_inc(m_ld[p], 16)

                sp.wait_ge(s["filled"], 2 * HU)
                for h in range(3):
                    load(h, 0, h)
                maximum_rows(0, 0, 0)
                maximum_rows(1, 0, 1)
                for t, more in turns(sp):
                    for p in range(HU):
                        if more or p + 3 < HU:
                            load(*at(t, p + 3))
                        if more or p + 2 < HU:
                            maximum_rows(*at(t, p + 2))

            @block.gpsimd
            def _(pool):
                for p in range(HU):
                    pool.memset(qs[stack.m0:R + 2, p, stack.m_chunk, :], stack.q_fill).then_inc(s["filled"], 1)
                    pool.memset(ks[stack.m0:R + 2, p, stack.m_chunk, :], 1.0).then_inc(s["filled"], 1)
                pool.wait_ge(s["filled"], 2 * HU)
                pool.memset(vs[:], 1.0).then_inc(s["filled"], 1)
                pool.wait_ge(s["filled"], 2 * HU + 1)

                def head_values(h, t, p):
                    src = v_all[:, :, ds((h if kv_of == 1 else t) * dh, dh)]
                    pool.wait_ge(s["values"], NB * h + 3 * NB)
                    pool.sem_inc(s["passed"], 1)
                    pool.tensor_copy(vs[:, p % 2, :, 0:dh], src).then_inc(s["v_hi"], 1)
                    pool.wait_ge(s["v_hi"], h + 1)
                    pool.sem_inc(s["passed"], 1)
                    pool.tensor_tensor(vs[:, p % 2, :, V1:VW], src, vs[:, p % 2, :, 0:dh], ALU.subtract).then_inc(s["v_ready"], 1)

                head_values(0, 0, 0)
                for t, more in turns(pool):
                    for m in range(M):
                        p, n = divmod(m, NB)
                        if by_pool[n]:
                            lower_part(pool, s["lo_pool"], t, m)
                        if n == min(LAG + 1, NB - 1) and (more or p + 1 < HU):
                            head_values(*at(t, p + 1))

            @block.tensor
            def _(pe):

                def first(h, t, p, i):
                    sa = SA[(p * NA + i) % 2]
                    if i == 0:
                        pe.wait_ge(qk_ld[p], 16 * n_ld * t + 16 * n_ld)
                    if i < NA - 1:
                        pe.wait_ge(s["maxed"], NA * h + i + 1)
                        f = firsts[i]
                        for j in range(f.n):
                            at_, tile = j * f.step, f.tile + j
                            ins = pe.matmul(sa[:, at_:at_ + f.w], qs[0:stack.max_rows, p, 0, tile * P:(tile + 1) * P],
                                            ks[0:stack.max_rows, p, 0, f.key:f.key + f.w], start=True, stop=not f.masked)
                        if f.masked:
                            ins = pe.matmul(sa[:, f.w - P:f.w], k.ident_b[:], k.mask[:], start=False, stop=True)
                    else:
                        if plan.merge:
                            pe.wait_ge(s["merged"], h + 1)
                        else:
                            pe.wait_ge(s["maxed"], NA * h + NA + 1)
                        ins = pe.transpose(sa[0:NT, 0:P], nmax[:, p % 2, 0, :], k.ident[:])
                    ins.then_inc(s["a_done"], 1)

                def scores(t, m):
                    h, t, p = at(t, m // NB)
                    n = m % NB
                    u = seconds[n]
                    bank = SB[m % NS]
                    if n == 0:
                        pe.wait_ge(m_ld[p], 32 * t + 32)
                    pe.wait_ge(s["exps"], NB * h + n + 1)
                    w = QC - u.off
                    q0 = u.group * QC + u.off
                    for d, r in enumerate(stack.rows):
                        ins = pe.matmul(bank[:, 0:w], ks[0:r, p, d, u.key:u.key + KR], qs[0:r, p, d, q0:q0 + w], start=d == 0,
                                        stop=d == C - 1 and not u.masked)
                    if u.masked:
                        ins = pe.matmul(bank[:, 0:P], k.ident_b[:], k.mask_t[:], start=False, stop=True)
                    ins.then_inc(s["b_done"], 1)

                def values(t, m):
                    p, n = divmod(m, NB)
                    h = t * HU + p
                    u = seconds[n]
                    o, w = O[u.group % 2][:, u.off:QC], QC - u.off
                    v = vs[:, p % 2, u.vb, :]
                    hi, lo = p_hi[:, m % SLOTS, 0:w], p_lo[:, m % SLOTS, 0:w]
                    if n == 0:
                        pe.wait_ge(s["v_ready"], h + 1)
                    pe.wait_ge(s["exps"], NB * h + n + 1 + NS)
                    if u.first:
                        pe.wait_ge(s["o_copied"], OG * h + u.group + 1)
                    pe.matmul(o, v[:, 0:OM], hi, start=u.first, stop=False)
                    if not wide:
                        pe.matmul(o[0:dh, :], v[:, V1:VW], hi, start=False, stop=False)
                    if by_pool[n]:
                        pe.wait_ge(s["lo_pool"], NP * h + nth[n] + 1)
                    else:
                        pe.wait_ge(s["lo_dve"], NV * h + nth[n] + 1)
                    pe.matmul(o, v[:, 0:OM], lo, start=False, stop=u.last).then_inc(s["values"], 1)

                def turn(h, g):
                    pe.wait_ge(s["o_copied"], OG * h + g + 3)
                    pe.wait_ge(s["o_normed"], OG * h + g + 1)
                    pe.sem_inc(s["turning"], 1)
                    for i in range(GQ):
                        ins = pe.transpose(OR[:, i, :], o_st[:, g % 2, i * P:(i + 1) * P], k.ident[0:OM, 0:OM])
                    ins.then_inc(s["o_turned"], 1)

                pe.sem_inc(s["values"], 4 * NB)
                for h in range(2):
                    for i in range(NA):
                        first(h, 0, h, i)
                for m in range(AHEAD):
                    scores(0, m)
                for t, more in turns(pe):
                    for m in range(M + LAG + 2):
                        p, n = divmod(m, NB)
                        if m < M and (more or m + AHEAD < M):
                            scores(t, m + AHEAD)
                        if 0 <= m - LAG < M:
                            values(t, m - LAG)
                        g = m - LAG - 2
                        if 0 <= g < M and g % NB in last_of:
                            turn(t * HU + g // NB, last_of.index(g % NB))
                        if m < M and (more or p + 2 < HU):
                            for i in beside[n]:
                                first(*at(t, p + 2), i)

            @block.scalar
            def _(act):
                act.sem_inc(s["exps"], NS)
                for t, more in turns(act):
                    for m in range(M):
                        p, n = divmod(m, NB)
                        h = t * HU + p
                        w = QC - seconds[n].off
                        act.wait_ge(s["b_done"], NB * h + n + 1)
                        act.wait_ge(s["values"], NB * h + 4 * NB + n + 1 - SLOTS)
                        act.activation(p_hi[:, m % SLOTS, 0:w], SB[m % NS][:, 0:w], ACT.Exp)
                        act.activation(probs[:, m % SLOTS, 0:w], SB[m % NS][:, 0:w], ACT.Exp).then_inc(s["exps"], 1)

            @block.vector
            def _(dve):

                def first(h, t, p, i):
                    sa = SA[(p * NA + i) % 2]
                    dve.wait_ge(s["a_done"], NA * h + i + 1)
                    if i < NA - 1:
                        f = firsts[i]
                        src = sa[:, 0:f.w] if f.n == 1 else sa[:, 0:f.n * f.step].rearrange("p (t m) -> p t m", m=f.step)[:, :, 0:f.w]
                        dve.tensor_reduce(nmax[:, p % 2, f.chunk, f.tile:f.tile + f.n], src, AX.X, ALU.max, negate=True).then_inc(s["maxed"], 1)
                        if i == NA - 2 and plan.merge:
                            dve.wait_ge(s["maxed"], NA * h + i + 3)
                            both = [nmax[:, p % 2, c, :].rearrange("p (b t) -> p b t", t=TB)[:, :, GQ:TB] for c in range(2)]
                            dve.tensor_tensor(both[0], both[0], both[1], ALU.min).then_inc(s["merged"], 1)
                    else:
                        dve.tensor_copy(mh[:, p % 2, :], sa[0:NT, 0:P]).then_inc(s["split"], 1)
                        dve.wait_ge(s["split"], h + 1)
                        dve.tensor_tensor(ml[:, p % 2, :], sa[0:NT, 0:P], mh[:, p % 2, :], ALU.subtract).then_inc(s["maxed"], 1)

                def copy(h, g):
                    dve.wait_ge(s["values"], NB * h + 4 * NB + last_of[g] + 1)
                    dve.tensor_copy(o_st[:, g % 2, :], O[g % 2]).then_inc(s["o_copied"], 1)

                def norm(h, g):
                    dve.wait_ge(s["o_turned"], OG * h + g + 1)
                    rows = OR[:, :, 0:dh]
                    if wide:
                        dve.tensor_copy(both[:, 0], OR[:, :, V1:VW]).then_inc(s["lower"], 1)
                    dve.reciprocal(rinv[:, g % 2, :], OR[:, :, dh]).then_inc(s["recips"], 1)
                    if wide:
                        dve.wait_ge(s["lower"], OG * h + g + 1)
                        dve.tensor_tensor(both[:, 1], rows, both[:, 0], ALU.add).then_inc(s["summed"], 1)
                        dve.wait_ge(s["summed"], OG * h + g + 1)
                        rows = both[:, 1]
                    dve.wait_ge(s["recips"], OG * h + g + 1)
                    dve.tensor_tensor(o_all[:, g * GQ:(g + 1) * GQ, ds(h * dh, dh)], rows,
                                      rinv[:, g % 2, :, None].to_broadcast([P, GQ, dh]), ALU.mult).then_inc(s["o_normed"], 1)

                dve.sem_inc(s["maxed"], 2)
                dve.sem_inc(s["o_copied"], 2)
                dve.sem_inc(s["o_normed"], 1)
                for h in range(2):
                    for i in range(NA):
                        first(h, 0, h, i)
                for t, more in turns(dve):
                    for m in range(M + LAG + 3):
                        p, n = divmod(m, NB)
                        if m < M and not by_pool[n]:
                            lower_part(dve, s["lo_dve"], t, m)
                        for what in after_turn:
                            step, back = (norm, norm_at) if what == "norm" else (copy, LAG + 1)
                            if 0 <= m - back < M and (m - back) % NB in last_of:
                                step(t * HU + (m - back) // NB, last_of.index((m - back) % NB))
                        if m < M and (more or p + 2 < HU):
                            for i in beside[n]:
                                first(*at(t, p + 2), i)


def project_out(k, name, o_all, F, wo, x_in, x_out, xt_out, bias=None, pre=None, gate=None):
    nc = k.nc
    FC = F // P
    with Phase(k, name) as ph:
        tail_bias = ph.sb("bias", [P, D]) if bias is not None else None
        own = [ph.sb("ln_w", [P, D]), ph.sb("ln_b", [P, D])] if pre else None
        tail = Tail(ph, x_in, x_out, xt_out, tail_bias, own)
        w = ph.sb("w", [P, FC, D]) if wo is not None else None
        gated = ph.sb("gated", [P, 2, GT, F]) if gate is not None else None
        o_cols = ph.sb("o_cols", [P, 2, FC, GN]) if wo is not None else None
        ph.sems_of("w_ld o_ready o_turned o_moved")
        n_ld = 16 * ((wo is not None) + (bias is not None) + 2 * bool(pre))
        TP = [k.ps[:, 0, :], k.ps[:, 1, :]]
        if wo is not None:
            Y = [k.ps[:, b:b + 2, :].rearrange("p b (t d) -> p (b t) d", d=D) for b in (2, 6)]
            tail.y_of = lambda g: Y[g % 2]
        else:
            tail.y_of = lambda g: o_all[:, g * GT:(g + 1) * GT, :]
            tail.own_y = False
        with nc.Block() as block:

            @block.sync
            def _(sp):
                tail.load(sp, 0)
                if wo is not None:
                    sp.dma_start(w[:], weight_rows(wo)).then_inc(ph.s["w_ld"], 16)
                if bias is not None:
                    sp.dma_start(tail_bias[:], bias).then_inc(ph.s["w_ld"], 16)
                if pre:
                    sp.dma_start(own[0][:], pre[0]).then_inc(ph.s["w_ld"], 16)
                    sp.dma_start(own[1][:], pre[1]).then_inc(ph.s["w_ld"], 16)
                for g in range(1, NG):
                    tail.load(sp, g)

            @block.gpsimd
            def _(pool):
                for g in range(NG):
                    if gate is not None:
                        after(pool, ph.s["o_turned"], max(g - 1, 0) * FC)
                        tiles = slice(g * GT, (g + 1) * GT)
                        pool.tensor_tensor(gated[:, g % 2, :, :], o_all[:, tiles, :], gate[:, tiles, :], ALU.mult).then_inc(ph.s["o_ready"], 1)
                    if g:
                        tail.store(pool, g - 1)
                tail.store(pool, NG - 1)
                tail.finish(pool)

            @block.tensor
            def _(pe):
                for g in range(NG):
                    if wo is not None:
                        if gate is not None:
                            pe.wait_ge(ph.s["o_ready"], g + 1)
                        for c in range(FC):
                            after(pe, ph.s["o_moved"], max(g * FC + c - 1, 0))
                            for t in range(GT):
                                rows = gated[:, g % 2, t, :] if gate is not None else o_all[:, g * GT + t, :]
                                ins = pe.transpose(TP[(g * FC + c) % 2][:, t * P:(t + 1) * P], rows[:, c * P:(c + 1) * P], k.ident[:])
                            ins.then_inc(ph.s["o_turned"], 1)
                        if g == 0:
                            pe.wait_ge(ph.s["w_ld"], n_ld)
                        pe.wait_ge(ph.s["o_moved"], g * FC + FC)
                        after(pe, ph.s["r_done"], max(g - 1, 0))
                        for t in range(GT):
                            for c in range(FC):
                                ins = pe.matmul(Y[g % 2][:, t, :], o_cols[:, g % 2, c, t * P:(t + 1) * P], w[:, c, :],
                                                start=c == 0, stop=c == FC - 1)
                        ins.then_inc(ph.s["y_ready"], 1)
                    if g:
                        tail.tensor(pe, g - 1)
                tail.tensor(pe, NG - 1)

            @block.scalar
            def _(act):
                for g in range(NG):
                    if wo is not None:
                        after(act, ph.s["y_ready"], max(g - 1, 0))
                        for c in range(FC):
                            act.wait_ge(ph.s["o_turned"], g * FC + c + 1)
                            act.activation(o_cols[:, g % 2, c, :], TP[(g * FC + c) % 2][:], ACT.Copy).then_inc(ph.s["o_moved"], 1)
                    if g:
                        tail.scalar(act, g - 1)
                tail.scalar(act, NG - 1)

            @block.vector
            def _(dve):
                if n_ld:
                    dve.wait_ge(ph.s["w_ld"], n_ld)
                for g in range(NG):
                    tail.vector(dve, g)


def add_and_norm(k, name, y, x_in, x_out, xt_out):
    nc = k.nc
    with Phase(k, name) as ph:
        xin, r, xn = (ph.sb(n, [P, 2, GT, D]) for n in ("xin", "r", "xn"))
        stats, mv = ph.sb("stats", [P, 2, GT, 6]), ph.sb("mv", [P, 2, GT, 2])
        ve, sd, rs = (ph.sb(n, [P, 2, GT]) for n in ("ve", "sd", "rs"))
        gap = ph.sb("gap", [P, 1])
        xts = ph.sb("xts", [P, 2, DC, GN])
        TP = [k.ps[:, 4:6, :], k.ps[:, 6:8, :]]
        ph.sems_of("chain r_done ve_ready sd_ready xn_ready xn_turned xts_ready x_st xt_st")
        xin_ld = [ph.sem("xin_ld0"), ph.sem("xin_ld1")]
        with nc.Block() as block:

            @block.sync
            def _(sp):
                for g in range(NG):
                    after(sp, ph.s["r_done"], max(g - 1, 0))
                    sp.dma_start(xin[:, g % 2], x_in[g * GN:(g + 1) * GN, :].rearrange("(t p) d -> p t d", p=P)).then_inc(xin_ld[g % 2], 16)

            @block.vector
            def _(dve):
                ch = Count(dve, ph.s["chain"], 0, 0)

                def moments(g):
                    i = g % 2
                    dve.wait_ge(xin_ld[i], 16 * (g // 2) + 16)
                    after(dve, ph.s["xn_ready"], max(g - 1, 0))
                    dve.tensor_tensor(r[:, i], y[:, g * GT:(g + 1) * GT, :], xin[:, i], ALU.add).then_inc(ph.s["r_done"], 1)
                    dve.wait_ge(ph.s["r_done"], g + 1)
                    for t in range(GT):
                        ch.step(dve.bn_stats(stats[:, i, t, :], r[:, i, t, :]))
                    ch.wait()
                    dve.memset(gap[:], 0.0)
                    for t in range(GT):
                        ch.step(dve.bn_aggr(mv[:, i, t, :], stats[:, i, t, :]))
                    ch.wait()
                    dve.tensor_scalar(ve[:, i, :], mv[:, i, :, 1], EPS, None, ALU.add).then_inc(ph.s["ve_ready"], 1)

                def scaled(g):
                    i = g % 2
                    dve.wait_ge(ph.s["sd_ready"], g + 1)
                    ch.step(dve.reciprocal(rs[:, i, :], sd[:, i, :]))
                    ch.wait()
                    if g >= 2:
                        dve.wait_ge(ph.s["x_st"], 16 * (g - 1))
                        if xt_out is not None:
                            dve.wait_ge(ph.s["xn_turned"], g - 1)
                    for t in range(GT):
                        ins = dve.tensor_scalar(xn[:, i, t, :], r[:, i, t, :], mv[:, i, t, 0:1], rs[:, i, t:t + 1], ALU.subtract, ALU.mult)
                    ins.then_inc(ph.s["xn_ready"], 1)

                moments(0)
                for g in range(NG):
                    if g + 1 < NG:
                        moments(g + 1)
                    scaled(g)

            @block.scalar
            def _(act):
                for g in range(NG + 1):
                    if g < NG:
                        act.wait_ge(ph.s["ve_ready"], g + 1)
                        act.activation(sd[:, g % 2, :], ve[:, g % 2, :], ACT.Sqrt).then_inc(ph.s["sd_ready"], 1)
                    if g and xt_out is not None:
                        act.wait_ge(ph.s["xn_turned"], g)
                        if g >= 3:
                            act.wait_ge(ph.s["xt_st"], 16 * (g - 2))
                        act.activation(xts[:, (g - 1) % 2], TP[(g - 1) % 2], ACT.Copy).then_inc(ph.s["xts_ready"], 1)

            @block.tensor
            def _(pe):
                if xt_out is None:
                    return
                for g in range(NG):
                    pe.wait_ge(ph.s["xn_ready"], g + 1)
                    after(pe, ph.s["xts_ready"], max(g - 1, 0))
                    for c in range(DC):
                        for t in range(GT):
                            ins = pe.transpose(TP[g % 2][:, c, t * P:(t + 1) * P], xn[:, g % 2, t, c * P:(c + 1) * P], k.ident[:])
                    ins.then_inc(ph.s["xn_turned"], 1)

            @block.gpsimd
            def _(pool):
                for g in range(NG):
                    pool.wait_ge(ph.s["xn_ready"], g + 1)
                    after(pool, ph.s["x_st"], 16 * g)
                    pool.dma_start(x_out[g * GN:(g + 1) * GN, :].rearrange("(t p) d -> p t d", p=P), xn[:, g % 2]).then_inc(ph.s["x_st"], 16)
                    if xt_out is not None:
                        pool.wait_ge(ph.s["xts_ready"], g + 1)
                        after(pool, ph.s["xt_st"], 16 * g)
                        pool.dma_start(xt_out[:, g * GN:(g + 1) * GN].rearrange("(c p) t -> p c t", p=P), xts[:, g % 2]).then_inc(ph.s["xt_st"], 16)
                pool.wait_ge(ph.s["x_st"], 16 * NG)
                if xt_out is not None:
                    pool.wait_ge(ph.s["xt_st"], 16 * NG)


def l0_self_attention(k, x_in, x_out, xt_out):
    nc, a = k.nc, k.a
    H, E = 16, 512
    DH = E // H
    EC = E // P
    HPC = P // DH
    norm_columns(k, "l0n", x_in, k.xnt, a["L0_attn_in_ln_w"], a["L0_attn_in_ln_b"])
    qt, kt = halves_of(k, "l0_q", E), halves_of(k, "l0_k", E)
    q_pos, k_pos = k.dram("l0_q_pos", [H, 3, N], F16), k.dram("l0_k_pos", [H, 3, N], F16)
    with ExitStack() as keep:
        v_all = keep.enter_context(nc.sbuf_tensor("l0_v_all", [P, NT, E], F32))
        o_all = keep.enter_context(nc.sbuf_tensor("l0_o_all", [P, NT, E], F32))
        gate = keep.enter_context(nc.sbuf_tensor("l0_gate", [P, NT, E], F32))
        with Phase(k, "l0p") as ph:
            w = ph.sb("w", [P, DC, 4 * E + H])
            bc = ph.sb("bc", [P, 2 * EC])
            by = ph.sb("by", [H, 1])
            brow = ph.sb("brow", [P, 2 * E])
            hf = ph.sb("hf", [P, 2, EC])
            sg = ph.sb("sg", [P, 6, EC])
            qb, kb = ph.sb("qb", [P, EC]), ph.sb("kb", [P, EC])
            xs = ph.sb("xs", [P, DC, T])
            st = ph.sb("st", [P, 2, T])
            kraw = ph.sb("kraw", [P, T])
            gap = ph.sb("gap", [P, 1])
            vtmp = ph.sb("vtmp", [P, E])
            sig = ph.sb("sig", [H, T])
            ones = ph.sb("ones", [H, T])
            pos = ph.sb("pos", [H, T])
            rest = ph.sb("rest", [H, 2, T])
            pp, npp = ph.sb("pp", [H, 3, T], F16), ph.sb("npp", [H, 3, T], F16)
            his, los = ph.sb("his", [P, 2, T], F16), ph.sb("los", [P, 2, T], F16)
            ph.sems_of("w_ld x_ld prep pe_done act_q kraw_ready smear k_ready st_st0 st_st1 sig_ready ones_ready "
                       "pos_ready pos_st v_ready gate_sum gate_ready act_prep q_hi lo_done pos_parts k_hi storing")
            st_st = [ph.s["st_st0"], ph.s["st_st1"]]
            PA = [k.ps[:, 0:2, :].rearrange("p b c -> p (b c)"), k.ps[:, 2:4, :].rearrange("p b c -> p (b c)")]
            PY = k.ps[0:H, 4:6, :].rearrange("p b c -> p (b c)")
            PV, PG = k.ps[:, 6, :], k.ps[:, 7, :]
            CH = 2 * EC
            with nc.Block() as block:

                @block.sync
                def _(sp):
                    for dst, src in ((w[:], weight_rows(a["L0_attn_W_in"])), (bc[:], a["L0_attn_b_col"]), (by[:], a["L0_attn_b_y"]),
                                     (brow[:], a["L0_attn_b_row"]), (hf[:], a["L0_attn_by_head"])):
                        sp.dma_start(dst, src).then_inc(ph.s["w_ld"], 16)
                    with sp.Fori(0, B) as b:
                        sp.wait_ge(ph.s["pe_done"], b * (CH + 1 + 2 * TB))
                        sp.dma_start(xs[:], k.xnt[:, ds(b * T, T)].rearrange("(c p) t -> p c t", p=P)).then_inc(ph.s["x_ld"], 16)
                        for c in range(CH):
                            dst = qt if c < EC else kt
                            sp.wait_ge(ph.s["lo_done"], b * CH + c + 1)
                            sp.sem_inc(ph.s["storing"], 1)
                            for part, stage in (("h", his), ("l", los)):
                                e = c % EC
                                sp.dma_start(dst[part][e * P:(e + 1) * P, ds(b * T, T)], stage[:, c % 2, :]).then_inc(st_st[c % 2], 16)

                @block.gpsimd
                def _(pool):
                    pool.memset(ones[:], 1.0).then_inc(ph.s["ones_ready"], 1)
                    pool.wait_ge(ph.s["ones_ready"], 1)
                    with pool.Fori(0, B) as b:
                        pool.wait_ge(ph.s["pos_parts"], 6 * b + 6)
                        pool.dma_start(k_pos[:, :, ds(b * T, T)], pp[:]).then_inc(ph.s["pos_st"], 16)
                        pool.dma_start(q_pos[:, :, ds(b * T, T)], npp[:]).then_inc(ph.s["pos_st"], 16)
                    pool.wait_ge(ph.s["pos_st"], 16 * 2 * B)
                    for s in st_st:
                        pool.wait_ge(s, 16 * 2 * B * EC)

                @block.tensor
                def _(pe):
                    pe.wait_ge(ph.s["w_ld"], 80)
                    with pe.Fori(0, B) as b:
                        pe.wait_ge(ph.s["x_ld"], 16 * b + 16)
                        pe.wait_ge(ph.s["sig_ready"], b)
                        for half in range(2):
                            for c in range(DC):
                                ins = pe.matmul(PY[:, half * 512:(half + 1) * 512], w[:, c, 4 * E:4 * E + H],
                                                xs[:, c, half * 512:(half + 1) * 512], start=c == 0, stop=c == DC - 1)
                        ins.then_inc(ph.s["pe_done"], 1)
                        for c in range(CH):
                            if c < 2:
                                pe.wait_ge(ph.s["kraw_ready"], b * EC)
                            elif c < EC + 2:
                                pe.wait_ge(ph.s["act_q"], b * EC + c - 1)
                            else:
                                pe.wait_ge(ph.s["kraw_ready"], b * EC + c - EC - 1)
                            for half in range(2):
                                for d in range(DC):
                                    ins = pe.matmul(PA[c % 2][:, half * 512:(half + 1) * 512], w[:, d, c * P:(c + 1) * P],
                                                    xs[:, d, half * 512:(half + 1) * 512], start=d == 0, stop=d == DC - 1)
                            ins.then_inc(ph.s["pe_done"], 1)
                        for j in range(TB):
                            pe.wait_ge(ph.s["v_ready"], b * TB + j)
                            for d in range(DC):
                                ins = pe.matmul(PV, xs[:, d, j * P:(j + 1) * P], w[:, d, 2 * E:3 * E], start=d == 0, stop=d == DC - 1)
                            ins.then_inc(ph.s["pe_done"], 1)
                            pe.wait_ge(ph.s["gate_sum"], b * TB + j)
                            for d in range(DC):
                                ins = pe.matmul(PG, xs[:, d, j * P:(j + 1) * P], w[:, d, 3 * E:4 * E], start=d == 0, stop=d == DC - 1)
                            ins.then_inc(ph.s["pe_done"], 1)

                @block.scalar
                def _(act):
                    act.wait_ge(ph.s["w_ld"], 80)
                    act.activation(sg[:, 0, :], hf[:, 0, :], ACT.Sigmoid).then_inc(ph.s["act_prep"], 1)
                    act.activation(sg[:, 1, :], hf[:, 1, :], ACT.Exp, scale=-1.0).then_inc(ph.s["act_prep"], 1)
                    act.wait_ge(ph.s["prep"], 5)
                    with act.Fori(0, B) as b:
                        done = b * (CH + 1 + 2 * TB)
                        act.wait_ge(ph.s["pe_done"], done + 1)
                        act.wait_ge(ph.s["pos_ready"], b)
                        act.activation(sig[:], PY, ACT.Sigmoid, bias=by[:, 0:1]).then_inc(ph.s["sig_ready"], 1)
                        for c in range(CH):
                            act.wait_ge(ph.s["pe_done"], done + c + 2)
                            e = c % EC
                            if c < EC:
                                act.wait_ge(st_st[c % 2], 16 * 2 * (b * EC + c // 2))
                                act.activation(his[:, c % 2, :], PA[c % 2], ACT.Identity, scale=sg[:, 2, e:e + 1], bias=qb[:, e:e + 1])\
                                    .then_inc(ph.s["q_hi"], 1)
                                act.activation(st[:, c % 2, :], PA[c % 2], ACT.Identity, scale=sg[:, 2, e:e + 1], bias=qb[:, e:e + 1])\
                                    .then_inc(ph.s["act_q"], 1)
                            else:
                                act.wait_ge(ph.s["k_ready"], b * EC + e)
                                act.activation(kraw[:], PA[c % 2], ACT.Identity, scale=sg[:, 1, e:e + 1], bias=kb[:, e:e + 1])\
                                    .then_inc(ph.s["kraw_ready"], 1)
                                act.wait_ge(ph.s["k_ready"], b * EC + e + 1)
                                act.wait_ge(st_st[c % 2], 16 * 2 * (b * EC + c // 2))
                                act.activation(his[:, c % 2, :], st[:, c % 2, :], ACT.Copy).then_inc(ph.s["k_hi"], 1)
                        for j in range(TB):
                            act.wait_ge(ph.s["gate_sum"], b * TB + j + 1)
                            act.activation(gate[:, ds(b * TB + j, 1), :], vtmp[:, None, :], ACT.Silu).then_inc(ph.s["gate_ready"], 1)

                @block.vector
                def _(dve):
                    dve.wait_ge(ph.s["act_prep"], 2)
                    dve.tensor_scalar(sg[:, 2, :], sg[:, 1, :], DH ** -0.5, None, ALU.mult).then_inc(ph.s["prep"], 1)
                    dve.tensor_scalar(sg[:, 3, :], sg[:, 0, :], -1.0, 1.0, ALU.mult, ALU.add).then_inc(ph.s["prep"], 1)
                    dve.tensor_tensor(kb[:], bc[:, EC:2 * EC], sg[:, 1, :], ALU.mult).then_inc(ph.s["prep"], 1)
                    dve.wait_ge(ph.s["prep"], 3)
                    dve.tensor_tensor(qb[:], bc[:, 0:EC], sg[:, 2, :], ALU.mult).then_inc(ph.s["prep"], 1)
                    dve.wait_ge(ph.s["ones_ready"], 1)
                    dve.tensor_copy(sg[:, 4, :], sg[:, 3, :]).then_inc(ph.s["prep"], 1)
                    with dve.Fori(0, B) as b:
                        done = b * (CH + 1 + 2 * TB)
                        dve.wait_ge(ph.s["sig_ready"], b + 1)
                        dve.tensor_tensor_scan(pos[:], ones[:], sig[:], 0.0, ALU.mult, ALU.add).then_inc(ph.s["pos_ready"], 1)
                        dve.wait_ge(ph.s["pos_ready"], b + 1)
                        dve.wait_ge(ph.s["pos_st"], 32 * b)
                        parts = Count(dve, ph.s["pos_parts"], 6, b)
                        left = pos[:]
                        for i in range(3):
                            parts.step(dve.tensor_copy(pp[:, i, :], left))
                            if i < 2:
                                parts.wait()
                                parts.step(dve.tensor_tensor(rest[:, i, :], left, pp[:, i, :], ALU.subtract))
                                left = rest[:, i, :]
                            parts.wait()
                        dve.memset(gap[:], 0.0)
                        parts.step(dve.tensor_scalar(npp[:], pp[:], -1.0, None, ALU.mult))
                        parts.close()
                        for c in range(EC):
                            dve.wait_ge(ph.s["act_q"], b * EC + c + 1)
                            dve.wait_ge(ph.s["q_hi"], b * EC + c + 1)
                            dve.tensor_tensor(los[:, c % 2, :], st[:, c % 2, :], his[:, c % 2, :], ALU.subtract).then_inc(ph.s["lo_done"], 1)
                        for c in range(EC):
                            dve.wait_ge(ph.s["kraw_ready"], b * EC + c + 1)
                            dve.wait_ge(ph.s["lo_done"], b * CH + EC + c - 1)
                            s = st[:, c % 2, :]
                            dve.tensor_scalar(s, kraw[:], sg[:, 4, c:c + 1], None, ALU.mult).then_inc(ph.s["smear"], 1)
                            dve.wait_ge(ph.s["smear"], b * EC + c + 1)
                            dve.scalar_tensor_tensor(out=st[:, c % 2, 1:T], in0=kraw[:, 0:T - 1], scalar=sg[:, 0, c:c + 1],
                                                     in1=st[:, c % 2, 1:T], op0=ALU.mult, op1=ALU.add).then_inc(ph.s["k_ready"], 1)
                            dve.wait_ge(ph.s["k_hi"], b * EC + c + 1)
                            dve.tensor_tensor(los[:, c % 2, :], st[:, c % 2, :], his[:, c % 2, :], ALU.subtract).then_inc(ph.s["lo_done"], 1)
                        for j in range(TB):
                            dve.wait_ge(ph.s["pe_done"], done + CH + 2 + 2 * j)
                            dve.tensor_tensor(v_all[:, ds(b * TB + j, 1), :], PV[:, None, :], brow[:, None, 0:E], ALU.add).then_inc(ph.s["v_ready"], 1)
                            dve.wait_ge(ph.s["pe_done"], done + CH + 3 + 2 * j)
                            dve.wait_ge(ph.s["gate_ready"], b * TB + j)
                            dve.tensor_tensor(vtmp[:], PG, brow[:, E:2 * E], ALU.add).then_inc(ph.s["gate_sum"], 1)

        stacked_attention(k, "l0a", causal_plan(), H, STACK_32, qt, kt, v_all, o_all, q_pos=q_pos, k_pos=k_pos)
        project_out(k, "l0o", o_all, E, a["L0_attn_W_out"], x_in, x_out, xt_out, pre=(a["L0_attn_out_ln_w"], a["L0_attn_out_ln_b"]),
                    gate=gate)


class Job:

    def __init__(self, parts, kind, scale=1.0, bias=None, dsts=None, n_dst=0, dst=None, needs=0):
        self.parts, self.kind, self.scale, self.bias, self.dsts, self.n_dst, self.dst, self.needs = \
            parts, kind, scale, bias, dsts, n_dst, dst, needs


def column_parts(w, xs, c):
    return [(h * 512, 512, [(w[:, d, c * P:(c + 1) * P], xs[:, d, h * 512:(h + 1) * 512]) for d in range(w.shape[1])])
            for h in range(T // 512)]


def row_parts(w, xs, c0, F, j0):
    return [(i * F, F, [(xs[:, d, (j0 + i) * P:(j0 + i + 1) * P], w[:, d, c0:c0 + F]) for d in range(w.shape[1])])
            for i in range(1024 // F)]


def project_in(k, ph, xt, xs, jobs, loads, rope=None, split=False):
    nc = k.nc
    NJ = len(jobs)
    assert NJ % 2 == 0
    st = ph.sb("st", [P, 2, T])
    tmp = ph.sb("tmp", [P, 4, T]) if rope else None
    freed = [ph.sem("freed0"), ph.sem("freed1")]
    stored = [ph.sem("stored0"), ph.sem("stored1")]
    his, los = (ph.sb("his", [P, 2, T], F16), ph.sb("los", [P, 2, T], F16)) if split else (None, None)
    ph.sems_of("storing hi_done lo_done w_ld x_ld jobs_done staged kept rows_done mults rotated rstored")
    slot = [k.ps[:, 0:2, :].rearrange("p b c -> p (b c)"), k.ps[:, 2:4, :].rearrange("p b c -> p (b c)")]
    stores = [j for j in range(NJ) if jobs[j].kind == "store"]
    keeps = [j for j in range(NJ) if jobs[j].kind == "keep"]
    firsts = [j for j in range(NJ) if jobs[j].kind == "first"]
    rows = [j for j in range(NJ) if jobs[j].kind == "rows"]
    R = len(firsts)
    out_of = [[sum(jobs[i].n_dst for i in range(j) if i % 2 == s and jobs[i].kind == "store") for j in range(NJ + 1)] for s in range(2)]
    with nc.Block() as block:

        @block.sync
        def _(sp):
            for dst, src in loads:
                sp.dma_start(dst, src).then_inc(ph.s["w_ld"], 16)
            with sp.Fori(0, B) as b:
                sp.wait_ge(ph.s["jobs_done"], b * NJ)
                sp.dma_start(xs[:], xt[:, ds(b * T, T)].rearrange("(c p) t -> p c t", p=P)).then_inc(ph.s["x_ld"], 16)
                for n, j in enumerate(stores):
                    places = jobs[j].dsts(b)
                    sp.wait_ge(ph.s["lo_done"] if split else ph.s["staged"], b * len(stores) + n + 1)
                    if split:
                        sp.sem_inc(ph.s["storing"], 1)
                    for r0, r1, *dst in places:
                        for stage, d in zip((his, los) if split else (st,), dst):
                            sp.dma_start(d, stage[r0:r1, j % 2, :]).then_inc(stored[j % 2], 16)
                for n, j in enumerate(firsts):
                    places = [jobs[j + half].dsts(b) for half in range(2)]
                    for half in range(2):
                        sp.wait_ge(ph.s["lo_done"], 2 * (b * R + n) + half + 1)
                        sp.sem_inc(ph.s["storing"], 1)
                        for r0, r1, *dst in places[half]:
                            for stage, d in zip((his, los), dst):
                                sp.dma_start(d, stage[r0:r1, half, :]).then_inc(ph.s["rstored"], 16)
            for s in range(2):
                if out_of[s][NJ]:
                    sp.wait_ge(stored[s], 16 * B * out_of[s][NJ])
            if R:
                sp.wait_ge(ph.s["rstored"], 16 * B * R * 2 * jobs[firsts[0]].n_dst)

        @block.tensor
        def _(pe):
            pe.wait_ge(ph.s["w_ld"], 16 * len(loads))
            with pe.Fori(0, B) as b:
                pe.wait_ge(ph.s["x_ld"], 16 * b + 16)
                for j, job in enumerate(jobs):
                    pe.wait_ge(freed[j % 2], b * (NJ // 2) + j // 2)
                    if job.needs:
                        pe.wait_ge(ph.s["kept"], b * len(keeps) + job.needs)
                    for c0, w, terms in job.parts:
                        for n, (lhsT, rhs) in enumerate(terms):
                            ins = pe.matmul(slot[j % 2][:, c0:c0 + w], lhsT, rhs, start=n == 0, stop=n == len(terms) - 1)
                    ins.then_inc(ph.s["jobs_done"], 1)

        @block.scalar
        def _(act):
            act.wait_ge(ph.s["w_ld"], 16 * len(loads))
            with act.Fori(0, B) as b:
                for j, job in enumerate(jobs):
                    if job.kind in ("first", "second"):
                        if job.kind == "second":
                            for half in range(2):
                                r = b * R + firsts.index(j - 1)
                                act.wait_ge(ph.s["rotated"], 2 * r + half + 1)
                                act.wait_ge(ph.s["rstored"], 16 * 2 * job.n_dst * r)
                                act.activation(his[:, half, :], st[:, half, :], ACT.Copy).then_inc(ph.s["hi_done"], 1)
                        continue
                    act.wait_ge(ph.s["jobs_done"], b * NJ + j + 1)
                    bias = 0.0 if job.bias is None else job.bias
                    if job.kind == "store":
                        act.wait_ge(stored[j % 2], 16 * (b * out_of[j % 2][NJ] + out_of[j % 2][j]))
                        if split:
                            act.activation(his[:, j % 2, :], slot[j % 2], ACT.Identity, scale=job.scale, bias=bias).then_inc(ph.s["hi_done"], 1)
                        act.activation(st[:, j % 2, :], slot[j % 2], ACT.Identity, scale=job.scale, bias=bias).then_inc(ph.s["staged"], 1)
                        act.wait_ge(ph.s["staged"], b * len(stores) + stores.index(j) + 1)
                    elif job.kind == "keep":
                        act.activation(job.dst, slot[j % 2], ACT.Identity, scale=job.scale, bias=bias).then_inc(ph.s["kept"], 1)
                        act.wait_ge(ph.s["kept"], b * len(keeps) + keeps.index(j) + 1)
                    else:
                        F = job.parts[0][1]
                        act.activation(job.dst(b), slot[j % 2].rearrange("p (t f) -> p t f", f=F), ACT.Copy).then_inc(ph.s["rows_done"], 1)
                        act.wait_ge(ph.s["rows_done"], b * len(rows) + rows.index(j) + 1)
                    act.sem_inc(freed[j % 2], 1)

        @block.vector
        def _(dve):

            def lower(n, half):
                dve.wait_ge(ph.s["hi_done"], n + 1)
                dve.tensor_tensor(los[:, half, :], st[:, half, :], his[:, half, :], ALU.subtract).then_inc(ph.s["lo_done"], 1)

            if not R:
                if split:
                    with dve.Fori(0, B) as b:
                        for n, j in enumerate(stores):
                            dve.wait_ge(ph.s["staged"], b * len(stores) + n + 1)
                            lower(b * len(stores) + n, j % 2)
                return
            cos, sin = rope
            dve.wait_ge(ph.s["w_ld"], 16 * len(loads))
            with dve.Fori(0, B) as b:
                for n, j in enumerate(firsts):
                    for half, (f, o) in enumerate(((cos, sin), (sin, cos))):
                        dve.wait_ge(ph.s["jobs_done"], b * NJ + j + half + 1)
                        if half == 0:
                            dve.wait_ge(ph.s["rotated"], 2 * (b * R + n))
                        dve.tensor_tensor(tmp[:, 2 * half, :], slot[half], f[:], ALU.mult).then_inc(ph.s["mults"], 1)
                        dve.tensor_tensor(tmp[:, 2 * half + 1, :], slot[half], o[:], ALU.mult).then_inc(freed[half], 1)
                    dve.wait_ge(freed[1], b * (NJ // 2) + (j + 1) // 2 + 1)
                    dve.sem_inc(ph.s["mults"], 1)
                    for half in range(2):
                        lower(2 * (b * R + n) + half, half)

        @block.gpsimd
        def _(pool):
            if not R:
                return
            with pool.Fori(0, B) as b:
                for n, j in enumerate(firsts):
                    pool.wait_ge(ph.s["mults"], 3 * (b * R + n) + 3)
                    pool.wait_ge(ph.s["lo_done"], 2 * (b * R + n))
                    pool.tensor_tensor(st[:, 0, :], tmp[:, 0, :], tmp[:, 2, :], ALU.subtract).then_inc(ph.s["rotated"], 1)
                    pool.tensor_tensor(st[:, 1, :], tmp[:, 1, :], tmp[:, 3, :], ALU.add).then_inc(ph.s["rotated"], 1)


def flat(dram):
    return dram.rearrange("h d n -> (h d) n")


def halves_of(k, name, rows):
    return {part: k.dram(f"{name}_{part}", [rows, N], F16) for part in "hl"}


def to_halves(pair, c):
    return lambda b: [(0, P) + tuple(pair[x][c * P:(c + 1) * P, ds(b * T, T)] for x in "hl")]


def to_flat(dram, c):
    return lambda b: [(0, P, flat(dram)[c * P:(c + 1) * P, ds(b * T, T)])]


def l1_self_attention(k, x_in, x_out, xt_out):
    nc, a = k.nc, k.a
    H, KV, DH = 16, 4, 64
    HF = DH // 2
    FQ, FK = H * DH, KV * DH
    qt, kt = halves_of(k, "l1_q", FQ), halves_of(k, "l1_k", FK)
    with ExitStack() as keep:
        v_all = keep.enter_context(nc.sbuf_tensor("l1_v_all", [P, NT, FK], F32))
        o_all = keep.enter_context(nc.sbuf_tensor("l1_o_all", [P, NT, FQ], F32))
        with Phase(k, "l1p") as ph:
            w = ph.sb("w", [P, DC, FQ + 2 * FK])
            cos, sin = ph.sb("cos", [P, T]), ph.sb("sin", [P, T])
            xs = ph.sb("xs", [P, DC, T])
            jobs = []

            def halves(pair, g, half):
                def dsts(b):
                    r = [(4 * g + h) * DH + half * HF for h in range(4)]
                    return [(h * HF, (h + 1) * HF) + tuple(pair[x][r[h]:r[h] + HF, ds(b * T, T)] for x in "hl") for h in range(4)]
                return dsts

            for dram, n, c0 in ((qt, FQ // (2 * P), 0), (kt, FK // (2 * P), FQ // P)):
                for g in range(n):
                    for half, kind in enumerate(("first", "second")):
                        jobs.append(Job(column_parts(w, xs, c0 + 2 * g + half), kind, dsts=halves(dram, g, half), n_dst=8))
            for j in range(0, TB, 4):
                jobs.append(Job(row_parts(w, xs, FQ + FK, FK, j), "rows", dst=lambda b, j=j: v_all[:, ds(b * TB + j, 4), :]))
            project_in(k, ph, k.xt, xs, jobs,
                       [(w[:, :, 0:FQ], weight_rows(a["L1_attn_Wq"])), (w[:, :, FQ:FQ + FK], weight_rows(a["L1_attn_Wk"])),
                        (w[:, :, FQ + FK:], weight_rows(a["L1_attn_Wv"])), (cos[:], a["c_cos"]), (sin[:], a["c_sin"])], (cos, sin),
                       split=True)
        stacked_attention(k, "l1a", causal_plan(), H, STACK_64, qt, kt, v_all, o_all, kv_of=H // KV)
        project_out(k, "l1o", o_all, FQ, a["L1_attn_Wo"], x_in, x_out, xt_out)


def l2_self_attention(k, x_in, x_out, xt_out):
    nc, a = k.nc, k.a
    qt, kt = k.dram("l2_qt", [1, D, N]), k.dram("l2_kt", [1, D, N])
    with ExitStack() as keep:
        v_all = keep.enter_context(nc.sbuf_tensor("l2_v_all", [P, NT, D], F32))
        o_all = keep.enter_context(nc.sbuf_tensor("l2_o_all", [P, NT, D], F32))
        with Phase(k, "l2p") as ph:
            w = ph.sb("w", [P, DC, 3 * D])
            xs = ph.sb("xs", [P, DC, T])
            jobs = [Job(column_parts(w, xs, c), "store", scale=D ** -0.5 if c < DC else 1.0, dsts=to_flat((qt, kt)[c // DC], c % DC), n_dst=1)
                    for c in range(2 * DC)]
            jobs += [Job(row_parts(w, xs, 2 * D, D, j), "rows", dst=lambda b, j=j: v_all[:, ds(b * TB + j, 4), :]) for j in range(0, TB, 4)]
            project_in(k, ph, k.xt, xs, jobs, [(w[:, :, i * D:(i + 1) * D], weight_rows(a[f"L2_attn_{m}"])) for i, m in enumerate(("Wq", "Wk", "Wv"))])
        attention(k, "l2a", causal_units(D), 1, D, D, qt, kt, v_all, o_all)
        project_out(k, "l2o", o_all, D, a["L2_attn_Wo"], x_in, x_out, xt_out)


def l3_self_attention(k, x_in, x_out, xt_out):
    nc, a = k.nc, k.a
    H, DH = 16, 16
    qt, kt = halves_of(k, "l3_q", D), halves_of(k, "l3_k", D)
    with ExitStack() as keep:
        v_all = keep.enter_context(nc.sbuf_tensor("l3_v_all", [P, NT, D], F32))
        o_all = keep.enter_context(nc.sbuf_tensor("l3_o_all", [P, NT, D], F32))
        k_eff = keep.enter_context(nc.sbuf_tensor("l3_k_eff", [P, 1, D], F32))
        v_eff = keep.enter_context(nc.sbuf_tensor("l3_v_eff", [P, 1, D], F32))
        with Phase(k, "l3e") as ph:
            ph.sems_of("w_ld prod copied")
            uq, uk, uv = (ph.sb(n, [P, DC, P]) for n in ("uq", "uk", "uv"))
            wo = ph.sb("wo", [P, DC, D])
            dq = ph.sb("dq", [P, D])
            inner = ph.sb("inner", [P, P])
            with nc.Block() as block:

                @block.sync
                def _(sp):
                    for dst, src in ((uq, "W_uq"), (uk, "W_uk"), (uv, "W_uv"), (wo, "W_o")):
                        sp.dma_start(dst[:], weight_rows(a[f"L3_attn_{src}"])).then_inc(ph.s["w_ld"], 16)
                    sp.dma_start(dq[:], a["L3_attn_W_dq"]).then_inc(ph.s["w_ld"], 16)

                @block.tensor
                def _(pe):
                    pe.wait_ge(ph.s["w_ld"], 80)
                    for c in range(DC):
                        ins = pe.matmul(k.ps[:, 0, 0:P], uq[:, c, :], uk[:, c, :], start=c == 0, stop=c == DC - 1)
                    ins.then_inc(ph.s["prod"], 1)
                    for c in range(DC):
                        ins = pe.matmul(k.ps[:, 1, 0:D], uv[:, c, :], wo[:, c, :], start=c == 0, stop=c == DC - 1)
                    ins.then_inc(ph.s["prod"], 1)
                    pe.wait_ge(ph.s["copied"], 1)
                    pe.matmul(k.ps[:, 2, 0:D], inner[:], dq[:], start=True, stop=True).then_inc(ph.s["prod"], 1)

                @block.scalar
                def _(act):
                    for n, (dst, src) in enumerate(((inner[:], k.ps[:, 0, 0:P]), (v_eff[:, 0, :], k.ps[:, 1, 0:D]), (k_eff[:, 0, :], k.ps[:, 2, 0:D]))):
                        act.wait_ge(ph.s["prod"], n + 1)
                        act.activation(dst, src, ACT.Copy).then_inc(ph.s["copied"], 1)
                    act.wait_ge(ph.s["copied"], 3)

        with Phase(k, "l3p") as ph:
            w = ph.sb("w", [P, DC, 2 * P])
            uq = ph.sb("uq", [P, 1, D])
            xs = ph.sb("xs", [P, DC, T])
            lat = ph.sb("lat", [P, 2, T])
            low, latent = lat[:, 0:1, :], lat[:, 1:2, :]
            jobs = [Job(column_parts(w, xs, c), "keep", dst=lat[:, c, :]) for c in range(2)]
            jobs += [Job(column_parts(uq, low, c), "store", scale=DH ** -0.5, dsts=to_halves(qt, c), n_dst=2, needs=2) for c in range(2)]
            jobs += [Job(column_parts(k_eff, latent, c), "store", dsts=to_halves(kt, c), n_dst=2, needs=2) for c in range(2)]
            jobs += [Job(row_parts(v_eff, latent, 0, D, j), "rows", dst=lambda b, j=j: v_all[:, ds(b * TB + j, 4), :], needs=2) for j in range(0, TB, 4)]
            project_in(k, ph, k.xt, xs, jobs, [(w[:, :, 0:P], weight_rows(a["L3_attn_W_dq_T"])), (w[:, :, P:], weight_rows(a["L3_attn_W_dkv"])),
                                               (uq[:, 0, :], a["L3_attn_W_uq_T"])], split=True)
        stacked_attention(k, "l3a", causal_plan(), H, STACK_16, qt, kt, v_all, o_all)
        add_and_norm(k, "l3o", o_all, x_in, x_out, xt_out)


def context(k, name, kt, v_all, F, wk, wv, bk=None, bv=None, norm=None):
    nc, a = k.nc, k.a
    FC = F // P
    CR = CTX - P
    NM = B * M
    W = min(F, 512)
    with Phase(k, name) as ph:
        ca, cb = ph.sb("ca", [P, NM]), ph.sb("cb", [CR, NM])
        wka, wkb = ph.sb("wka", [P, F]), ph.sb("wkb", [CR, F])
        wva, wvb = ph.sb("wva", [P, F]), ph.sb("wvb", [CR, F])
        bkc = ph.sb("bkc", [P, FC]) if bk is not None else None
        bvr = ph.sb("bvr", [M, F]) if bv is not None else None
        st = ph.sb("st", [P, FC, NM])
        loads = [(wka[:], wk[0:P, :]), (wkb[:], wk[P:CTX, :]), (wva[:], wv[0:P, :]), (wvb[:], wv[P:CTX, :])]
        if bk is not None:
            loads += [(bkc[:], bk), (bvr[:], bv)]
        if norm is None:
            loads += [(ca[:], a["ctx_T"][0:P, :]), (cb[:], a["ctx_T"][P:CTX, :])]
        else:
            rows = ph.sb("rows", [M, B, CTX])
            stats, mv = ph.sb("stats", [M, B, 6]), ph.sb("mv", [M, B, 2])
            ve, sd, rs = ph.sb("ve", [M, B]), ph.sb("sd", [M, B]), ph.sb("rs", [M, B])
            na, nb = ph.sb("na", [P, 2]), ph.sb("nb", [CR, 2])
            gap = ph.sb("gap", [M, 1])
            loads += [(rows[:], a["ctx_rows"]), (na[:], norm[0:P, :]), (nb[:], norm[P:CTX, :])]
        split = isinstance(kt, dict)
        his, los = (ph.sb("his", [P, FC, NM], F16), ph.sb("los", [P, FC, NM], F16)) if split else (None, None)
        ph.sems_of("hi_done lo_done ld chain sd_ready turned cols prods k_moved v_moved k_st")
        bank = [k.ps[:, 0, :], k.ps[:, 1, :]]
        n_v = B * (F // W)
        with nc.Block() as block:

            @block.sync
            def _(sp):
                for dst, src in loads:
                    sp.dma_start(dst, src).then_inc(ph.s["ld"], 16)
                sp.wait_ge(ph.s["k_moved"], FC)
                if split:
                    sp.wait_ge(ph.s["lo_done"], 1)
                pairs = ((kt["h"], his), (kt["l"], los)) if split else ((flat(kt), st),)
                for dst, src in pairs:
                    sp.dma_start(dst.rearrange("(c p) n -> p c n", p=P), src[:]).then_inc(ph.s["k_st"], 16)
                sp.wait_ge(ph.s["k_st"], 16 * len(pairs))

            @block.tensor
            def _(pe):
                pe.wait_ge(ph.s["ld"], 16 * len(loads))
                if norm is not None:
                    pe.wait_ge(ph.s["chain"], 2 * B + 3)
                    for b in range(B):
                        pe.transpose(k.ps[:, 2, b * P:b * P + M], rows[:, b, 0:P], k.ident[0:M, 0:M])
                        ins = pe.transpose(k.ps[0:CR, 3, b * P:b * P + M], rows[:, b, P:CTX], k.ident[0:M, 0:M])
                    ins.then_inc(ph.s["turned"], 1)
                    pe.wait_ge(ph.s["cols"], 2 * B)
                n = 0
                for c in range(FC):
                    if n >= 2:
                        pe.wait_ge(ph.s["k_moved"], n - 1)
                    pe.matmul(bank[n % 2][:, 0:NM], wka[:, c * P:(c + 1) * P], ca[:], start=True, stop=False)
                    pe.matmul(bank[n % 2][:, 0:NM], wkb[:, c * P:(c + 1) * P], cb[:], start=False, stop=True).then_inc(ph.s["prods"], 1)
                    n += 1
                pe.wait_ge(ph.s["k_moved"], FC)
                for i in range(n_v):
                    b, f = i // (F // W), i % (F // W)
                    if i >= 2:
                        pe.wait_ge(ph.s["v_moved"], i - 1)
                    o = bank[n % 2][0:M, 0:W]
                    pe.matmul(o, ca[:, b * M:(b + 1) * M], wva[:, f * W:(f + 1) * W], start=True, stop=False)
                    pe.matmul(o, cb[:, b * M:(b + 1) * M], wvb[:, f * W:(f + 1) * W], start=False, stop=True).then_inc(ph.s["prods"], 1)
                    n += 1

            @block.scalar
            def _(act):
                act.wait_ge(ph.s["ld"], 16 * len(loads))
                if norm is not None:
                    act.wait_ge(ph.s["chain"], 2 * B + 1)
                    act.activation(sd[:], ve[:], ACT.Sqrt).then_inc(ph.s["sd_ready"], 1)
                    act.wait_ge(ph.s["turned"], 1)
                    for b in range(B):
                        act.activation(ca[:, b * M:(b + 1) * M], k.ps[:, 2, b * P:b * P + M], ACT.Identity, scale=na[:, 0:1], bias=na[:, 1:2]).then_inc(ph.s["cols"], 1)
                        act.activation(cb[:, b * M:(b + 1) * M], k.ps[0:CR, 3, b * P:b * P + M], ACT.Identity, scale=nb[:, 0:1], bias=nb[:, 1:2]).then_inc(ph.s["cols"], 1)
                for c in range(FC):
                    act.wait_ge(ph.s["prods"], c + 1)
                    act.activation(st[:, c, :], bank[c % 2][:, 0:NM], ACT.Identity, bias=0.0 if bk is None else bkc[:, c:c + 1]).then_inc(ph.s["k_moved"], 1)
                if split:
                    act.wait_ge(ph.s["k_moved"], FC)
                    act.activation(his[:], st[:], ACT.Copy).then_inc(ph.s["hi_done"], 1)

            @block.vector
            def _(dve):
                dve.wait_ge(ph.s["ld"], 16 * len(loads))
                if norm is not None:
                    for b in range(B):
                        dve.bn_stats(stats[:, b, :], rows[:, b, :]).then_inc(ph.s["chain"], 1)
                    dve.wait_ge(ph.s["chain"], B)
                    dve.memset(gap[:], 0.0)
                    for b in range(B):
                        dve.bn_aggr(mv[:, b, :], stats[:, b, :]).then_inc(ph.s["chain"], 1)
                    dve.wait_ge(ph.s["chain"], 2 * B)
                    dve.tensor_scalar(ve[:], mv[:, :, 1], EPS, None, ALU.add).then_inc(ph.s["chain"], 1)
                    dve.wait_ge(ph.s["sd_ready"], 1)
                    dve.reciprocal(rs[:], sd[:]).then_inc(ph.s["chain"], 1)
                    dve.wait_ge(ph.s["chain"], 2 * B + 2)
                    for b in range(B):
                        ins = dve.tensor_scalar(rows[:, b, :], rows[:, b, :], mv[:, b, 0:1], rs[:, b:b + 1], ALU.subtract, ALU.mult)
                    ins.then_inc(ph.s["chain"], 1)
                for i in range(n_v):
                    b, f = i // (F // W), i % (F // W)
                    dve.wait_ge(ph.s["prods"], FC + i + 1)
                    src = bank[(FC + i) % 2][0:M, 0:W]
                    if bv is None:
                        ins = dve.tensor_copy(v_all[:, b, f * W:(f + 1) * W], src)
                    else:
                        ins = dve.tensor_tensor(v_all[:, b, f * W:(f + 1) * W], src, bvr[:, f * W:(f + 1) * W], ALU.add)
                    ins.then_inc(ph.s["v_moved"], 1)
                if split:
                    dve.wait_ge(ph.s["hi_done"], 1)
                    dve.tensor_tensor(los[:], st[:], his[:], ALU.subtract).then_inc(ph.s["lo_done"], 1)


def cross_attention(k, name, H, DH, x_in, x_out, xt_out, xq, wq, wk, wv, wo, scale, bq=None, bk=None, bv=None, bo=None,
                    norm=None, shared_keys=False):
    nc = k.nc
    F = H * DH
    FC = F // P
    stack = None if shared_keys else {16: STACK_16, 64: STACK_64}[DH]
    if stack:
        qt = halves_of(k, f"{name}_q", F)
        kt = {part: k.dram(f"{name}_k_{part}", [F, B * M], F16) for part in "hl"}
    else:
        qt, kt = k.dram(f"{name}_qt", [H, DH, N]), k.dram(f"{name}_kt", [H, DH, B * M])
    with ExitStack() as keep:
        v_all = keep.enter_context(nc.sbuf_tensor(f"{name}_v_all", [M, B, F], F32))
        o_all = keep.enter_context(nc.sbuf_tensor(f"{name}_o_all", [P, NT, F], F32))
        context(k, f"{name}c", kt, v_all, F, wk, wv, bk, bv, norm)
        with Phase(k, f"{name}p") as ph:
            w = ph.sb("w", [P, DC, F])
            xs = ph.sb("xs", [P, DC, T])
            loads = [(w[:], weight_rows(wq))]
            if bq is not None:
                b_q, b_s = ph.sb("b_q", [P, FC]), ph.sb("b_s", [P, FC])
                ph.sems_of("b_ld b_scaled")
                with nc.Block() as block:

                    @block.sync
                    def _(sp):
                        sp.dma_start(b_q[:], bq).then_inc(ph.s["b_ld"], 16)

                    @block.vector
                    def _(dve):
                        dve.wait_ge(ph.s["b_ld"], 16)
                        dve.tensor_scalar(b_s[:], b_q[:], scale, None, ALU.mult).then_inc(ph.s["b_scaled"], 1)
                        dve.wait_ge(ph.s["b_scaled"], 1)

            jobs = [Job(column_parts(w, xs, c), "store", scale=scale, bias=None if bq is None else b_s[:, c:c + 1], dsts=to_halves(qt, c) if stack else to_flat(qt, c), n_dst=2 if stack else 1)
                    for c in range(FC)]
            project_in(k, ph, xq, xs, jobs, loads, split=stack is not None)
        if stack:
            stacked_attention(k, f"{name}a", context_plan(), H, stack, qt, kt, v_all, o_all)
        else:
            attention(k, f"{name}a", cross_units(DH, M, B if shared_keys else 1), H, DH, DH, qt, kt, v_all, o_all, n_keys=B * M, key_rows=M)
        project_out(k, f"{name}o", o_all, F, wo, x_in, x_out, xt_out, bias=bo)


def l0_cross_attention(k, x_in, x_out, xt_out):
    a = k.a
    H, DH = 8, 128
    cross_attention(k, "x0", H, DH, x_in, x_out, xt_out, k.xt, a["L0_xattn_Wq"], a["L0_xattn_Wk"], a["L0_xattn_Wv"], a["L0_xattn_Wout"],
                    1.5 * DH ** -0.5, bo=a["L0_xattn_bout"], shared_keys=True)


def l1_cross_attention(k, x_in, x_out, xt_out):
    a = k.a
    cross_attention(k, "x1", 16, 16, x_in, x_out, xt_out, k.xt, a["L1_xattn_Wq"], a["L1_xattn_Wk"], a["L1_xattn_Wv"], a["L1_xattn_Wo"],
                    16 ** -0.5, bq=a["L1_xattn_bq"], bk=a["L1_xattn_bk"], bv=a["L1_xattn_bv"], bo=a["L1_xattn_bo"])


def l2_cross_attention(k, x_in, x_out, xt_out):
    a = k.a
    cross_attention(k, "x2", 4, 64, x_in, x_out, xt_out, k.xt, a["L2_xattn_Wq"], a["L2_xattn_Wk"], a["L2_xattn_Wv"], a["L2_xattn_Wo"],
                    64 ** -0.5, bo=a["L2_xattn_bo"])


def l3_cross_attention(k, x_in, x_out, xt_out):
    a = k.a
    norm_columns(k, "x3n", x_in, k.xnt, a["L3_xattn_g_x"], a["L3_xattn_b_x"])
    cross_attention(k, "x3", 16, 64, x_in, x_out, xt_out, k.xnt, a["L3_xattn_Wq"], a["L3_xattn_Wk"], a["L3_xattn_Wv"], a["L3_xattn_Wo"],
                    64 ** -0.5, norm=a["L3_xattn_norm_c"])


def top_mask(dve, ph, ch, sel, m8, K, E, tmp, mask):
    gt, eq, rank, need, reset = tmp
    for t in range(NT):
        ch.step(dve.max(m8[:, t, :], sel[:, t, :]))
    ch.wait()
    least = m8[:, :, K - 1:K].to_broadcast([P, NT, E])
    ch.step(dve.tensor_tensor(gt[:], sel[:], least, ALU.is_gt))
    ch.step(dve.tensor_tensor(eq[:], sel[:], least, ALU.is_equal))
    ch.wait()
    ch.step(dve.tensor_reduce(need[:], gt[:], AX.X, ALU.add))
    ch.step(dve.tensor_tensor_scan(rank[:].rearrange("p t e -> p (t e)"), reset[:].rearrange("p t e -> p (t e)"),
                                   eq[:].rearrange("p t e -> p (t e)"), 0.0, ALU.mult, ALU.add))
    ch.wait()
    ch.step(dve.tensor_scalar(need[:], need[:], -1.0, float(K), ALU.mult, ALU.add))
    ch.wait()
    ch.step(dve.tensor_tensor(rank[:], rank[:], need[:, :, None].to_broadcast([P, NT, E]), ALU.is_le))
    ch.wait()
    ch.step(dve.tensor_tensor(eq[:], eq[:], rank[:], ALU.mult))
    ch.wait()
    ch.step(dve.tensor_tensor(mask[:], gt[:], eq[:], ALU.add))
    ch.wait()


def top_mask_buffers(ph, E):
    return [ph.sb("gt", [P, NT, E]), ph.sb("eq", [P, NT, E]), ph.sb("rank", [P, NT, E]), ph.sb("need", [P, NT]), ph.sb("reset", [P, NT, E])]


def l0_gates(k, gates, xt_all):
    nc, a = k.nc, k.a
    E, K = 32, 4
    CAP = 2 * (N // 2) * K // E
    with Phase(k, "g0") as ph:
        wgb, wg = ph.sb("wgb", [P, DC, E], BF16), ph.sb("wg", [P, DC, E])
        bias = ph.sb("bias", [P, E])
        before = ph.sb("before", [P, P])
        ones = ph.sb("ones", [P, P])
        sc, sel, mask = ph.sb("sc", [P, NT, E]), ph.sb("sel", [P, NT, E]), ph.sb("mask", [P, NT, E])
        by_expert, resets, upto = ph.sb("by_expert", [P, E, NT]), ph.sb("resets", [P, E, NT]), ph.sb("upto", [P, E, NT])
        earlier = ph.sb("earlier", [P, NT, E])
        m8 = ph.sb("m8", [P, NT, 8])
        total, inv = ph.sb("total", [P, NT]), ph.sb("inv", [P, NT])
        tmp = top_mask_buffers(ph, E)
        ph.sems_of("ld conv logits_done sc_ready chain mask_ready pos_done")
        logits = k.ps[:, 0, :].rearrange("p (t e) -> p t e", e=E)
        place = k.ps[:, 1, :].rearrange("p (t e) -> p t e", e=E)
        with nc.Block() as block:

            @block.sync
            def _(sp):
                sp.dma_start(wgb[:], weight_rows(a["L0_ffn_gate_w"])).then_inc(ph.s["ld"], 16)
                sp.dma_start(bias[:], a["L0_ffn_bias"]).then_inc(ph.s["ld"], 16)
                sp.dma_start(before[:], a["c_before"]).then_inc(ph.s["ld"], 16)
                sp.dma_start(xt_all[:], weight_rows(k.xt)).then_inc(ph.s["ld"], 16)

            @block.gpsimd
            def _(pool):
                pool.memset(ones[:], 1.0).then_inc(ph.s["conv"], 1)
                pool.memset(tmp[4][:], 1.0).then_inc(ph.s["conv"], 1)
                pool.memset(resets[:], 1.0).then_inc(ph.s["conv"], 1)
                pool.wait_ge(ph.s["conv"], 3)
                pool.memset(tmp[4][:, :, 0:1], 0.0).then_inc(ph.s["conv"], 1)
                pool.memset(resets[:, :, 0:1], 0.0).then_inc(ph.s["conv"], 1)
                pool.wait_ge(ph.s["ld"], 64)
                pool.tensor_copy(wg[:], wgb[:]).then_inc(ph.s["conv"], 1)

            @block.tensor
            def _(pe):
                pe.wait_ge(ph.s["conv"], 6)
                for t in range(NT):
                    for d in range(DC):
                        ins = pe.matmul(logits[:, t, :], xt_all[:, d, t * P:(t + 1) * P], wg[:, d, :], start=d == 0, stop=d == DC - 1)
                ins.then_inc(ph.s["logits_done"], 1)
                pe.wait_ge(ph.s["mask_ready"], 1)
                for t in range(NT):
                    pe.matmul(place[:, t, :], before[:], mask[:, t, :], start=True, stop=False)
                    ins = pe.matmul(place[:, t, :], ones[:], earlier[:, t, :], start=False, stop=True)
                ins.then_inc(ph.s["pos_done"], 1)

            @block.scalar
            def _(act):
                act.wait_ge(ph.s["logits_done"], 1)
                act.activation(sc[:], logits, ACT.Sigmoid).then_inc(ph.s["sc_ready"], 1)

            @block.vector
            def _(dve):
                ch = Count(dve, ph.s["chain"], 0, 0)
                dve.wait_ge(ph.s["conv"], 6)
                dve.wait_ge(ph.s["sc_ready"], 1)
                ch.step(dve.tensor_tensor(sel[:], sc[:], bias[:, None, :].to_broadcast([P, NT, E]), ALU.add))
                ch.wait()
                top_mask(dve, ph, ch, sel, m8, K, E, tmp, mask)
                ch.step(dve.tensor_copy(by_expert[:], mask[:].rearrange("p t e -> p e t")))
                ch.step(dve.tensor_tensor(sel[:], sc[:], mask[:], ALU.mult))
                ch.wait()
                ch.step(dve.tensor_tensor_scan(upto[:].rearrange("p e t -> p (e t)"), resets[:].rearrange("p e t -> p (e t)"),
                                               by_expert[:].rearrange("p e t -> p (e t)"), 0.0, ALU.mult, ALU.add))
                ch.wait()
                dve.tensor_tensor(earlier[:], upto[:].rearrange("p e t -> p t e"), mask[:], ALU.subtract).then_inc(ph.s["mask_ready"], 1)
                ch.step(dve.tensor_reduce(total[:], sel[:], AX.X, ALU.add))
                ch.wait()
                ch.step(dve.tensor_scalar(total[:], total[:], 1e-12, None, ALU.max))
                ch.wait()
                ch.step(dve.reciprocal(inv[:], total[:]))
                ch.wait()
                ch.step(dve.tensor_tensor(sel[:], sel[:], inv[:, :, None].to_broadcast([P, NT, E]), ALU.mult))
                dve.wait_ge(ph.s["pos_done"], 1)
                ch.wait()
                ch.step(dve.scalar_tensor_tensor(out=gates[:, :, 0:E], in0=place, scalar=float(CAP), in1=sel[:], op0=ALU.is_lt, op1=ALU.mult))
                ch.step(dve.memset(gates[:, :, E:E + 1], 1.0))
                ch.wait()


def l1_gates(k, gates, xt_all):
    nc, a = k.nc, k.a
    E, K = 8, 2
    with Phase(k, "g1") as ph:
        wg = ph.sb("wg", [P, DC, E])
        lg, m8 = ph.sb("lg", [P, NT, E]), ph.sb("m8", [P, NT, 8])
        gap, ex, den = ph.sb("gap", [P, NT]), ph.sb("ex", [P, NT]), ph.sb("den", [P, NT])
        inv, r = ph.sb("inv", [P, NT]), ph.sb("r", [P, 2, NT])
        m1, m2 = ph.sb("m1", [P, NT, E]), ph.sb("m2", [P, NT, E])
        tmp = top_mask_buffers(ph, E)
        ph.sems_of("ld conv logits_done chain gap_ready ex_ready")
        logits = k.ps[:, 0, 0:NT * E].rearrange("p (t e) -> p t e", e=E)
        with nc.Block() as block:

            @block.sync
            def _(sp):
                sp.dma_start(wg[:], weight_rows(a["L1_ffn_Wr"])).then_inc(ph.s["ld"], 16)
                sp.dma_start(xt_all[:], weight_rows(k.xt)).then_inc(ph.s["ld"], 16)

            @block.gpsimd
            def _(pool):
                pool.memset(tmp[4][:], 1.0).then_inc(ph.s["conv"], 1)
                pool.wait_ge(ph.s["conv"], 1)
                pool.memset(tmp[4][:, :, 0:1], 0.0).then_inc(ph.s["conv"], 1)

            @block.tensor
            def _(pe):
                pe.wait_ge(ph.s["ld"], 32)
                for t in range(NT):
                    for d in range(DC):
                        ins = pe.matmul(logits[:, t, :], xt_all[:, d, t * P:(t + 1) * P], wg[:, d, :], start=d == 0, stop=d == DC - 1)
                ins.then_inc(ph.s["logits_done"], 1)

            @block.scalar
            def _(act):
                act.wait_ge(ph.s["gap_ready"], 1)
                act.activation(ex[:], gap[:], ACT.Exp).then_inc(ph.s["ex_ready"], 1)

            @block.vector
            def _(dve):
                ch = Count(dve, ph.s["chain"], 0, 0)
                dve.wait_ge(ph.s["conv"], 2)
                dve.wait_ge(ph.s["logits_done"], 1)
                ch.step(dve.tensor_copy(lg[:], logits))
                ch.wait()
                top_mask(dve, ph, ch, lg, m8, 2, E, tmp, m2)
                dve.tensor_tensor(gap[:], m8[:, :, 1], m8[:, :, 0], ALU.subtract).then_inc(ph.s["gap_ready"], 1)
                dve.wait_ge(ph.s["gap_ready"], 1)
                top_mask(dve, ph, ch, lg, m8, 1, E, tmp, m1)
                ch.step(dve.tensor_tensor(m2[:], m2[:], m1[:], ALU.subtract))
                dve.wait_ge(ph.s["ex_ready"], 1)
                ch.step(dve.tensor_scalar(den[:], ex[:], 1.0, None, ALU.add))
                ch.wait()
                ch.step(dve.reciprocal(inv[:], den[:]))
                ch.wait()
                ch.step(dve.tensor_scalar(r[:, 0, :], inv[:], 1.0, None, ALU.is_ge))
                ch.step(dve.tensor_tensor(r[:, 1, :], ex[:], inv[:], ALU.mult))
                ch.wait()
                ch.step(dve.tensor_scalar(den[:], r[:, 1, :], 1.0, None, ALU.is_ge))
                ch.wait()
                ch.step(dve.tensor_tensor(m1[:], m1[:], r[:, 0, :, None].to_broadcast([P, NT, E]), ALU.mult))
                ch.step(dve.tensor_tensor(m2[:], m2[:], den[:, :, None].to_broadcast([P, NT, E]), ALU.mult))
                ch.wait()
                ch.step(dve.tensor_tensor(gates[:, :, 0:E], m1[:], m2[:], ALU.add))
                ch.step(dve.memset(gates[:, :, E:E + 1], 1.0))
                ch.wait()


def experts(k, name, E, acc, gates, xt_all, w1, w2, w3=None, half=False):
    nc = k.nc
    I = P
    gated = w3 is not None
    mats = [m for m in (w1, w3) if m is not None]
    NM = len(mats)
    with Phase(k, name) as ph:
        wf = ph.sb("wf", [P, 2, NM + 1, 2 * P], BF16 if half else F32)
        sl = ph.sb("sl", [P, 2, GN])
        hid = ph.sb("hid", [P, 4, GN])
        if half:
            x_parts = ph.sb("x_parts", [P, 2, DC, N], F16)
            h_parts = ph.sb("h_parts", [P, 2, 4, GN], F16)
        ph.sems_of("x_hi x_lo h_done sl_ready hid_ready loading hid_hi hid_lo y_done added cleared")
        w_ld = [ph.sem("w_ld0"), ph.sem("w_ld1")]
        H1 = [k.ps[:, 0, :], k.ps[:, 1, :]]
        H3 = [k.ps[:, 2, :], k.ps[:, 3, :]]
        Y = [k.ps[:, 4 + 2 * s:6 + 2 * s, :].rearrange("p b (t d) -> p (b t) d", d=D) for s in range(2)]
        xs = [x_parts[:, i] for i in range(2)] if half else [xt_all]
        hs = [h_parts[:, i] for i in range(2)] if half else [hid]
        LEAD = 2

        def turns(eng):
            with eng.Fori(0, E // 2) as t:
                yield t * 2, 2
            yield E, 1

        with nc.Block() as block:

            @block.sync
            def _(sp):
                for e, n in turns(sp):
                    for s in range(n):
                        sp.wait_ge(ph.s["y_done"], NG * (e + s + 1))
                        sp.sem_inc(ph.s["loading"], 1)
                        for m in range(NM):
                            sp.dma_start(wf[:, s, m, :].rearrange("p (c i) -> p c i", c=DC),
                                         mats[m][ds(e + s, 1), :, :].rearrange("o (c p) i -> p (o c) i", p=P)).then_inc(w_ld[s], 16)
                        sp.dma_start(wf[:, s, NM, :], w2[ds(e + s, 1), :, :].rearrange("o i d -> i (o d)")).then_inc(w_ld[s], 16)

            @block.gpsimd
            def _(pool):
                pool.memset(acc[:], 0.0).then_inc(ph.s["cleared"], 1)
                if not half:
                    return
                for e, n in turns(pool):
                    for i in range(NG * n):
                        pool.wait_ge(ph.s["hid_hi"], NG * e + i + 1)
                        pool.tensor_tensor(h_parts[:, 1, i % 4, :], hid[:, i % 4, :], h_parts[:, 0, i % 4, :], ALU.subtract)\
                            .then_inc(ph.s["hid_lo"], 1)

            @block.tensor
            def _(pe):
                pe.sem_inc(ph.s["y_done"], 2 * NG)
                if half:
                    pe.wait_ge(ph.s["x_lo"], NG)

                def hidden(e, i):
                    s, g = i // NG, i % NG
                    if g == 0:
                        pe.wait_ge(w_ld[s % 2], (e + (s - s % 2)) * (8 * (NM + 1)) + 16 * (NM + 1))
                    pe.wait_ge(ph.s["hid_ready"], NG * e + i + 1)
                    for m, bank in zip(range(NM), (H1, H3)):
                        terms = [(d, x) for d in range(DC) for x in xs]
                        for j, (d, x) in enumerate(terms):
                            ins = pe.matmul(bank[i % 2], wf[:, s % 2, m, d * I:(d + 1) * I], x[:, d, g * GN:(g + 1) * GN], start=j == 0, stop=j == len(terms) - 1)
                    ins.then_inc(ph.s["h_done"], 1)

                def outputs(e, i):
                    s, g = i // NG, i % NG
                    if half:
                        pe.wait_ge(ph.s["hid_lo"], NG * e + i + 1)
                    else:
                        pe.wait_ge(ph.s["hid_ready"], NG * e + i + 3)
                    pe.wait_ge(ph.s["added"], NG * e + i + 1)
                    for j in range(GT):
                        for part, h in enumerate(hs):
                            ins = pe.matmul(Y[i % 2][:, j, :], h[:, i % 4, j * P:(j + 1) * P], wf[:, s, NM, :], start=part == 0, stop=part == len(hs) - 1)
                    ins.then_inc(ph.s["y_done"], 1)

                for i in range(LEAD):
                    hidden(0, i)
                for e, n in turns(pe):
                    for i in range(NG * n):
                        if n == 2 or i + LEAD < NG:
                            hidden(e, i + LEAD)
                        outputs(e, i)

            @block.scalar
            def _(act):
                if half:
                    for g in range(NG):
                        act.activation(x_parts[:, 0, :, g * GN:(g + 1) * GN], xt_all[:, :, g * GN:(g + 1) * GN], ACT.Copy).then_inc(ph.s["x_hi"], 1)

                def upper(e, i):
                    act.wait_ge(ph.s["hid_ready"], NG * e + i + 3)
                    act.activation(h_parts[:, 0, i % 4, :], hid[:, i % 4, :], ACT.Copy).then_inc(ph.s["hid_hi"], 1)

                for e, n in turns(act):
                    for i in range(NG * n):
                        if gated:
                            act.wait_ge(ph.s["h_done"], NG * e + i + 1)
                            act.wait_ge(ph.s["hid_ready"], NG * e + i + 1)
                            act.activation(sl[:, i % 2, :], H1[i % 2], ACT.Silu).then_inc(ph.s["sl_ready"], 1)
                        if half and i:
                            upper(e, i - 1)
                    if half:
                        upper(e, NG * n - 1)

            @block.vector
            def _(dve):
                dve.sem_inc(ph.s["hid_ready"], 2)
                dve.sem_inc(ph.s["added"], 2)
                if half:
                    for g in range(NG):
                        t = slice(g * GN, (g + 1) * GN)
                        dve.wait_ge(ph.s["x_hi"], g + 1)
                        dve.tensor_tensor(x_parts[:, 1, :, t], xt_all[:, :, t], x_parts[:, 0, :, t], ALU.subtract).then_inc(ph.s["x_lo"], 1)
                dve.wait_ge(ph.s["cleared"], 1)
                def hidden(e, i):
                    dve.wait_ge(ph.s["y_done"], NG * e + i - 3 + 2 * NG)
                    if gated:
                        dve.wait_ge(ph.s["sl_ready"], NG * e + i + 1)
                        ins = dve.tensor_tensor(hid[:, i % 4, :], sl[:, i % 2, :], H3[i % 2], ALU.mult)
                    else:
                        dve.wait_ge(ph.s["h_done"], NG * e + i + 1)
                        dve.tensor_scalar(sl[:, i % 2, :], H1[i % 2], 0.0, None, ALU.max).then_inc(ph.s["sl_ready"], 1)
                        dve.wait_ge(ph.s["sl_ready"], NG * e + i + 1)
                        ins = dve.tensor_tensor(hid[:, i % 4, :], sl[:, i % 2, :], sl[:, i % 2, :], ALU.mult)
                    ins.then_inc(ph.s["hid_ready"], 1)

                for i in range(LEAD):
                    hidden(0, i)
                for e, n in turns(dve):

                    def add(i):
                        s, g = i // NG, i % NG
                        dve.wait_ge(ph.s["y_done"], NG * e + i + 1 + 2 * NG)
                        dve.wait_ge(ph.s["added"], NG * e + max(i + 2 - 1, 0))
                        for j in range(GT):
                            t = g * GT + j
                            ins = dve.scalar_tensor_tensor(out=acc[:, t, :], in0=Y[i % 2][:, j, :], scalar=gates[:, t, ds(e + s, 1)],
                                                           in1=acc[:, t, :], op0=ALU.mult, op1=ALU.add)
                        ins.then_inc(ph.s["added"], 1)

                    for i in range(NG * n):
                        if n == 2 or i + LEAD < NG:
                            hidden(e, i + LEAD)
                        add(i)


def l0_feed_forward(k, x_in, x_out, xt_out):
    nc, a = k.nc, k.a
    with ExitStack() as keep:
        acc = keep.enter_context(nc.sbuf_tensor("f0_acc", [P, NT, D], F32))
        gates = keep.enter_context(nc.sbuf_tensor("f0_gates", [P, NT, 33], F32))
        xt_all = keep.enter_context(nc.sbuf_tensor("f0_xt", [P, DC, N], F32))
        l0_gates(k, gates, xt_all)
        experts(k, "f0", 32, acc, gates, xt_all, a["L0_ffn_W1"], a["L0_ffn_W2"], a["L0_ffn_W3"], half=True)
        add_and_norm(k, "f0o", acc, x_in, x_out, xt_out)


def l1_feed_forward(k, x_in, x_out, xt_out):
    nc, a = k.nc, k.a
    with ExitStack() as keep:
        acc = keep.enter_context(nc.sbuf_tensor("f1_acc", [P, NT, D], F32))
        gates = keep.enter_context(nc.sbuf_tensor("f1_gates", [P, NT, 9], F32))
        xt_all = keep.enter_context(nc.sbuf_tensor("f1_xt", [P, DC, N], F32))
        l1_gates(k, gates, xt_all)
        experts(k, "f1", 8, acc, gates, xt_all, a["L1_ffn_W1"], a["L1_ffn_W2"])
        add_and_norm(k, "f1o", acc, x_in, x_out, xt_out)


def l2_weights(k, wts):
    nc, a = k.nc, k.a
    E = 32
    with Phase(k, "g2") as ph:
        xt_all = ph.sb("xt", [P, DC, N])
        xr = ph.sb("xr", [P, NT, D])
        pt = ph.sb("pt", [P, DC, E])
        pt2 = ph.sb("pt2", [P, DC, E])
        ones = ph.sb("ones", [P, P])
        temp = ph.sb("temp", [P, 2])
        p2 = ph.sb("p2", [P, E])
        x2 = ph.sb("x2", [P, NT])
        d2, w = ph.sb("d2", [P, NT, E]), ph.sb("w", [P, NT, E])
        mask = ph.sb("mask", [P, NT, E])
        m8 = ph.sb("m8", [P, NT, 8])
        least, total, inv = ph.sb("least", [P, NT]), ph.sb("total", [P, NT]), ph.sb("inv", [P, NT])
        tmp = top_mask_buffers(ph, E)
        ph.sems_of("ld xr_ld conv pt2_ready prods chain d_ready sq_ready z_ready e_ready x2_done")
        xp = k.ps[:, 0, :].rearrange("p (t e) -> p t e", e=E)
        pp = k.ps[:, 1, 0:E]
        with nc.Block() as block:

            @block.sync
            def _(sp):
                sp.dma_start(pt[:], weight_rows(a["L2_ffn_prototypes"])).then_inc(ph.s["ld"], 16)
                sp.dma_start(temp[:, 0:1], a["L2_ffn_temp"]).then_inc(ph.s["ld"], 16)
                sp.dma_start(xt_all[:], weight_rows(k.xt)).then_inc(ph.s["ld"], 16)
                sp.dma_start(xr[:], k.x_now.rearrange("(t p) d -> p t d", p=P)).then_inc(ph.s["xr_ld"], 16)

            @block.gpsimd
            def _(pool):
                pool.memset(ones[:], 1.0).then_inc(ph.s["conv"], 1)
                pool.memset(tmp[4][:], 1.0).then_inc(ph.s["conv"], 1)
                pool.wait_ge(ph.s["conv"], 2)
                pool.memset(tmp[4][:, :, 0:1], 0.0).then_inc(ph.s["conv"], 1)

            @block.tensor
            def _(pe):
                pe.wait_ge(ph.s["ld"], 48)
                pe.wait_ge(ph.s["conv"], 3)
                for t in range(NT):
                    for d in range(DC):
                        pe.matmul(xp[:, t, :], xt_all[:, d, t * P:(t + 1) * P], pt[:, d, :], start=d == 0, stop=d == DC - 1)
                pe.wait_ge(ph.s["pt2_ready"], 1)
                for d in range(DC):
                    ins = pe.matmul(pp, ones[:], pt2[:, d, :], start=d == 0, stop=d == DC - 1)
                ins.then_inc(ph.s["prods"], 1)

            @block.scalar
            def _(act):
                act.wait_ge(ph.s["xr_ld"], 16)
                for t in range(NT):
                    ins = act.activation(xr[:, t, :], xr[:, t, :], ACT.Square, accum_out=x2[:, t:t + 1])
                ins.then_inc(ph.s["x2_done"], 1)
                act.wait_ge(ph.s["d_ready"], 1)
                act.activation(d2[:], d2[:], ACT.Sqrt).then_inc(ph.s["sq_ready"], 1)
                act.wait_ge(ph.s["z_ready"], 1)
                act.activation(w[:], d2[:], ACT.Exp).then_inc(ph.s["e_ready"], 1)

            @block.vector
            def _(dve):
                ch = Count(dve, ph.s["chain"], 0, 0)

                def wide(v):
                    return v[:, :, None].to_broadcast([P, NT, E])

                dve.wait_ge(ph.s["ld"], 48)
                dve.tensor_tensor(pt2[:], pt[:], pt[:], ALU.mult).then_inc(ph.s["pt2_ready"], 1)
                ch.step(dve.tensor_scalar(temp[:, 1:2], temp[:, 0:1], -1.0, None, ALU.mult))
                ch.wait()
                ch.step(dve.tensor_tensor(temp[:, 0:1], temp[:, 0:1], temp[:, 1:2], ALU.max))
                ch.wait()
                ch.step(dve.tensor_scalar(temp[:, 0:1], temp[:, 0:1], 0.1, -1.0, ALU.max, ALU.mult))
                ch.wait()
                ch.step(dve.reciprocal(temp[:, 1:2], temp[:, 0:1]))
                dve.wait_ge(ph.s["prods"], 1)
                ch.step(dve.tensor_copy(p2[:], pp))
                ch.wait()
                ch.step(dve.scalar_tensor_tensor(out=d2[:], in0=xp, scalar=-2.0, in1=p2[:, None, :].to_broadcast([P, NT, E]), op0=ALU.mult, op1=ALU.add))
                ch.wait()
                dve.wait_ge(ph.s["x2_done"], 1)
                ch.step(dve.tensor_tensor(d2[:], d2[:], wide(x2), ALU.add))
                ch.wait()
                dve.tensor_scalar(d2[:], d2[:], 0.0, None, ALU.max).then_inc(ph.s["d_ready"], 1)
                dve.wait_ge(ph.s["sq_ready"], 1)
                ch.step(dve.tensor_scalar(d2[:], d2[:], temp[:, 1:2], None, ALU.mult))
                ch.wait()
                ch.step(dve.tensor_reduce(least[:], d2[:], AX.X, ALU.max))
                ch.wait()
                dve.tensor_tensor(d2[:], d2[:], wide(least), ALU.subtract).then_inc(ph.s["z_ready"], 1)
                dve.wait_ge(ph.s["e_ready"], 1)
                ch.step(dve.tensor_reduce(total[:], w[:], AX.X, ALU.add))
                ch.wait()
                ch.step(dve.reciprocal(inv[:], total[:]))
                ch.wait()
                ch.step(dve.tensor_tensor(w[:], w[:], wide(inv), ALU.mult))
                ch.wait()
                dve.wait_ge(ph.s["conv"], 3)
                top_mask(dve, ph, ch, w, m8, 2, E, tmp, mask)
                ch.step(dve.tensor_tensor(w[:], w[:], mask[:], ALU.mult))
                ch.wait()
                ch.step(dve.tensor_reduce(total[:], w[:], AX.X, ALU.add))
                ch.wait()
                ch.step(dve.reciprocal(inv[:], total[:]))
                ch.wait()
                ch.step(dve.tensor_tensor(wts[:], w[:], wide(inv), ALU.mult))
                ch.wait()


def l2_feed_forward(k, x_in, x_out, xt_out):
    nc, a = k.nc, k.a
    E, R = 32, 16
    ER = E * R
    RC = ER // P
    k.x_now = x_in
    with ExitStack() as keep:
        wts = keep.enter_context(nc.sbuf_tensor("f2_wts", [P, NT, E], F32))
        l2_weights(k, wts)
        with Phase(k, "f2") as ph:
            tail = Tail(ph, x_in, x_out, xt_out)
            wb, wa, bias = ph.sb("wb", [P, DC, ER]), ph.sb("wa", [P, RC, D]), ph.sb("wbias", [E, D])
            xs = ph.sb("xs", [P, DC, GN])
            low = ph.sb("low", [P, 2, ER])
            wrow = ph.sb("wrow", [P, GT, E])
            cols = ph.sb("cols", [P, RC, P])
            wcol = ph.sb("wcol", [E, P])
            ph.sems_of("w_ld xs_ld low_done weighted turned moved tile_done wrow_ready")
            with nc.Block() as block:

                @block.sync
                def _(sp):
                    for dst, src in ((wb[:], weight_rows(a["L2_ffn_B"])), (wa[:], weight_rows(a["L2_ffn_A"])), (bias[:], a["L2_ffn_bias"])):
                        sp.dma_start(dst, src).then_inc(ph.s["w_ld"], 16)
                    with sp.Fori(0, NG) as g:
                        sp.wait_ge(ph.s["low_done"], GT * g)
                        sp.dma_start(xs[:], k.xt[:, ds(g * GN, GN)].rearrange("(c p) t -> p c t", p=P)).then_inc(ph.s["xs_ld"], 16)
                        tail.load(sp, g)

                @block.gpsimd
                def _(pool):
                    with pool.Fori(0, NG) as g:
                        pool.wait_ge(ph.s["y_ready"], g)
                        pool.tensor_copy(wrow[:], wts[:, ds(g * GT, GT), :]).then_inc(ph.s["wrow_ready"], 1)
                        tail.store(pool, g)
                    tail.finish(pool)

                @block.tensor
                def _(pe):
                    pe.wait_ge(ph.s["w_ld"], 48)
                    with pe.Fori(0, NG) as g:
                        pe.wait_ge(ph.s["xs_ld"], 16 * g + 16)

                        def lower(j):
                            pe.wait_ge(ph.s["weighted"], GT * g + max(j - 1, 0))
                            for d in range(DC):
                                ins = pe.matmul(k.ps[:, j % 2, :], xs[:, d, j * P:(j + 1) * P], wb[:, d, :], start=d == 0, stop=d == DC - 1)
                            ins.then_inc(ph.s["low_done"], 1)

                        lower(0)
                        for j in range(GT):
                            if j + 1 < GT:
                                lower(j + 1)
                            pe.wait_ge(ph.s["weighted"], GT * g + j + 1)
                            pe.wait_ge(ph.s["wrow_ready"], g + 1)
                            pe.wait_ge(ph.s["moved"], 2 * (GT * g + j))
                            for c in range(RC):
                                pe.transpose(k.ps[:, 6, c * P:(c + 1) * P], low[:, j % 2, c * P:(c + 1) * P], k.ident[:])
                            pe.transpose(k.ps[0:E, 7, 0:P], wrow[:, j, :], k.ident[:]).then_inc(ph.s["turned"], 1)
                            pe.wait_ge(ph.s["moved"], 2 * (GT * g + j) + 2)
                            if j == 0:
                                pe.wait_ge(ph.s["r_done"], g)
                            for c in range(RC):
                                pe.matmul(tail.y[:, j, :], cols[:, c, :], wa[:, c, :], start=c == 0, stop=False)
                            ins = pe.matmul(tail.y[:, j, :], wcol[:], bias[:], start=False, stop=True)
                            ins.then_inc(ph.s["tile_done"] if j < GT - 1 else ph.s["y_ready"], 1)
                        tail.tensor(pe, g)

                @block.scalar
                def _(act):
                    with act.Fori(0, NG) as g:
                        for j in range(GT):
                            act.wait_ge(ph.s["turned"], GT * g + j + 1)
                            if j:
                                act.wait_ge(ph.s["tile_done"], (GT - 1) * g + j)
                            else:
                                act.wait_ge(ph.s["y_ready"], g)
                            act.activation(cols[:].rearrange("p c t -> p (c t)"), k.ps[:, 6, :], ACT.Copy).then_inc(ph.s["moved"], 1)
                            act.activation(wcol[:], k.ps[0:E, 7, 0:P], ACT.Copy).then_inc(ph.s["moved"], 1)
                        tail.scalar(act, g)

                @block.vector
                def _(dve):
                    with dve.Fori(0, NG) as g:
                        for j in range(GT):
                            dve.wait_ge(ph.s["low_done"], GT * g + j + 1)
                            dve.wait_ge(ph.s["wrow_ready"], g + 1)
                            dve.wait_ge(ph.s["turned"], GT * g + max(j - 1, 0))
                            dve.tensor_tensor(low[:, j % 2, :].rearrange("p (e r) -> p e r", r=R), k.ps[:, j % 2, :].rearrange("p (e r) -> p e r", r=R),
                                              wrow[:, j, :, None].to_broadcast([P, E, R]), ALU.mult).then_inc(ph.s["weighted"], 1)
                        tail.vector(dve, g)


def l3_feed_forward(k, x_in, x_out, xt_out):
    nc, a = k.nc, k.a
    E, HID = 8, 1024
    HC = HID // P
    TW = 2 * P
    norm_columns(k, "f3n", x_in, k.xnt, a["L3_ffn_ln_scale"], a["L3_ffn_ln_bias"])
    with ExitStack() as keep:
        y_all = keep.enter_context(nc.sbuf_tensor("f3_y_all", [P, NT, D], F32))
        with Phase(k, "f3") as ph:
            wat, wnx = ph.sb("wat", [P, DC, D]), ph.sb("wnx", [P, DC, D])
            bat, bnx = ph.sb("bat", [P, DC]), ph.sb("bnx", [P, D])
            xn, xs = ph.sb("xn", [P, 2, DC, TW]), ph.sb("xs", [P, 2, DC, TW])
            w1, w2 = ph.sb("w1", [P, 2, DC, HID]), ph.sb("w2", [P, 2, HC, D])
            b1, b2 = ph.sb("b1", [P, 2, HC]), ph.sb("b2", [P, 2, DC])
            xa = ph.sb("xa", [P, DC, TW])
            hid = ph.sb("hid", [P, HC, TW])
            eo = ph.sb("eo", [P, DC, TW])
            pre = ph.sb("pre", [P, 2, D])
            ph.sems_of("c_ld xa_mm xa_ready h_mm h_ready eo_mm eo_ready y_mm pre_ready y_ready")
            ld = [ph.sem("ld0"), ph.sem("ld1")]
            NLD = 8
            with nc.Block() as block:

                @block.sync
                def _(sp):
                    for dst, src in ((wat[:], weight_rows(a["L3_ffn_attn_w"])), (wnx[:], weight_rows(a["L3_ffn_next_w"])), (bat[:], a["L3_ffn_attn_b"]),
                                     (bnx[:], a["L3_ffn_next_b"])):
                        sp.dma_start(dst, src).then_inc(ph.s["c_ld"], 16)
                    with sp.Fori(0, E // 2) as t:
                        for s in range(2):
                            e = t * 2 + s
                            sp.wait_ge(ph.s["y_mm"], e + 1)
                            for half in range(2):
                                for dst, src in ((xn, k.xnt), (xs, k.xt)):
                                    sp.dma_start(dst[:, s, :, half * P:(half + 1) * P], src[:, ds(half * T + e * P, P)].rearrange("(c p) t -> p c t", p=P)).then_inc(ld[s], 16)
                            sp.dma_start(w1[:, s, :, :], a["L3_ffn_w1"][ds(e, 1), :, :].rearrange("o (c p) n -> p (o c) n", p=P)).then_inc(ld[s], 16)
                            sp.dma_start(w2[:, s, :, :], a["L3_ffn_w2"][ds(e, 1), :, :].rearrange("o (c p) n -> p (o c) n", p=P)).then_inc(ld[s], 16)
                            sp.dma_start(b1[:, s, :], a["L3_ffn_b1"][ds(e, 1), :, :].rearrange("o p c -> p (o c)")).then_inc(ld[s], 16)
                            sp.dma_start(b2[:, s, :], a["L3_ffn_b2"][ds(e, 1), :, :].rearrange("o p c -> p (o c)")).then_inc(ld[s], 16)

                @block.tensor
                def _(pe):
                    pe.sem_inc(ph.s["y_mm"], 2)
                    pe.wait_ge(ph.s["c_ld"], 64)
                    with pe.Fori(0, E // 2) as t:
                        for s in range(2):
                            e = t * 2 + s
                            pe.wait_ge(ld[s], 16 * NLD * t + 16 * NLD)
                            pe.wait_ge(ph.s["xa_ready"], DC * e)
                            for c in range(DC):
                                for d in range(DC):
                                    ins = pe.matmul(k.ps[:, 0, c * TW:(c + 1) * TW], wat[:, d, c * P:(c + 1) * P], xn[:, s, d, :], start=d == 0, stop=d == DC - 1)
                            ins.then_inc(ph.s["xa_mm"], 1)
                            pe.wait_ge(ph.s["xa_ready"], DC * e + DC)
                            for c in range(HC):
                                pe.wait_ge(ph.s["h_ready"], HC * e + max(c - 3, 0))
                                for d in range(DC):
                                    ins = pe.matmul(k.ps[:, 1 + c % 4, 0:TW], w1[:, s, d, c * P:(c + 1) * P], xa[:, d, :], start=d == 0, stop=d == DC - 1)
                                ins.then_inc(ph.s["h_mm"], 1)
                            pe.wait_ge(ph.s["eo_ready"], DC * e)
                            for c in range(DC):
                                for d in range(HC):
                                    if c == 0:
                                        pe.wait_ge(ph.s["h_ready"], HC * e + d + 1)
                                    ins = pe.matmul(k.ps[:, 5, c * TW:(c + 1) * TW], w2[:, s, d, c * P:(c + 1) * P], hid[:, d, :], start=d == 0, stop=d == HC - 1)
                            ins.then_inc(ph.s["eo_mm"], 1)
                            pe.wait_ge(ph.s["eo_ready"], DC * e + DC)
                            pe.wait_ge(ph.s["pre_ready"], e)
                            for j in range(2):
                                for d in range(DC):
                                    ins = pe.matmul(k.ps[:, 6, j * D:(j + 1) * D], eo[:, d, j * P:(j + 1) * P], wnx[:, d, :], start=d == 0, stop=d == DC - 1)
                            ins.then_inc(ph.s["y_mm"], 1)

                @block.scalar
                def _(act):
                    act.wait_ge(ph.s["c_ld"], 64)
                    with act.Fori(0, E // 2) as t:
                        for s in range(2):
                            e = t * 2 + s
                            act.wait_ge(ld[s], 16 * NLD * t + 16 * NLD)
                            for c in range(HC):
                                act.wait_ge(ph.s["h_mm"], HC * e + c + 1)
                                if c == 0:
                                    act.wait_ge(ph.s["eo_mm"], e)
                                act.activation(hid[:, c, :], k.ps[:, 1 + c % 4, 0:TW], ACT.Gelu, bias=b1[:, s, c:c + 1]).then_inc(ph.s["h_ready"], 1)
                            act.wait_ge(ph.s["pre_ready"], e + 1)
                            act.activation(y_all[:, ds(e, 2, E), :], pre[:], ACT.Gelu).then_inc(ph.s["y_ready"], 1)
                    act.wait_ge(ph.s["y_ready"], E)

                @block.vector
                def _(dve):
                    dve.wait_ge(ph.s["c_ld"], 64)
                    with dve.Fori(0, E // 2) as t:
                        for s in range(2):
                            e = t * 2 + s
                            dve.wait_ge(ld[s], 16 * NLD * t + 16 * NLD)
                            dve.wait_ge(ph.s["xa_mm"], e + 1)
                            dve.wait_ge(ph.s["h_mm"], HC * e)
                            for c in range(DC):
                                dve.scalar_tensor_tensor(out=xa[:, c, :], in0=k.ps[:, 0, c * TW:(c + 1) * TW], scalar=bat[:, c:c + 1], in1=xs[:, s, c, :],
                                                         op0=ALU.add, op1=ALU.add).then_inc(ph.s["xa_ready"], 1)
                            dve.wait_ge(ph.s["eo_mm"], e + 1)
                            dve.wait_ge(ph.s["y_mm"], e + 2)
                            for c in range(DC):
                                dve.tensor_scalar(eo[:, c, :], k.ps[:, 5, c * TW:(c + 1) * TW], b2[:, s, c:c + 1], None, ALU.add).then_inc(ph.s["eo_ready"], 1)
                            dve.wait_ge(ph.s["y_mm"], e + 3)
                            dve.wait_ge(ph.s["y_ready"], e)
                            dve.tensor_tensor(pre[:], k.ps[:, 6, :].rearrange("p (j d) -> p j d", d=D), bnx[:, None, :].to_broadcast([P, 2, D]), ALU.add).then_inc(ph.s["pre_ready"], 1)

        add_and_norm(k, "f3o", y_all, x_in, x_out, xt_out)


class Kernel:

    def __init__(self, nc, a):
        self.nc, self.a = nc, a
        self.ps = nc.alloc_psum_tensor("ps", [P, 8, 512], F32)
        self.ident = nc.alloc_sbuf_tensor("ident", [P, P], F32)
        self.ident_b = nc.alloc_sbuf_tensor("ident_b", [P, P], BF16)
        self.mask = nc.alloc_sbuf_tensor("mask", [P, P], BF16)
        self.mask_t = nc.alloc_sbuf_tensor("mask_t", [P, P], BF16)
        self.x = [self.dram("x0", [N, D]), self.dram("x1", [N, D])]
        self.xt = self.dram("xt", [D, N])
        self.xnt = self.dram("xnt", [D, N])

    def dram(self, name, shape, dt=F32):
        return self.nc.dram_tensor(name, tuple(shape), dt).ap()


def constants(k):
    nc = k.nc
    with Phase(k, "const") as ph:
        ph.sems_of("ld conv")
        idf = ph.sb("idf", [P, 2, P])
        with nc.Block() as block:

            @block.sync
            def _(sp):
                sp.dma_start(k.ident[:], k.a["c_ident"]).then_inc(ph.s["ld"], 16)
                sp.dma_start(idf[:, 0, :], k.a["c_mask"]).then_inc(ph.s["ld"], 16)
                sp.dma_start(idf[:, 1, :], k.a["c_mask_t"]).then_inc(ph.s["ld"], 16)
                sp.wait_ge(ph.s["ld"], 48)

            @block.vector
            def _(dve):
                dve.wait_ge(ph.s["ld"], 48)
                dve.tensor_copy(k.ident_b[:], k.ident[:]).then_inc(ph.s["conv"], 1)
                dve.tensor_copy(k.mask[:], idf[:, 0, :]).then_inc(ph.s["conv"], 1)
                dve.tensor_copy(k.mask_t[:], idf[:, 1, :]).then_inc(ph.s["conv"], 1)
                dve.wait_ge(ph.s["conv"], 3)


STAGES = [l0_self_attention, l0_cross_attention, l0_feed_forward, l1_self_attention, l1_cross_attention, l1_feed_forward,
          l2_self_attention, l2_cross_attention, l2_feed_forward, l3_self_attention, l3_cross_attention, l3_feed_forward]


def build(nc, a, out, stages):
    k = Kernel(nc, a)
    constants(k)
    x = a["x"]
    for n, stage in enumerate(stages):
        last = n == len(stages) - 1
        x_out = out if last else k.x[n % 2]
        stage(k, x, x_out, None if last else k.xt)
        x = x_out


def layouts(i):
    import numpy as np

    def cols(v):
        return np.ascontiguousarray(np.reshape(v, (-1, P)).T)

    def rows(v, n=P):
        return np.ascontiguousarray(np.broadcast_to(np.reshape(v, (1, -1)), (n, np.size(v))))

    def by_halves(w):
        return w.reshape(D, -1, 4, 32, 2).transpose(0, 1, 4, 2, 3).reshape(D, -1)

    def kv(w, n):
        return w.reshape((16, 2, 16) + w.shape[1:])[:, n].reshape((256,) + w.shape[1:])

    freq = np.float32(1.0) / np.float32(10000.0) ** (np.arange(0, 64, 2, dtype=np.float32) / np.float32(64))
    angle = np.tile(freq, 4)[:, None] * np.arange(T, dtype=np.float32)[None, :]
    rope = [(f(angle.astype(np.float64)) * 64 ** -0.25).astype(np.float32) for f in (np.cos, np.sin)]

    c = {k: np.asarray(v) for k, v in i.items()}
    r = {
        "c_ident": np.eye(P, dtype=np.float32),
        "c_mask": np.where(np.arange(P)[None, :] > np.arange(P)[:, None], np.float32(-1e30), np.float32(0)),
        "c_mask_t": np.where(np.arange(P)[:, None] > np.arange(P)[None, :], np.float32(-1e30), np.float32(0)),
        "x": c["x"].reshape(N, D),
        "L0_attn_in_ln_w": cols(c["L0_attn_in_ln_w"]),
        "L0_attn_in_ln_b": cols(c["L0_attn_in_ln_b"]),
        "L0_attn_W_in": c["L0_attn_W_in"].T,
        "L0_attn_b_col": cols(c["L0_attn_b_in"][:1024]),
        "L0_attn_b_y": c["L0_attn_b_in"][2048:].reshape(16, 1),
        "L0_attn_b_row": rows(c["L0_attn_b_in"][1024:2048]),
        "L0_attn_by_head": np.stack([cols(np.repeat(c["L0_attn_smear_factor"], 32)), cols(np.repeat(c["L0_attn_log_scale"], 32))], 1),
        "L0_attn_W_out": c["L0_attn_W_out"].T,
        "L0_attn_out_ln_w": rows(c["L0_attn_out_ln_w"]),
        "L0_attn_out_ln_b": rows(c["L0_attn_out_ln_b"]),
        "c_before": np.triu(np.ones((P, P), np.float32), 1),
        "L0_ffn_gate_w": c["L0_ffn_gate_w"].T,
        "L0_ffn_bias": rows(c["L0_ffn_bias"]),
        "L0_ffn_W1": np.concatenate([c["L0_ffn_W1"], c["L0_ffn_sw1"].T[None]]),
        "L0_ffn_W3": np.concatenate([c["L0_ffn_W3"], c["L0_ffn_sw3"].T[None]]),
        "L0_ffn_W2": np.concatenate([c["L0_ffn_W2"], c["L0_ffn_sw2"].T[None]]),
        "L1_ffn_W1": np.concatenate([c["L1_ffn_W1"], c["L1_ffn_Ws1"][None]]),
        "L1_ffn_W2": np.concatenate([c["L1_ffn_W2"], c["L1_ffn_Ws2"][None]]),
        "L1_ffn_Wr": c["L1_ffn_Wr"],
        "L2_ffn_prototypes": c["L2_ffn_prototypes"].T,
        "L2_ffn_temp": rows(c["L2_ffn_temp"]),
        "L2_ffn_B": c["L2_ffn_B"].reshape(512, D).T,
        "L2_ffn_A": c["L2_ffn_A"].transpose(0, 2, 1).reshape(512, D),
        "L2_ffn_bias": c["L2_ffn_bias"],
        "L3_ffn_ln_scale": cols(c["L3_ffn_ln_scale"]),
        "L3_ffn_ln_bias": cols(c["L3_ffn_ln_bias"]),
        "L3_ffn_attn_w": c["L3_ffn_attn_w"].T,
        "L3_ffn_attn_b": cols(c["L3_ffn_attn_b"]),
        "L3_ffn_next_w": c["L3_ffn_next_w"].T,
        "L3_ffn_next_b": rows(c["L3_ffn_next_b"]),
        "L3_ffn_w1": c["L3_ffn_w1"],
        "L3_ffn_w2": c["L3_ffn_w2"],
        "L3_ffn_b1": c["L3_ffn_b1"].reshape(8, 8, P).transpose(0, 2, 1),
        "L3_ffn_b2": c["L3_ffn_b2"].reshape(8, 2, P).transpose(0, 2, 1),
        "c_cos": rope[0],
        "c_sin": rope[1],
        "L1_attn_Wq": by_halves(c["L1_attn_Wq"]),
        "L1_attn_Wk": by_halves(c["L1_attn_Wk"]),
        "L3_attn_W_dq": c["L3_attn_W_dq"],
        "L3_attn_W_dq_T": c["L3_attn_W_dq"].T,
        "L3_attn_W_dkv": c["L3_attn_W_dkv"].T,
        "L3_attn_W_uq": c["L3_attn_W_uq"],
        "L3_attn_W_uq_T": c["L3_attn_W_uq"].T,
        "L3_attn_W_uk": c["L3_attn_W_uk"],
        "L3_attn_W_uv": c["L3_attn_W_uv"],
        "L3_attn_W_o": c["L3_attn_W_o"].T,
        "ctx_T": c["ctx_768"].reshape(B * M, CTX).T,
        "ctx_rows": c["ctx_768"].transpose(1, 0, 2),
        "L0_xattn_bout": rows(c["L0_xattn_bout"]),
        "L1_xattn_Wq": c["L1_xattn_Wq"].T,
        "L1_xattn_bq": cols(c["L1_xattn_bq"]),
        "L1_xattn_Wk": kv(c["L1_xattn_Wkv"], 0).T,
        "L1_xattn_Wv": kv(c["L1_xattn_Wkv"], 1).T,
        "L1_xattn_bk": cols(kv(c["L1_xattn_bkv"], 0)),
        "L1_xattn_bv": rows(kv(c["L1_xattn_bkv"], 1), M),
        "L1_xattn_Wo": c["L1_xattn_Wo"].T,
        "L1_xattn_bo": rows(c["L1_xattn_bo"]),
        "L2_xattn_bo": rows(c["L2_xattn_bo"]),
        "L3_xattn_g_x": cols(c["L3_xattn_g_x"]),
        "L3_xattn_b_x": cols(c["L3_xattn_b_x"]),
        "L3_xattn_norm_c": np.stack([c["L3_xattn_g_c"], c["L3_xattn_b_c"]], 1),
    }
    for name in ("L0_xattn_Wq L0_xattn_Wk L0_xattn_Wv L0_xattn_Wout L1_attn_Wv L1_attn_Wo L2_attn_Wq L2_attn_Wk L2_attn_Wv L2_attn_Wo "
                 "L3_xattn_Wq L3_xattn_Wk L3_xattn_Wv L3_xattn_Wo").split():
        r[name] = c[name]
    for name in "L2_xattn_Wq L2_xattn_Wk L2_xattn_Wv L2_xattn_Wo".split():
        r[name] = c[name].T
    return {k: np.ascontiguousarray(v) for k, v in r.items()}


def kernel(**inputs):
    import numpy as _np
    import concourse.bacc as _bacc
    from concourse import mybir as _mybir
    from concourse.bass_utils import run_bass_kernel_spmd as _run

    nc = _bacc.Bacc("TRN2", target_bir_lowering=False, num_devices=1)
    arrays, args = {}, {}
    for name, v in layouts(inputs).items():
        arrays[f"in_{name}_dram"] = v
        args[name] = nc.dram_tensor(f"in_{name}_dram", v.shape, _mybir.dt.from_np(v.dtype), kind="ExternalInput").ap()
    out = nc.dram_tensor("out_dram", (N, D), F32, kind="ExternalOutput").ap()
    build(nc, args, out, STAGES)
    r = _run(nc, [arrays], core_ids=[0])
    return _np.asarray(r.results[0]["out_dram"]).reshape(B, T, D)
```
